# Optimizing a Trainium2 kernel written in Bass

```python
import numpy as np
import jax
import jax.numpy as jnp

def _softmax(x, axis=-1):
    return jax.nn.softmax(x, axis=axis)

def _gelu(x):
    return jax.nn.gelu(x, approximate=True)

def _silu(x):
    return jax.nn.silu(x)

def _sigmoid(x):
    return jax.nn.sigmoid(x)

def _layernorm(x, axis=-1, eps=1e-05):
    m = jnp.mean(x, axis=axis, keepdims=True)
    v = jnp.var(x, axis=axis, keepdims=True)
    return (x - m) / jnp.sqrt(v + eps)

def _scatter_add(tgt, idx, src, axis=0):
    return tgt.at[idx].add(src)

def _segment_sum(src, seg, n):
    return jax.ops.segment_sum(src, seg, n)
kernel_name = 'mk_decoder_postln_d1_seqx_r8_0d24fe'

def setup_inputs(seed: int=0):
    np.random.seed(seed)
    _w = jnp.asarray

    def _rec_inputs():
        import jax
        import jax.numpy as jnp
        _rk = jax.random.key(seed)
        x = -0.0002928 + 1 * jax.random.normal(jax.random.fold_in(_rk, 1), (16, 100, 128), jnp.float32)
        _lenS = 100 - jax.random.randint(jax.random.fold_in(_rk, 7), (16,), 0, max(1, 100 // 4) + 1, jnp.int32)
        _lenS2 = 1444 - jax.random.randint(jax.random.fold_in(_rk, 8), (16,), 0, max(1, 1444 // 4) + 1, jnp.int32)
        _ctx_1024P = jax.random.normal(jax.random.fold_in(_rk, 11), (16, 16, 128), jnp.float32)
        _ctx_1024c = jax.random.dirichlet(jax.random.fold_in(_rk, 511), 0.3 * jnp.ones((16,), jnp.float32), (16, 1444))
        _ctx_1024t = jnp.einsum('bsk,bkd->bsd', _ctx_1024c, _ctx_1024P)
        _ctx_1024t = _ctx_1024t * jax.lax.rsqrt(jnp.mean(jnp.square(_ctx_1024t)) + 1e-12) * 0.953939
        ctx_1024 = -1.39393e-06 + 0.999914 * (_ctx_1024t + 0.3 * jax.random.normal(jax.random.fold_in(_rk, 611), (16, 1444, 128), jnp.float32))
        return (x, ctx_1024)
    x, ctx_1024 = _rec_inputs()

    def _L0_attn_setup():
        import jax, jax.numpy as jnp
        import numpy as np
        B, N, HID = (8, 512, 128)
        HEADS = 16
        D = HID // HEADS
        LN_EPS = 1e-05
        key = jax.random.key(seed)
        ks = jax.random.split(key, 8)
        s = 1.0 / np.sqrt(HID)
        x = jax.random.normal(ks[0], (B, N, HID), dtype=jnp.float32)
        Wh = jax.random.uniform(ks[1], (HID, HID), jnp.float32, -s, s)
        Wq = jax.random.uniform(ks[2], (HID, HID), jnp.float32, -s, s)
        Wk = jax.random.uniform(ks[3], (HID, HID), jnp.float32, -s, s)
        Wv = jax.random.uniform(ks[4], (HID, HID), jnp.float32, -s, s)
        Wo = jax.random.uniform(ks[5], (HID, HID), jnp.float32, -s, s)
        bh = jax.random.uniform(ks[6], (HID,), jnp.float32, -s, s)
        bq = jnp.zeros((HID,), jnp.float32)
        bk = jnp.zeros((HID,), jnp.float32)
        bv = jnp.zeros((HID,), jnp.float32)
        bo = jax.random.uniform(ks[7], (HID,), jnp.float32, -s, s)
        beta = jnp.full((HID,), 0.1, jnp.float32)
        ln_w = jnp.ones((HID,), jnp.float32)
        ln_b = jnp.zeros((HID,), jnp.float32)
        return {'x': x, 'Wh': Wh, 'bh': bh, 'Wq': Wq, 'bq': bq, 'Wk': Wk, 'bk': bk, 'Wv': Wv, 'bv': bv, 'beta': beta, 'ln_w': ln_w, 'ln_b': ln_b, 'Wo': Wo, 'bo': bo}
    _L0_attn_all = _L0_attn_setup()
    _L0_attn_in = {k: v for k, v in _L0_attn_all.items() if k in ('Wh', 'bh', 'Wq', 'bq', 'Wk', 'bk', 'Wv', 'bv', 'beta', 'ln_w', 'ln_b', 'Wo', 'bo')}
    del _L0_attn_all

    def _L0_xattn_setup():
        import jax, jax.numpy as jnp
        import numpy as np
        DMODEL = 128
        NHEAD = 16
        DHEAD = DMODEL // NHEAD

        def _layernorm(x, g, b, eps=1e-05):
            mu = jnp.mean(x, axis=-1, keepdims=True)
            var = jnp.var(x, axis=-1, keepdims=True)
            return (x - mu) * jax.lax.rsqrt(var + eps) * g + b
        key = jax.random.key(seed)
        ks = jax.random.split(key, 12)
        b, lq, lv, d = (2, 256, 256, DMODEL)
        s = 1.0 / np.sqrt(d)
        return {'q': jax.random.normal(ks[0], (b, lq, d), jnp.float32), 'k': jax.random.normal(ks[1], (b, lv, d), jnp.float32), 'v': jax.random.normal(ks[2], (b, lv, d), jnp.float32), 'qln_g': jnp.ones((d,), jnp.float32), 'qln_b': jnp.zeros((d,), jnp.float32), 'kvln_g': jnp.ones((d,), jnp.float32), 'kvln_b': jnp.zeros((d,), jnp.float32), 'Wq': jax.random.normal(ks[3], (d, d), jnp.float32) * s, 'Wk': jax.random.normal(ks[4], (d, d), jnp.float32) * s, 'Wv': jax.random.normal(ks[5], (d, d), jnp.float32) * s, 'Wg': jax.random.normal(ks[6], (d, d), jnp.float32) * s, 'bg': jnp.zeros((d,), jnp.float32), 'Wo': jax.random.normal(ks[7], (d, d), jnp.float32) * s}
    _L0_xattn_all = _L0_xattn_setup()
    _L0_xattn_in = {k: v for k, v in _L0_xattn_all.items() if k in ('qln_g', 'qln_b', 'kvln_g', 'kvln_b', 'Wq', 'Wk', 'Wv', 'Wg', 'bg', 'Wo')}
    del _L0_xattn_all

    def _L0_ffn_setup():
        import jax, jax.numpy as jnp
        import numpy as np
        D_MODEL = 128
        HIDDEN = 512
        NUM_EXPERTS = 8
        TOP_K = 2
        DEPTH = 12
        DEPTH_SCALE = 1.0 / np.sqrt(DEPTH)
        key = jax.random.key(seed)
        k_x, k_r, k_g, k_u, k_d = jax.random.split(key, 5)
        s_in = 1.0 / np.sqrt(D_MODEL)
        s_hid = 1.0 / np.sqrt(HIDDEN)
        return {'x': jax.random.normal(k_x, (2, 256, D_MODEL), dtype=jnp.float32), 'Wr': jax.random.normal(k_r, (D_MODEL, NUM_EXPERTS), dtype=jnp.float32) * s_in, 'Wg': jax.random.normal(k_g, (NUM_EXPERTS, D_MODEL, HIDDEN), dtype=jnp.float32) * s_in, 'Wu': jax.random.normal(k_u, (NUM_EXPERTS, D_MODEL, HIDDEN), dtype=jnp.float32) * s_in, 'Wd': jax.random.normal(k_d, (NUM_EXPERTS, HIDDEN, D_MODEL), dtype=jnp.float32) * s_hid}
    _L0_ffn_all = _L0_ffn_setup()
    _L0_ffn_in = {k: v for k, v in _L0_ffn_all.items() if k in ('Wr', 'Wg', 'Wu', 'Wd')}
    del _L0_ffn_all
    return {'x': x, 'ctx_1024': ctx_1024, 'L0_attn_Wh': _L0_attn_in['Wh'], 'L0_attn_bh': _L0_attn_in['bh'], 'L0_attn_Wq': _L0_attn_in['Wq'], 'L0_attn_bq': _L0_attn_in['bq'], 'L0_attn_Wk': _L0_attn_in['Wk'], 'L0_attn_bk': _L0_attn_in['bk'], 'L0_attn_Wv': _L0_attn_in['Wv'], 'L0_attn_bv': _L0_attn_in['bv'], 'L0_attn_beta': _L0_attn_in['beta'], 'L0_attn_ln_w': _L0_attn_in['ln_w'], 'L0_attn_ln_b': _L0_attn_in['ln_b'], 'L0_attn_Wo': _L0_attn_in['Wo'], 'L0_attn_bo': _L0_attn_in['bo'], 'L0_xattn_qln_g': _L0_xattn_in['qln_g'], 'L0_xattn_qln_b': _L0_xattn_in['qln_b'], 'L0_xattn_kvln_g': _L0_xattn_in['kvln_g'], 'L0_xattn_kvln_b': _L0_xattn_in['kvln_b'], 'L0_xattn_Wq': _L0_xattn_in['Wq'], 'L0_xattn_Wk': _L0_xattn_in['Wk'], 'L0_xattn_Wv': _L0_xattn_in['Wv'], 'L0_xattn_Wg': _L0_xattn_in['Wg'], 'L0_xattn_bg': _L0_xattn_in['bg'], 'L0_xattn_Wo': _L0_xattn_in['Wo'], 'L0_ffn_Wr': _L0_ffn_in['Wr'], 'L0_ffn_Wg': _L0_ffn_in['Wg'], 'L0_ffn_Wu': _L0_ffn_in['Wu'], 'L0_ffn_Wd': _L0_ffn_in['Wd']}

def reference(x, ctx_1024, L0_attn_Wh, L0_attn_bh, L0_attn_Wq, L0_attn_bq, L0_attn_Wk, L0_attn_bk, L0_attn_Wv, L0_attn_bv, L0_attn_beta, L0_attn_ln_w, L0_attn_ln_b, L0_attn_Wo, L0_attn_bo, L0_xattn_qln_g, L0_xattn_qln_b, L0_xattn_kvln_g, L0_xattn_kvln_b, L0_xattn_Wq, L0_xattn_Wk, L0_xattn_Wv, L0_xattn_Wg, L0_xattn_bg, L0_xattn_Wo, L0_ffn_Wr, L0_ffn_Wg, L0_ffn_Wu, L0_ffn_Wd):
    import jax
    import jax.numpy as jnp

    def _L0_attn_ref(x, Wh, bh, Wq, bq, Wk, bk, Wv, bv, beta, ln_w, ln_b, Wo, bo):
        import jax, jax.numpy as jnp
        import numpy as np
        B, N, HID = (8, 512, 128)
        HEADS = 16
        D = HID // HEADS
        LN_EPS = 1e-05
        b, n, _ = x.shape
        h = x @ Wh + bh
        q = jax.nn.sigmoid(x @ Wq + bq).reshape(b, n, D, HEADS)
        k = jax.nn.sigmoid(x @ Wk + bk).reshape(b, n, D, HEADS)
        v = (x @ Wv + bv).reshape(b, n, D, HEADS)
        kv = jnp.einsum('bndh,bnmh->bdmh', k, v)
        num = jnp.einsum('bndh,bdmh->bnmh', q, kv)
        k_sum = jnp.einsum('bndh->bdh', k)
        den = jnp.einsum('bndh,bdh->bnh', q, k_sum)[:, :, None, :]
        attn = (num / den).reshape(b, n, HEADS * D)
        mu = jnp.mean(attn, axis=-1, keepdims=True)
        var = jnp.var(attn, axis=-1, keepdims=True)
        ln = (attn - mu) * jax.lax.rsqrt(var + LN_EPS) * ln_w + ln_b
        gated = ln * (h + beta)
        out = jax.nn.relu(gated @ Wo + bo)
        return out

    def _L0_xattn_ref(q, k, v, qln_g, qln_b, kvln_g, kvln_b, Wq, Wk, Wv, Wg, bg, Wo):
        import jax, jax.numpy as jnp
        import numpy as np
        DMODEL = 128
        NHEAD = 16
        DHEAD = DMODEL // NHEAD

        def _layernorm(x, g, b, eps=1e-05):
            mu = jnp.mean(x, axis=-1, keepdims=True)
            var = jnp.var(x, axis=-1, keepdims=True)
            return (x - mu) * jax.lax.rsqrt(var + eps) * g + b
        b, lq, d = q.shape
        lv = v.shape[1]
        qn = _layernorm(q, qln_g, qln_b)
        q_ = qn @ Wq.T
        kk = _layernorm(k, kvln_g, kvln_b) @ Wk.T
        vv = _layernorm(v, kvln_g, kvln_b) @ Wv.T
        qh = q_.reshape(b, lq, NHEAD, DHEAD)
        kh = kk.reshape(b, lv, NHEAD, DHEAD)
        vh = vv.reshape(b, lv, NHEAD, DHEAD)
        scores = jnp.einsum('bqhd,bkhd->bhqk', qh, kh) / np.sqrt(DHEAD)
        attn = jax.nn.softmax(scores, axis=-1)
        y = jnp.einsum('bhqk,bkhd->bqhd', attn, vh).reshape(b, lq, d)
        g = jax.nn.sigmoid(qn @ Wg.T + bg)
        return y * g @ Wo.T

    def _L0_ffn_ref(x, Wr, Wg, Wu, Wd):
        import jax, jax.numpy as jnp
        import numpy as np
        D_MODEL = 128
        HIDDEN = 512
        NUM_EXPERTS = 8
        TOP_K = 2
        DEPTH = 12
        DEPTH_SCALE = 1.0 / np.sqrt(DEPTH)
        B, T, C = x.shape
        flat_x = x.reshape(-1, C)
        logits = flat_x @ Wr
        top_vals, top_idx = jax.lax.top_k(logits, TOP_K)
        rw = jax.nn.softmax(top_vals.astype(jnp.float32), axis=-1).astype(x.dtype)
        combine = jnp.sum(rw[..., None] * jax.nn.one_hot(top_idx, NUM_EXPERTS, dtype=x.dtype), axis=1)
        g = jnp.einsum('nc,ech->neh', flat_x, Wg)
        u = jnp.einsum('nc,ech->neh', flat_x, Wu)
        h = jax.nn.silu(g) * u
        eo = jnp.einsum('neh,ehc->nec', h, Wd) * DEPTH_SCALE
        out = jnp.einsum('ne,nec->nc', combine, eo)
        return out.reshape(B, T, C)
    x = _layernorm(x + _L0_attn_ref(x, L0_attn_Wh, L0_attn_bh, L0_attn_Wq, L0_attn_bq, L0_attn_Wk, L0_attn_bk, L0_attn_Wv, L0_attn_bv, L0_attn_beta, L0_attn_ln_w, L0_attn_ln_b, L0_attn_Wo, L0_attn_bo), axis=-1)
    x = _layernorm(x + _L0_xattn_ref(x, ctx_1024, ctx_1024, L0_xattn_qln_g, L0_xattn_qln_b, L0_xattn_kvln_g, L0_xattn_kvln_b, L0_xattn_Wq, L0_xattn_Wk, L0_xattn_Wv, L0_xattn_Wg, L0_xattn_bg, L0_xattn_Wo), axis=-1)
    x = _layernorm(x + _L0_ffn_ref(x, L0_ffn_Wr, L0_ffn_Wg, L0_ffn_Wu, L0_ffn_Wd), axis=-1)
    return x

_drawn_inputs = setup_inputs


def setup_inputs(seed=0):
    import zlib

    import numpy as np

    out = dict(_drawn_inputs(seed))
    spreads = {'L0_attn_bq': (0.0, 0.8),
     'L0_attn_bk': (0.0, 0.8),
     'L0_attn_bv': (0.0, 0.1),
     'L0_attn_beta': (0.10000000149011612, 0.6),
     'L0_attn_ln_w': (1.0, 0.2),
     'L0_attn_ln_b': (0.0, 0.272),
     'L0_xattn_qln_g': (1.0, 0.2),
     'L0_xattn_qln_b': (0.0, 0.43),
     'L0_xattn_kvln_g': (1.0, 0.2),
     'L0_xattn_kvln_b': (0.0, 0.1),
     'L0_xattn_bg': (0.0, 0.521)}
    factors = {'L0_attn_Wq': 7.923, 'L0_attn_Wk': 2.889}
    for name, (base, spread) in spreads.items():
        noise = np.random.default_rng([zlib.crc32(name.encode()), seed]).standard_normal(out[name].shape)
        drawn = base * np.exp(spread * noise) if base else spread * noise
        out[name] = jnp.asarray(drawn.astype(out[name].dtype))
    for name, factor in factors.items():
        out[name] = (out[name] * factor).astype(out[name].dtype)
    return out
```

```python
from contextlib import ExitStack

import concourse.bass as bass
from concourse import mybir

ALU = mybir.AluOpType
ACT = mybir.ActivationFunctionType
AXL = mybir.AxisListType
F32 = mybir.dt.float32
F16 = mybir.dt.float16

P = 128
BANK = 512
EPS = 1e-5
STEPS = 24
MX_EARLY = 17
MX_FROM = 14
MX_UNTIL = 14
STATS_FROM = 6

FILLS = {1: "Y0", 2: "T0", 3: "T1", 4: "T2", 5: "G0", 6: "K0", 7: "O0", 8: "K1", 10: "K2", 12: "K3",
         15: "M0", 17: "V0", 18: "V1", 20: "V2"}
STAGE_OF = {"T": "A", "K": "A", "V": "B", "M": "B", "Y": "D", "G": "D", "O": "D"}
AHEAD = {"A": 2, "B": 1, "C": 0, "D": -1}


def stages(p, batches):
    return "".join(x for x in "ABCD" if 0 <= p + AHEAD[x] < batches)


def fills_of(has):
    return [FILLS[u] for u in sorted(FILLS) if STAGE_OF[FILLS[u][0]] in has]


def fills_before(p, batches):
    return sum(len(fills_of(stages(q, batches))) for q in range(-2, p))


def mx_units(u, has, units):
    def late(v):
        return MX_EARLY + min(v, MX_UNTIL) * (units - MX_EARLY) // MX_UNTIL

    def first(v):
        return max(0, v - MX_FROM) * MX_EARLY // (STEPS - MX_FROM)

    found = [(1, k) for k in range(late(u), late(u + 1)) if "B" in has]
    return found + [(2, k) for k in range(first(u), first(u + 1)) if "A" in has]


def wait_past(eng, semaphore, value):
    if not isinstance(value, int) or value > 0:
        eng.wait_ge(semaphore, value)


class Ring:

    def __init__(self, psum, filled, read, order):
        self.psum, self.filled_sem, self.read, self.n = psum, filled, read, len(read)
        self.at = {key: i for i, key in enumerate(order)}

    def bank(self, *key):
        return self.psum[:, self.at[key] % self.n, :]

    def start(self, pe, *key):
        i = self.at[key]
        if i >= self.n:
            pe.wait_ge(self.read[i % self.n], i // self.n)
        return self.bank(*key)

    def filled(self, eng, *key):
        eng.wait_ge(self.filled_sem, self.at[key] + 1)
        return self.bank(*key)

    def reader(self, *key):
        return self.read[self.at[key] % self.n]

    def taken(self, eng, *key):
        i = self.at[key]
        eng.wait_ge(self.read[i % self.n], i // self.n + 1)


def decoder_layer(nc, t, out, comb_dram):
    B, N, D = t["x"].shape
    S = t["ctx_1024"].shape[1]
    H, DH = 16, 8
    E = t["L0_ffn_Wr"].shape[1]
    HID = t["L0_ffn_Wg"].shape[2]
    TOK = B * N
    KT = -(-S // P)
    LAST = S - (KT - 1) * P
    GR = 4
    HG = H // GR
    GW = HG * N
    QW = H * N
    RT = -(-QW // P)
    LASTR = QW - (RT - 1) * P
    CH = 3
    CHW = [S // CH + (1 if c < S % CH else 0) for c in range(CH)]
    CHO = [sum(CHW[:c]) for c in range(CH)]
    UNITS = RT * CH
    MROW = 96
    DEPTH = MROW + RT
    KC = 4
    KCW = S // KC
    TB = 4
    TW = TOK // TB
    BPB = B // TB
    HC = HID // P
    UPE = TB * HC
    VW = DH + 1
    SCALE = float(DH) ** -0.5
    DEPTH_SCALE = 12 ** -0.5
    NF = len(fills_of("ABCD"))
    assert D == P and STEPS == 2 * KT and KC * KCW == S and B % 2 == 0 and GW <= BANK

    def later(batch, k):
        return batch[0] + (batch[1] + k) // 2, (batch[1] + k) % 2

    def num(batch):
        return 2 * batch[0] + batch[1]

    def unit_slot(s, unit):
        return (UNITS * s + unit) % 2

    def w_at(name, n):
        stage = STAGE_OF[name[0]]
        p = n - AHEAD[stage]
        if isinstance(n, int):
            return fills_before(p, B) + fills_of(stages(p, B)).index(name)
        return NF * p + (fills_before(1, B) - NF + fills_of("ABCD").index(name))

    def phases(eng, phase, peeled=2):
        for p in (-2, -1, 0, 1):
            phase((p // 2, p % 2), stages(p, B))
        with eng.Fori(1, (B - peeled) // 2) as j:
            for s in range(2):
                phase((j, s), "ABCD")
        for p in range(B - peeled, B + 1):
            phase((p // 2, p % 2), stages(p, B))

    def widen(ap, n, width):
        return ap.unsqueeze(2).to_broadcast([n, ap.shape[1], width])

    def repeat(ap, n, k):
        return ap.unsqueeze(1).to_broadcast([n, k, ap.shape[1]])

    with ExitStack() as ctx:
        def sb(name, shape, dt=F32, stack=ctx):
            return stack.enter_context(nc.sbuf_tensor(name, shape, dt))

        def sem(name):
            return ctx.enter_context(nc.semaphore(name))

        PS = ctx.enter_context(nc.psum_tensor("PS", [P, 8, BANK], F32))
        score = [PS[:, 2 * h:2 * h + 2, 0:GW] for h in range(2)]
        mxp = [PS[:, 4 + i, :] for i in range(2)]
        pvp = PS[:, 6, 0:GR * N]
        wk = PS[:, 7, :]

        ident = sb("ident", [P, P])
        headmask = sb("headmask", [P, H], F16)
        stackmask = sb("stackmask", [96, HG], F16)
        kvmask = sb("kvmask", [P, P + H])
        rowmask = sb("rowmask", [P, RT], F16)
        minushalf = sb("minushalf", [P, B])
        ones = sb("ones", [P, H])
        before = sb("before", [N, E, E])
        aWq = sb("aWq", [P, P])
        aWo = sb("aWo", [P, P])
        aWkvh = sb("aWkvh", [P, 3 * P])
        abq = sb("abq", [P, 1])
        kvhrow = sb("kvhrow", [N, 3 * P])
        arow = {n: sb("arow_" + n, [N, P]) for n in ("beta", "ln_w", "ln_b", "bo")}
        xW = sb("xW", [P, 5, P])
        xWT = sb("xWT", [P, 5, P])
        WkTg = sb("WkTg", [P, P])
        WvTg = sb("WvTg", [P, P])
        kvg = sb("kvg", [P, 1])
        kvb = sb("kvb", [P, 1])
        kbias = sb("kbias", [P, 1])
        vrow = sb("vrow", [N, P])
        xrow = {n: sb("xrow_" + n, [N, P]) for n in ("qln_g", "qln_b", "bg")}
        Wr = sb("Wr", [P, E])
        X1 = sb("X1", [N, B, P])
        X2 = sb("X2", [N, B, P])
        GATE = sb("GATE", [N, B, P])
        qhi = sb("qhi", [P, TOK], F16)
        qlo = sb("qlo", [P, TOK], F16)
        qrows = sb("qrows", [96, GR, TOK], F16)
        tstat = sb("tstat", [N, B, 6])
        tsm = sb("tsm", [N, 8, B])

        early = ExitStack()
        ct = [sb(f"ct{i}", [P, KT, P], stack=early) for i in range(2)]
        xn = sb("xn", [P, KT, P], stack=early)
        cstat = [sb(f"cstat{i}", [P, KT, 6], stack=early) for i in range(2)]
        csm = sb("csm", [P, 8, KT], stack=early)
        xnT = [sb(f"xnT{i}", [P, S], stack=early) for i in range(2)]
        khi = [sb(f"khi{i}", [P, S], F16, early) for i in range(2)]
        klo = [sb(f"klo{i}", [P, S], F16, early) for i in range(2)]
        ks = [sb(f"ks{i}", [DEPTH, GR, S], F16, early) for i in range(2)]
        vs = [sb(f"vs{i}", [P, KT * H, VW], stack=early) for i in range(2)]
        qbd = [sb(f"qbd{i}", [P, H, N], F16, early) for i in range(2)]
        qs = [sb(f"qs{i}", [DEPTH, RT * P], F16, early) for i in range(2)]
        pr = [sb(f"pr{i}", [P, 2, HG, N], stack=early) for i in range(2)]
        mxs = [sb(f"mxs{i}", [P, RT, CH], stack=early) for i in range(2)]
        mx = sb("mx", [P, RT], stack=early)
        mrow = sb("mrow", [DEPTH, P], F16, early)
        pvs = sb("pvs", [P, GR * N], stack=early)
        rden = sb("rden", [N, GR, HG], stack=early)
        y = sb("y", [N, P], stack=early)
        yT = sb("yT", [P, N], stack=early)
        XT = sb("XT", [P, TOK], stack=early)
        QT = sb("QT", [P, TOK], stack=early)
        KVH = sb("KVH", [N, B, 3 * P], stack=early)
        R = sb("R", [P, 6, P + H], stack=early)
        DEN = sb("DEN", [N, B, H], stack=early)
        early.close()
        late = ExitStack()
        X2T = sb("X2T", [P, TOK], stack=late)
        x2hi = sb("x2hi", [P, TOK], F16, late)
        x2lo = sb("x2lo", [P, TOK], F16, late)
        LG = sb("LG", [N, B, E], stack=late)
        RK = [sb(f"RK{i}", [N, B, E, E], stack=late) for i in range(2)]
        rank = sb("rank", [N, B, E], stack=late)
        ex = sb("ex", [N, B, E], stack=late)
        rsm = sb("rsm", [N, 3, B], stack=late)
        combT = sb("combT", [E, TOK], stack=late)
        cb = [sb(f"cb{i}", [P, TOK], stack=late) for i in range(2)]
        xe = sb("xe", [P, TOK], stack=late)
        xehi = [sb(f"xehi{i}", [P, TOK], F16, late) for i in range(2)]
        xelo = [sb(f"xelo{i}", [P, TOK], F16, late) for i in range(2)]
        wst = [sb(f"wst{i}", [P, 2, HID], stack=late) for i in range(2)]
        whi = [sb(f"whi{i}", [P, 2, HID], F16, late) for i in range(2)]
        wlo = [sb(f"wlo{i}", [P, 2, HID], F16, late) for i in range(2)]
        wd = [sb(f"wd{i}", [P, HC, P], stack=late) for i in range(2)]
        sg = [sb(f"sg{i}", [P, TW], stack=late) for i in range(2)]
        hh = [sb(f"hh{i}", [P, TW], stack=late) for i in range(2)]
        zero = sb("zero", [P, P], F16, late)
        OT = sb("OT", [P, TOK], stack=late)
        late.close()

        x_in, weights_in = sem("x_in"), sem("weights_in")
        consts_done, zeros_done = sem("consts_done"), sem("zeros_done")
        tok_stats, tok_scale = sem("tok_stats"), sem("tok_scale")
        folded, k_done, nd_split, attn_done, x1_pre, qn_done = (
            sem(n) for n in ("folded", "k_done", "nd_split", "attn_done", "x1_pre", "qn_done"))
        qhi_done, gate_done, qrows_in = sem("qhi_done"), sem("gate_done"), sem("qrows_in")
        ctx_in = [sem(f"ctx_in{i}") for i in range(2)]
        ks_in = [sem(f"ks_in{i}") for i in range(2)]
        ctx_stats, ctx_normed, khi_done = sem("ctx_stats"), sem("ctx_normed"), sem("khi_done")
        qbd_done, qs_done = sem("qbd_done"), sem("qs_done")
        mx_filled, mx_reduced, max_done, max_stacked = (
            sem(n) for n in ("mx_filled", "mx_reduced", "max_done", "max_stacked"))
        scored, exp_done, pv_done, pv_copied = (sem(n) for n in ("scored", "exp_done", "pv_done", "pv_copied"))
        y_gated = sem("y_gated")
        w_filled, w_read = sem("w_filled"), sem("w_read")
        x2_done, x2hi_done, logits_less_max, exped, comb_done, comb_stored = (
            sem(n) for n in ("x2_done", "x2hi_done", "logits_less_max", "exped", "comb_done", "comb_stored"))
        cb_in = [sem(f"cb_in{i}") for i in range(2)]
        wst_in = [sem(f"wst_in{i}") for i in range(2)]
        wd_in = [sem(f"wd_in{i}") for i in range(2)]
        xe_done, xehi_done, xelo_done, whi_done, w_split = (sem(n) for n in ("xe_done", "xehi_done", "xelo_done", "whi_done", "w_split"))
        gu_filled, silu_done, h_done, d_done = (sem(n) for n in ("gu_filled", "silu_done", "h_done", "d_done"))
        out_copied, y_done, stored = sem("out_copied"), sem("y_done"), sem("stored")

        kv_nd = []
        for g in range(-(-B // 3) + 1):
            kv_nd += [("kv", b) for b in range(3 * g, min(3 * g + 3, B))]
            kv_nd += [("nd", g - 1)] if g else []
        pre = Ring(PS, sem("pre_filled"), [sem(f"pre_read{i}") for i in range(4)],
                   [("wT",), ("woT",)] + [("xT", k) for k in range(TB)] + [("bias",)] + [("qT", k) for k in range(TB)]
                   + [("kvh", b) for b in range(B)] + kv_nd
                   + [(n, k) for n in ("gT", "o", "qnT", "Q", "gate") for k in range(TB)])
        post = Ring(PS, sem("post_filled"), [sem(f"post_read{i}") for i in range(4)],
                    [("x2T", k) for k in range(TB)] + [("logits",)] + [("cT", k) for k in range(TB)]
                    + [("yN", k) for k in range(TB)])

        block = ctx.enter_context(nc.Block())

        loads = [(xW[:, i, :], t["L0_xattn_" + n]) for i, n in enumerate(("Wq", "Wk", "Wv", "Wg", "Wo"))]
        loads += [(aWq[:, :], t["L0_attn_Wq"]), (aWo[:, :], t["L0_attn_Wo"])]
        loads += [(aWkvh[:, P * i:P * i + P], t["L0_attn_" + n]) for i, n in enumerate(("Wk", "Wv", "Wh"))]
        loads += [(c[:, :], t[n].rearrange("(p o) -> p o", o=1)) for c, n in
                  ((abq, "L0_attn_bq"), (kvg, "L0_xattn_kvln_g"), (kvb, "L0_xattn_kvln_b"))]
        loads += [(kvhrow[:, P * i:P * i + P], t["L0_attn_" + n].partition_broadcast(N))
                  for i, n in enumerate(("bk", "bv", "bh"))]
        loads += [(arow[n][:, :], t["L0_attn_" + n].partition_broadcast(N)) for n in arow]
        loads += [(xrow[n][:, :], t["L0_xattn_" + n].partition_broadcast(N)) for n in xrow]
        loads += [(Wr[:, :], t["L0_ffn_Wr"])]
        WEIGHTS = 16 * len(loads)

        @block.sync
        def _(sp):
            sp.dma_start(X2[:, :, :], t["x"].rearrange("b n d -> n b d")).then_inc(x_in, 16)
            for dst, src in loads:
                sp.dma_start(dst, src).then_inc(weights_in, 16)

            def load_context(batch):
                n, s = num(batch), batch[1]
                if isinstance(n, int) and n < 4:
                    wait_past(sp, ctx_normed, n - 1)
                else:
                    sp.wait_ge(scored, STEPS * (n - 3))
                src = t["ctx_1024"]
                src = src[n] if isinstance(n, int) else src[bass.ds(n, 1)].rearrange("o s d -> (o s) d")
                sp.dma_start(ct[s][:, 0:KT - 1, :],
                             src[0:(KT - 1) * P, :].rearrange("(p t) d -> p t d", p=P)).then_inc(ctx_in[s], 16)
                sp.dma_start(ct[s][0:LAST, KT - 1, :], src[(KT - 1) * P:S, :]).then_inc(ctx_in[s], 16)

            sp.wait_ge(zeros_done, 1)
            load_context((0, 0))
            load_context((0, 1))
            for k in range(TB):
                pre.taken(sp, "Q", k)
            for k, part in enumerate((qhi, qlo, qhi)):
                for g in range(GR):
                    sp.dma_start(qrows[32 * k:32 * k + 32, g, :], part[32 * g:32 * g + 32, :]).then_inc(qrows_in, 16)

            def phase(batch, has):
                ahead = later(batch, 3)
                if not isinstance(batch[0], int) or 2 <= num(ahead) < B:
                    load_context(ahead)
                if "B" in has:
                    n, s = num(later(batch, 1)), later(batch, 1)[1]
                    if isinstance(n, int):
                        sp.wait_ge(w_read, w_at("K3", n) + 1)
                        wait_past(sp, scored, STEPS * (n - 1))
                    for k, part in enumerate((khi, khi, klo)):
                        for g in range(GR):
                            sp.dma_start(ks[s][32 * k:32 * k + 32, g, :], part[s][32 * g:32 * g + 32, :])\
                              .then_inc(ks_in[s], 16)

            phases(sp, phase, peeled=4)

            def load_expert(pair, s):
                e = 2 * pair + s
                if not isinstance(pair, int) or pair > 0:
                    sp.wait_ge(d_done, UPE * (e - 1))
                for i, w in enumerate(("Wg", "Wu")):
                    src = t["L0_ffn_" + w]
                    src = src[e] if isinstance(e, int) else src[bass.ds(e, 1)].rearrange("o c h -> (o c) h")
                    sp.dma_start(wst[s][:, i, :], src).then_inc(wst_in[s], 16)
                src = t["L0_ffn_Wd"]
                src = src[e] if isinstance(e, int) else src[bass.ds(e, 1)].rearrange("o h c -> (o h) c")
                sp.dma_start(wd[s][:, :, :], src.rearrange("(k p) c -> p k c", p=P)).then_inc(wd_in[s], 16)

            def load_comb(pair, s):
                e = 2 * pair + s
                if not isinstance(pair, int) or pair > 0:
                    sp.wait_ge(xe_done, e - 1)
                src = comb_dram[e:e + 1, :] if isinstance(e, int) else comb_dram[bass.ds(e, 1), :]
                sp.dma_start(cb[s][:, :], src.to_broadcast([P, TOK])).then_inc(cb_in[s], 16)

            sp.wait_ge(x2_done, 1)
            for s in range(2):
                load_expert(0, s)
            for k in range(TB):
                post.taken(sp, "cT", k)
            sp.dma_start(comb_dram, combT[:, :]).then_inc(comb_stored, 16)
            sp.wait_ge(comb_stored, 16)
            for s in range(2):
                load_comb(0, s)
            with sp.Fori(1, E // 2) as j:
                for s in range(2):
                    load_comb(j, s)
                    load_expert(j, s)
            sp.wait_ge(y_done, 1)
            sp.dma_start(out.rearrange("b n d -> n b d"), X2[:, :, :]).then_inc(stored, 16)
            sp.wait_ge(stored, 16)

        def moments(pool, stat, small, n, k):
            r = [small[0:n, i, 0:k] for i in range(8)]
            st = [stat[0:n, 0:k, i] for i in range(6)]
            nc.gpsimd.tensor_tensor(r[2], st[1], st[4], ALU.add)
            nc.gpsimd.tensor_tensor(r[3], st[1], st[4], ALU.subtract)
            nc.gpsimd.tensor_tensor(r[4], st[2], st[5], ALU.add)
            pool.drain()
            nc.gpsimd.tensor_scalar(r[0], r[2], 0.5, None, ALU.mult)
            nc.gpsimd.tensor_scalar(r[5], r[3], 0.5, None, ALU.mult)
            nc.gpsimd.tensor_scalar(r[6], r[4], 1.0 / D, EPS, ALU.mult, ALU.add)
            pool.drain()
            nc.gpsimd.tensor_tensor(r[7], r[5], r[5], ALU.mult)
            pool.drain()
            nc.gpsimd.tensor_tensor(r[2], r[7], r[6], ALU.add)
            pool.drain()
            return nc.gpsimd.tensor_tensor(r[1], r[2], minushalf[0:n, 0:k], ALU.pow)

        @block.gpsimd
        def _(pool):
            nc.gpsimd.memset(ident[:, :], 0.0)
            nc.gpsimd.memset(headmask[:, :], 1.0)
            nc.gpsimd.memset(kvmask[:, :], 0.0)
            nc.gpsimd.memset(rowmask[:, :], 0.0)
            nc.gpsimd.memset(minushalf[:, :], -0.5)
            nc.gpsimd.memset(before[:, :, :], 1.0)
            pool.drain()
            nc.gpsimd.affine_select(out=ident[:, :], in_=ident[:, :], compare_op=ALU.not_equal, fill=1.0,
                                    base=0, pattern=[[-1, P]], channel_multiplier=1)
            nc.gpsimd.affine_select(out=rowmask[:, :], in_=rowmask[:, :], compare_op=ALU.not_equal, fill=1.0,
                                    base=-MROW, pattern=[[-1, RT]], channel_multiplier=1)
            nc.gpsimd.affine_select(out=headmask[:, :], in_=headmask[:, :], compare_op=ALU.is_ge, fill=0.0,
                                    base=0, pattern=[[-DH, H]], channel_multiplier=1)
            nc.gpsimd.affine_select(out=before[:, :, :], in_=before[:, :, :], compare_op=ALU.is_gt, fill=0.0,
                                    base=0, pattern=[[1, E], [-1, E]], channel_multiplier=0)
            pool.drain()
            nc.gpsimd.affine_select(out=headmask[:, :], in_=headmask[:, :], compare_op=ALU.is_ge, fill=0.0,
                                    base=DH - 1, pattern=[[DH, H]], channel_multiplier=-1)
            for k in range(1 - P // H, P // H):
                nc.gpsimd.affine_select(out=kvmask[:, 0:P], in_=kvmask[:, 0:P], compare_op=ALU.not_equal, fill=1.0,
                                        base=-H * k, pattern=[[-1, P]], channel_multiplier=1)
                pool.drain()
            nc.gpsimd.tensor_copy(kvmask[:, P:P + H], kvmask[:, 0:H])
            for k in range(3):
                pool.drain()
                nc.gpsimd.tensor_copy(stackmask[32 * k:32 * k + 32, :], headmask[0:32, 0:HG])
            pool.drain()
            nc.gpsimd.memset(ones[:, :], 1.0).then_inc(consts_done, 1)

            def token_moments(count):
                pool.wait_ge(tok_stats, count)
                moments(pool, tstat, tsm, N, B).then_inc(tok_scale, 1)

            def norm_context(batch):
                n, s = num(batch), batch[1]
                pool.wait_ge(ctx_stats, n + 1)
                moments(pool, cstat[s], csm, P, KT)
                pool.drain()
                nc.gpsimd.tensor_tensor(ct[s][:, :, :], ct[s][:, :, :], widen(csm[:, 0, :], P, P), ALU.subtract)
                pool.drain()
                if not isinstance(n, int) or n > 0:
                    pool.wait_ge(w_filled, w_at("T2", n - 1) + 1)
                nc.gpsimd.tensor_tensor(xn[:, :, :], ct[s][:, :, :], widen(csm[:, 1, :], P, P), ALU.mult)\
                  .then_inc(ctx_normed, 1)

            def place_queries(batch):
                n, s = num(batch), batch[1]
                wait_past(pool, mx_filled, UNITS * (n - 1))
                src = qhi[:, n * N:n * N + N] if isinstance(n, int) else qhi[:, bass.ds(n * N, N)]
                nc.gpsimd.tensor_tensor(qbd[s][:, :, :], repeat(src, P, H), widen(headmask[:, :], P, N), ALU.mult)\
                  .then_inc(qbd_done, 1)

            for count in (1, 2):
                token_moments(count)
            for k in range(TB):
                pre.taken(pool, "Q", k)

            def phase(batch, has):
                n, s = num(later(batch, 1)), later(batch, 1)[1]
                if "D" in has:
                    m = num(later(batch, -1))
                    pool.wait_ge(w_read, w_at("Y0", m) + 1)
                    nc.gpsimd.tensor_tensor(y[:, :], y[:, :], vrow[:, :], ALU.add)
                    pool.drain()
                    if isinstance(m, int) and m == 0:
                        pool.wait_ge(gate_done, 1)
                    gate = GATE[:, m, :] if isinstance(m, int) else GATE[:, bass.ds(m, 1), :].rearrange("p o d -> p (o d)")
                    nc.gpsimd.tensor_tensor(y[:, :], y[:, :], gate, ALU.mult).then_inc(y_gated, 1)
                if "B" in has:
                    if isinstance(n, int) and n == 0:
                        pool.wait_ge(qrows_in, 16 * 3 * GR)
                    wait_past(pool, scored, STEPS * (n - 1))
                    for g in range(GR):
                        src = qrows[:, g, n * N:n * N + N] if isinstance(n, int) else qrows[:, g, bass.ds(n * N, N)]
                        last = nc.gpsimd.tensor_tensor(
                            qs[s][0:96, g * GW:g * GW + GW].rearrange("p (h q) -> p h q", h=HG),
                            repeat(src, 96, HG), widen(stackmask[:, :], 96, N), ALU.mult)
                    last.then_inc(qs_done, 1)
                if "A" in has:
                    place_queries(later(batch, 2))
                if "B" in has:
                    pool.drain()
                    pool.wait_ge(w_read, w_at("M0", n) + 1)
                    nc.gpsimd.tensor_tensor(qs[s][MROW:DEPTH, :].rearrange("p (c q) -> p c q", q=P),
                                            repeat(mrow[MROW:DEPTH, :], RT, RT), widen(rowmask[MROW:DEPTH, :], RT, P),
                                            ALU.mult).then_inc(max_stacked, 1)
                    pool.drain()
                if not isinstance(batch[0], int) or num(batch) + 3 < B:
                    norm_context(later(batch, 3))

            norm_context((0, 0))
            phases(pool, phase, peeled=4)
            token_moments(3)

            def split(pair, s):
                pool.wait_ge(wst_in[s], 32 * (pair + 1))
                if not isinstance(pair, int) or pair > 0:
                    pool.wait_ge(d_done, UPE * (2 * pair + s - 1))
                pool.wait_ge(whi_done, 2 * pair + s + 1)
                nc.gpsimd.tensor_tensor(wlo[s][:, :, :], wst[s][:, :, :], whi[s][:, :, :], ALU.subtract)\
                  .then_inc(w_split, 1)

            for s in range(2):
                split(0, s)
            with pool.Fori(1, E // 2) as j:
                for s in range(2):
                    split(j, s)
            token_moments(4)

        @block.scalar
        def _(act):
            act.wait_ge(weights_in, WEIGHTS)
            for k in range(TB):
                src = pre.filled(act, "xT", k)
                nc.scalar.activation(XT[:, TW * k:TW * k + TW], src[:, 0:TW], ACT.Copy).then_inc(pre.reader("xT", k), 1)
            for k in range(TB):
                src = pre.filled(act, "qT", k)
                nc.scalar.activation(QT[:, TW * k:TW * k + TW], src[:, 0:TW], ACT.Sigmoid, bias=abq[:, 0:1])\
                  .then_inc(pre.reader("qT", k), 1)
            for k in range(TB):
                for b in range(BPB * k, BPB * k + BPB):
                    pre.taken(act, "kvh", b)
                keys = KVH[:, BPB * k:BPB * k + BPB, 0:P]
                nc.scalar.activation(keys, keys, ACT.Sigmoid).then_inc(k_done, 1)
            for g in range(-(-B // 3)):
                src = pre.filled(act, "nd", g)
                k = min(3, B - 3 * g)
                src = src[0:N, 0:k * (P + H)].rearrange("p (b c) -> p b c", b=k)
                nc.scalar.activation(GATE[:, 3 * g:3 * g + k, :], src[:, :, 0:P], ACT.Copy)
                nc.scalar.activation(DEN[:, 3 * g:3 * g + k, :], src[:, :, P:P + H], ACT.Copy)\
                  .then_inc(pre.reader("nd", g), 1)
                act.wait_ge(pre.reader("nd", g), pre.at["nd", g] // 4 + 1)
            act.sem_inc(nd_split, 1)
            for name in ("gT", "qnT"):
                for k in range(TB):
                    src = pre.filled(act, name, k)
                    nc.scalar.activation(XT[:, TW * k:TW * k + TW], src[:, 0:TW], ACT.Copy)\
                      .then_inc(pre.reader(name, k), 1)
            for k in range(TB):
                src = pre.filled(act, "Q", k)
                nc.scalar.activation(qhi[:, TW * k:TW * k + TW], src[:, 0:TW], ACT.Copy).then_inc(qhi_done, 1)
            for k in range(TB):
                pre.taken(act, "gate", k)
            nc.scalar.activation(GATE[:, :, :], GATE[:, :, :], ACT.Sigmoid).then_inc(gate_done, 1)
            pre.taken(act, "bias")

            def read_work(name, batch):
                n, s = num(batch), batch[1]
                kind, k = name[0], int(name[1])
                act.wait_ge(w_filled, w_at(name, n) + 1)
                if kind == "T":
                    w = min(4 * P, S - 4 * P * k)
                    nc.scalar.activation(xnT[s][:, 4 * P * k:4 * P * k + w], wk[:, 0:w], ACT.Copy).then_inc(w_read, 1)
                if kind == "K":
                    if k == 0:
                        wait_past(act, mx_filled, UNITS * (n - 1))
                        if not isinstance(batch[0], int) or batch[0] > 0:
                            act.wait_ge(ks_in[s], 16 * 3 * GR * batch[0])
                    nc.scalar.activation(khi[s][:, KCW * k:KCW * k + KCW], wk[:, 0:KCW], ACT.Identity,
                                         bias=kbias[:, 0:1]).then_inc(khi_done, 1)
                if kind == "V":
                    if k == 0:
                        wait_past(act, pv_done, STEPS * (n - 1))
                    full = min(4, KT - 1 - 4 * k)
                    dst = vs[s][:, 4 * k * H:(4 * k + full) * H, 0:DH]
                    ins = nc.scalar.activation(dst, wk[:, 0:full * P].rearrange("p (h d) -> p h d", d=DH), ACT.Copy)
                    if full < 4:
                        ins = nc.scalar.activation(vs[s][0:LAST, (KT - 1) * H:KT * H, 0:DH],
                                                   wk[0:LAST, full * P:full * P + P].rearrange("p (h d) -> p h d", d=DH),
                                                   ACT.Copy)
                    ins.then_inc(w_read, 1)
                if kind == "G":
                    nc.scalar.activation(yT[:, :], wk[:, 0:N], ACT.Copy).then_inc(w_read, 1)

            def phase(batch, has):
                for u in range(STEPS):
                    if "C" in has:
                        n, h, w = num(batch), u % 2, P if u // 2 < KT - 1 else LAST
                        act.wait_ge(scored, STEPS * n + u + 1)
                        wait_past(act, pv_done, STEPS * n + u - 1)
                        nc.scalar.activation(pr[h][0:w, :, :, :].rearrange("p g h q -> p g (h q)"), score[h][0:w],
                                             ACT.Exp, scale=SCALE).then_inc(exp_done, 1)
                    name = FILLS.get(u)
                    if name and name[0] in "TKVG" and STAGE_OF[name[0]] in has:
                        read_work(name, later(batch, AHEAD[STAGE_OF[name[0]]]))

            act.wait_ge(zeros_done, 1)
            phases(act, phase)

            act.wait_ge(x2_done, 1)
            for k in range(TB):
                src = post.filled(act, "x2T", k)
                nc.scalar.activation(X2T[:, TW * k:TW * k + TW], src[:, 0:TW], ACT.Copy)
                nc.scalar.activation(x2hi[:, TW * k:TW * k + TW], src[:, 0:TW], ACT.Copy).then_inc(x2hi_done, 1)
            act.wait_ge(logits_less_max, 1)
            nc.scalar.activation(ex[:, :, :], ex[:, :, :], ACT.Exp).then_inc(exped, 1)
            for k in range(TB):
                src = post.filled(act, "cT", k)
                nc.scalar.activation(combT[:, TW * k:TW * k + TW], src[0:E, 0:TW], ACT.Copy)\
                  .then_inc(post.reader("cT", k), 1)

            def expert(pair, s):
                e = 2 * pair + s
                if not isinstance(pair, int) or pair > 0:
                    act.wait_ge(d_done, UPE * (e - 1))
                act.wait_ge(wst_in[s], 32 * (pair + 1))
                nc.scalar.activation(whi[s][:, :, :], wst[s][:, :, :], ACT.Copy).then_inc(whi_done, 1)
                act.wait_ge(xe_done, e + 1)
                nc.scalar.activation(xehi[s][:, :], xe[:, :], ACT.Copy).then_inc(xehi_done, 1)
                for i in range(UPE):
                    act.wait_ge(gu_filled, UPE * e + i + 1)
                    if not isinstance(pair, int) or pair > 0 or UPE * s + i >= 2:
                        act.wait_ge(h_done, UPE * e + i - 1)
                    nc.scalar.activation(sg[i % 2][:, :], PS[:, 2 * (i % 2), 0:TW], ACT.Silu).then_inc(silu_done, 1)

            expert(0, 0)
            expert(0, 1)
            with act.Fori(1, E // 2) as j:
                for s in range(2):
                    expert(j, s)
            act.wait_ge(d_done, UPE * E)
            for k in range(TB):
                nc.scalar.activation(OT[:, TW * k:TW * k + TW], PS[:, 4 + k, 0:TW], ACT.Copy).then_inc(out_copied, 1)

        @block.vector
        def _(dve):
            for s in range(2):
                nc.vector.memset(ct[s][:, KT - 1, :], 0.0)
                nc.vector.memset(cstat[s][:, KT - 1, :], 0.0)
                nc.vector.memset(mxs[s][:, :, :], 0.0)
                nc.vector.memset(ks[s][MROW:DEPTH, :, :], 1.0)
                nc.vector.memset(vs[s][:, :, :], 0.0)
                dve.drain()
                nc.vector.memset(vs[s][:, 0:(KT - 1) * H, DH:VW], 1.0)
                nc.vector.memset(vs[s][0:LAST, (KT - 1) * H:KT * H, DH:VW], 1.0)
            nc.vector.memset(pvp, 0.0).then_inc(zeros_done, 1)

            def token_norm(src, dst, count):
                for b in range(B):
                    last = nc.vector.bn_stats(tstat[:, b, :], src[:, b, :])
                last.then_inc(tok_stats, 1)
                dve.wait_ge(tok_scale, count)
                nc.vector.tensor_tensor(dst[:, :, :], src[:, :, :], widen(tsm[:, 0, :], N, P), ALU.subtract)
                dve.drain()
                return nc.vector.tensor_tensor(dst[:, :, :], dst[:, :, :], widen(tsm[:, 1, :], N, P), ALU.mult)

            dve.wait_ge(weights_in, WEIGHTS)
            src = pre.filled(dve, "wT")
            nc.vector.tensor_copy(xWT[:, 0:4, :], src.rearrange("p (i c) -> p i c", i=4)).then_inc(pre.reader("wT"), 1)
            src = pre.filled(dve, "woT")
            nc.vector.tensor_copy(xWT[:, 4, :], src[:, 0:P]).then_inc(pre.reader("woT"), 1)
            dve.drain()
            nc.vector.tensor_scalar(WkTg[:, :], xWT[:, 1, :], kvg[:, 0:1], None, ALU.mult)
            for h in range(2):
                half = slice(h * P // 2, (h + 1) * P // 2)
                last = nc.vector.tensor_scalar(WvTg[:, half].rearrange("p (c g d) -> p c g d", c=HG, g=2),
                                               xWT[:, 2, half].rearrange("p (g c d) -> p c g d", c=HG, g=2),
                                               kvg[:, 0:1], None, ALU.mult)
            last.then_inc(folded, 1)
            src = pre.filled(dve, "bias")
            nc.vector.tensor_copy(kbias[:, :], src[:, 0:1])
            nc.vector.tensor_copy(vrow[:, :], src[0:N, P:2 * P]).then_inc(pre.reader("bias"), 1)
            for b in range(B):
                src = pre.filled(dve, "kvh", b)
                nc.vector.tensor_tensor(KVH[:, b, :], src[0:N, 0:3 * P], kvhrow[:, :], ALU.add)\
                  .then_inc(pre.reader("kvh", b), 1)
            dve.wait_ge(consts_done, 1)
            for b in range(B):
                src = pre.filled(dve, "kv", b)
                if b >= 6:
                    pre.filled(dve, "nd", (b - 6) // 3)
                nc.vector.tensor_tensor(R[:, b % 6, :], src[:, 0:P + H], kvmask[:, :], ALU.mult)\
                  .then_inc(pre.reader("kv", b), 1)
            dve.wait_ge(nd_split, 1)
            nc.vector.reciprocal(DEN[:, :, :], DEN[:, :, :])
            dve.drain()
            for b in range(B):
                att = GATE[:, b, :].rearrange("p (m h) -> p m h", h=H)
                nc.vector.tensor_tensor(att, att, repeat(DEN[:, b, :], N, P // H), ALU.mult)
            dve.drain()
            token_norm(GATE, GATE, 1)
            dve.drain()
            nc.vector.tensor_tensor(GATE[:, :, :], GATE[:, :, :], repeat(arow["ln_w"][:, :], N, B), ALU.mult)
            nc.vector.tensor_tensor(KVH[:, :, 2 * P:3 * P], KVH[:, :, 2 * P:3 * P],
                                    repeat(arow["beta"][:, :], N, B), ALU.add)
            dve.drain()
            nc.vector.tensor_tensor(GATE[:, :, :], GATE[:, :, :], repeat(arow["ln_b"][:, :], N, B), ALU.add)
            dve.drain()
            nc.vector.tensor_tensor(GATE[:, :, :], GATE[:, :, :], KVH[:, :, 2 * P:3 * P], ALU.mult).then_inc(attn_done, 1)
            for k in range(TB):
                src = pre.filled(dve, "o", k)
                blk = slice(BPB * k, BPB * k + BPB)
                nc.vector.tensor_tensor(GATE[:, blk, :], src[0:N, :].rearrange("p (b c) -> p b c", b=BPB),
                                        repeat(arow["bo"][:, :], N, BPB), ALU.add).then_inc(pre.reader("o", k), 1)
                dve.drain()
                if k == 0:
                    dve.wait_ge(x_in, 16)
                nc.vector.scalar_tensor_tensor(X1[:, blk, :], GATE[:, blk, :], 0.0, X2[:, blk, :], ALU.max, ALU.add)
            dve.drain()
            token_norm(X1, X1, 2)
            dve.drain()
            nc.vector.tensor_tensor(GATE[:, :, :], X1[:, :, :], repeat(xrow["qln_g"][:, :], N, B), ALU.mult)
            dve.drain()
            nc.vector.tensor_tensor(GATE[:, :, :], GATE[:, :, :], repeat(xrow["qln_b"][:, :], N, B), ALU.add)\
              .then_inc(qn_done, 1)
            for k in range(TB):
                src = pre.filled(dve, "Q", k)
                dve.wait_ge(qhi_done, k + 1)
                cols = slice(TW * k, TW * k + TW)
                nc.vector.tensor_tensor(qlo[:, cols], src[:, 0:TW], qhi[:, cols], ALU.subtract)\
                  .then_inc(pre.reader("Q", k), 1)
            for k in range(TB):
                src = pre.filled(dve, "gate", k)
                nc.vector.tensor_tensor(GATE[:, BPB * k:BPB * k + BPB, :], src[0:N, :].rearrange("p (b c) -> p b c", b=BPB),
                                        repeat(xrow["bg"][:, :], N, BPB), ALU.add).then_inc(pre.reader("gate", k), 1)

            def context_stats(batch, tiles):
                n, s = num(batch), batch[1]
                for k in tiles:
                    if k == 0:
                        dve.wait_ge(ctx_in[s], 32 * (batch[0] + 1))
                    w = P if k < KT - 1 else LAST
                    ins = nc.vector.bn_stats(cstat[s][0:w, k, :], ct[s][0:w, k, :])
                    if k == KT - 1:
                        ins.then_inc(ctx_stats, 1)

            def read_work(name, batch):
                n, s = num(batch), batch[1]
                kind, k = name[0], int(name[1])
                dve.wait_ge(w_filled, w_at(name, n) + 1)
                if kind == "K":
                    dve.wait_ge(khi_done, KC * n + k + 1)
                    cols = slice(KCW * k, KCW * k + KCW)
                    nc.vector.scalar_tensor_tensor(klo[s][:, cols], wk[:, 0:KCW], kbias[:, 0:1], khi[s][:, cols],
                                                   ALU.add, ALU.subtract).then_inc(w_read, 1)
                if kind == "M":
                    nc.vector.tensor_scalar(mrow[MROW:DEPTH, :], wk[MROW:DEPTH, 0:P], -1.0, None, ALU.mult).then_inc(w_read, 1)
                if kind == "Y":
                    blocks = wk[0:N, :].rearrange("p (h g c i) -> p g h c i", h=2, g=2, c=HG)
                    for g in range(2):
                        nc.vector.reciprocal(rden[:, g::2, :], blocks[:, g, :, :, VW * g + DH])
                    dve.drain()
                    yv = y[:, :].rearrange("p (h g c d) -> p g h c d", h=2, g=2, c=HG)
                    for h in range(2):
                        for g in range(2):
                            ins = nc.vector.tensor_tensor(
                                yv[:, g, h], blocks[:, g, h, :, VW * g:VW * g + DH],
                                widen(rden[:, 2 * h + g, :], N, DH), ALU.mult)
                    ins.then_inc(w_read, 1)
                if kind == "O":
                    at = (slice(n, n + 1) if isinstance(n, int) else bass.ds(n, 1))
                    nc.vector.tensor_tensor(X2[:, at, :].rearrange("p o d -> p (o d)"), wk[0:N, 0:P],
                                            X1[:, at, :].rearrange("p o d -> p (o d)"), ALU.add).then_inc(w_read, 1)

            def phase(batch, has):
                for u in range(STEPS):
                    if u == 0 and "D" in has:
                        n = num(later(batch, -1))
                        dve.wait_ge(pv_done, STEPS * (n + 1))
                        if not isinstance(n, int) or n > 0:
                            dve.wait_ge(w_filled, w_at("Y0", n - 1) + 1)
                        nc.vector.tensor_copy(pvs[:, :], pvp).then_inc(pv_copied, 1)
                    name = FILLS.get(u)
                    if name and name[0] in "YO" and STAGE_OF[name[0]] in has:
                        read_work(name, later(batch, AHEAD[STAGE_OF[name[0]]]))
                    for ahead, unit in mx_units(u, has, UNITS):
                        n, s = num(later(batch, ahead)), later(batch, ahead)[1]
                        rt, c = unit // CH, unit % CH
                        w = P if rt < RT - 1 else LASTR
                        dve.wait_ge(mx_filled, UNITS * n + unit + 1)
                        nc.vector.reduce_max(mxs[s][0:w, rt, c:c + 1], mxp[unit_slot(s, unit)][0:w, 0:CHW[c]], AXL.X)\
                          .then_inc(mx_reduced, 1)
                        if unit == UNITS - 1:
                            dve.drain()
                            nc.vector.reduce_max(mx[:, :], mxs[s][:, :, :], AXL.X).then_inc(max_done, 1)
                    k = u - STATS_FROM
                    if 0 <= k < KT // 2 and (not isinstance(batch[0], int) or num(batch) + 3 < B):
                        context_stats(later(batch, 3), (2 * k, 2 * k + 1))
                    if name and name[0] in "KM" and STAGE_OF[name[0]] in has:
                        read_work(name, later(batch, AHEAD[STAGE_OF[name[0]]]))

            context_stats((0, 0), range(KT))
            phases(dve, phase, peeled=4)

            dve.drain()
            token_norm(X2, X2, 3).then_inc(x2_done, 1)
            for k in range(TB):
                src = post.filled(dve, "x2T", k)
                dve.wait_ge(x2hi_done, k + 1)
                cols = slice(TW * k, TW * k + TW)
                nc.vector.tensor_tensor(x2lo[:, cols], src[:, 0:TW], x2hi[:, cols], ALU.subtract)\
                  .then_inc(post.reader("x2T", k), 1)
            nc.vector.memset(zero[:, :], 0.0)
            src = post.filled(dve, "logits")
            nc.vector.tensor_copy(LG[:, :, :], src[0:N, 0:B * E].rearrange("p (b e) -> p b e", b=B))\
              .then_inc(post.reader("logits"), 1)
            dve.drain()
            shape = [N, B, E, E]
            other, own = LG[:, :, :].unsqueeze(2).to_broadcast(shape), LG[:, :, :].unsqueeze(3).to_broadcast(shape)
            nc.vector.reduce_max(rsm[:, 0, :], LG[:, :, :], AXL.X)
            nc.vector.tensor_tensor(RK[0][:, :, :, :], other, own, ALU.is_gt)
            nc.vector.tensor_tensor(RK[1][:, :, :, :], other, own, ALU.is_equal)
            dve.drain()
            nc.vector.tensor_tensor(ex[:, :, :], LG[:, :, :], widen(rsm[:, 0, :], N, E), ALU.subtract)\
              .then_inc(logits_less_max, 1)
            nc.vector.tensor_tensor(RK[1][:, :, :, :], RK[1][:, :, :, :],
                                    before[:, :, :].unsqueeze(1).to_broadcast(shape), ALU.mult)
            dve.drain()
            nc.vector.tensor_tensor(RK[0][:, :, :, :], RK[0][:, :, :, :], RK[1][:, :, :, :], ALU.add)
            dve.drain()
            nc.vector.reduce_sum(rank[:, :, :], RK[0][:, :, :, :], AXL.X)
            dve.drain()
            dve.wait_ge(exped, 1)
            nc.vector.scalar_tensor_tensor(ex[:, :, :], rank[:, :, :], 1.5, ex[:, :, :], ALU.is_lt, ALU.mult)
            dve.drain()
            nc.vector.reduce_sum(rsm[:, 1, :], ex[:, :, :], AXL.X)
            dve.drain()
            nc.vector.reciprocal(rsm[:, 2, :], rsm[:, 1, :])
            dve.drain()
            nc.vector.tensor_scalar(rsm[:, 1, :], rsm[:, 2, :], DEPTH_SCALE, None, ALU.mult)
            dve.drain()
            nc.vector.tensor_tensor(ex[:, :, :], ex[:, :, :], widen(rsm[:, 1, :], N, E), ALU.mult).then_inc(comb_done, 1)

            def scale_tokens(pair, s):
                e = 2 * pair + s
                dve.wait_ge(cb_in[s], 16 * (pair + 1))
                if not isinstance(pair, int) or pair > 0:
                    dve.wait_ge(d_done, UPE * (e - 1))
                nc.vector.tensor_tensor(xe[:, :], X2T[:, :], cb[s][:, :], ALU.mult).then_inc(xe_done, 1)
                dve.wait_ge(xehi_done, e + 1)
                nc.vector.tensor_tensor(xelo[s][:, :], xe[:, :], xehi[s][:, :], ALU.subtract).then_inc(xelo_done, 1)

            def expert(pair, s):
                e = 2 * pair + s
                scale_tokens(pair, s)
                for i in range(UPE):
                    dve.wait_ge(silu_done, UPE * e + i + 1)
                    if not isinstance(pair, int) or pair > 0 or UPE * s + i >= 2:
                        dve.wait_ge(d_done, UPE * e + i - 1)
                    nc.vector.tensor_tensor(hh[i % 2][:, :], sg[i % 2][:, :], PS[:, 2 * (i % 2) + 1, 0:TW], ALU.mult)\
                      .then_inc(h_done, 1)

            dve.drain()
            expert(0, 0)
            expert(0, 1)
            with dve.Fori(1, E // 2) as j:
                for s in range(2):
                    expert(j, s)
            for k in range(TB):
                src = post.filled(dve, "yN", k)
                blk = slice(BPB * k, BPB * k + BPB)
                nc.vector.tensor_tensor(X2[:, blk, :], X2[:, blk, :], src[0:N, :].rearrange("p (b c) -> p b c", b=BPB),
                                        ALU.add).then_inc(post.reader("yN", k), 1)
            dve.drain()
            token_norm(X2, X2, 4).then_inc(y_done, 1)

        @block.tensor
        def _(pe):
            def transpose_tokens(ring, name, src):
                for k in range(TB):
                    dst = ring.start(pe, name, k)
                    for i in range(BPB):
                        last = nc.tensor.transpose(dst[:, N * i:N * i + N], src[:, BPB * k + i, :], ident[0:N, 0:N])
                    last.then_inc(ring.filled_sem, 1)

            def project(ring, name, rhs):
                for k in range(TB):
                    dst = ring.start(pe, name, k)
                    for i in range(BPB):
                        b = BPB * k + i
                        last = nc.tensor.matmul(dst[0:N, P * i:P * i + P], XT[:, N * b:N * b + N], rhs, start=True, stop=True)
                    last.then_inc(ring.filled_sem, 1)

            pe.wait_ge(consts_done, 1)
            pe.wait_ge(weights_in, WEIGHTS)
            dst = pre.start(pe, "wT")
            for i in range(4):
                last = nc.tensor.transpose(dst[:, P * i:P * i + P], xW[:, i, :], ident[:, :])
            last.then_inc(pre.filled_sem, 1)
            nc.tensor.transpose(pre.start(pe, "woT")[:, 0:P], xW[:, 4, :], ident[:, :]).then_inc(pre.filled_sem, 1)
            pe.wait_ge(x_in, 16)
            transpose_tokens(pre, "xT", X2)
            dst = pre.start(pe, "bias")
            pre.taken(pe, "wT")
            nc.tensor.matmul(dst[:, 0:1], xWT[:, 1, :], kvb[:, 0:1], start=True, stop=True)
            nc.tensor.matmul(dst[0:N, P:2 * P], kvb[:, 0:1].to_broadcast([P, N]), xWT[:, 2, :], start=True, stop=True)\
              .then_inc(pre.filled_sem, 1)
            for k in range(TB):
                pre.taken(pe, "xT", k)
                nc.tensor.matmul(pre.start(pe, "qT", k)[:, 0:TW], aWq[:, :], XT[:, TW * k:TW * k + TW], start=True, stop=True)\
                  .then_inc(pre.filled_sem, 1)
            for b in range(B):
                nc.tensor.matmul(pre.start(pe, "kvh", b)[0:N, 0:3 * P], XT[:, N * b:N * b + N], aWkvh[:, :],
                                 start=True, stop=True).then_inc(pre.filled_sem, 1)
            for k in range(TB):
                pre.taken(pe, "qT", k)
            for name, b in kv_nd:
                dst = pre.start(pe, name, b)
                if name == "kv":
                    pe.wait_ge(k_done, b // BPB + 1)
                    keys = KVH[:, b, 0:P]
                    nc.tensor.matmul(dst[:, 0:P], keys, KVH[:, b, P:2 * P], start=True, stop=True)
                    last = nc.tensor.matmul(dst[:, P:P + H], keys, ones[0:N, :], start=True, stop=True)
                else:
                    for i in range(min(3, B - 3 * b)):
                        c = 3 * b + i
                        pre.taken(pe, "kv", c)
                        last = nc.tensor.matmul(dst[0:N, (P + H) * i:(P + H) * (i + 1)], QT[:, N * c:N * c + N],
                                                R[:, c % 6, :], start=True, stop=True)
                last.then_inc(pre.filled_sem, 1)
            pe.wait_ge(attn_done, 1)
            transpose_tokens(pre, "gT", GATE)
            for k in range(TB):
                pre.taken(pe, "gT", k)
            project(pre, "o", aWo[:, :])
            pe.wait_ge(qn_done, 1)
            transpose_tokens(pre, "qnT", GATE)
            for k in range(TB):
                pre.taken(pe, "qnT", k)
                nc.tensor.matmul(pre.start(pe, "Q", k)[:, 0:TW], xWT[:, 0, :], XT[:, TW * k:TW * k + TW],
                                 start=True, stop=True).then_inc(pre.filled_sem, 1)
            project(pre, "gate", xWT[:, 3, :])
            for k in range(TB):
                pre.taken(pe, "gate", k)
            pre.taken(pe, "woT")
            pe.wait_ge(zeros_done, 1)
            pe.wait_ge(folded, 1)

            def fill_work(name, batch):
                n, s = num(batch), batch[1]
                kind, k = name[0], int(name[1])
                wait_past(pe, w_read, w_at(name, n))
                if kind == "T":
                    if k == 0:
                        pe.wait_ge(ctx_normed, n + 1)
                    for i in range(4 * k, min(4 * k + 4, KT)):
                        w = P if i < KT - 1 else LAST
                        last = nc.tensor.transpose(wk[:, P * (i - 4 * k):P * (i - 4 * k) + w], xn[0:w, i, :], ident[0:w, 0:w])
                if kind == "K":
                    last = nc.tensor.matmul(wk[:, 0:KCW], WkTg[:, :], xnT[s][:, KCW * k:KCW * k + KCW], start=True, stop=True)
                if kind == "V":
                    for i in range(4 * k, min(4 * k + 4, KT)):
                        w = P if i < KT - 1 else LAST
                        last = nc.tensor.matmul(wk[0:w, P * (i - 4 * k):P * (i - 4 * k) + P], xnT[s][:, P * i:P * i + w],
                                                WvTg[:, :], start=True, stop=True)
                if kind == "M":
                    pe.wait_ge(max_done, n + 1)
                    last = nc.tensor.matmul(wk[MROW:DEPTH, 0:P], mx[:, :], ident[:, :], start=True, stop=True)
                if kind == "Y":
                    pe.wait_ge(pv_copied, n + 1)
                    for g in range(GR):
                        last = nc.tensor.transpose(wk[0:N, P * g:P * g + P], pvs[:, N * g:N * g + N], ident[:, :])
                if kind == "G":
                    pe.wait_ge(y_gated, n + 1)
                    last = nc.tensor.transpose(wk[:, 0:N], y[:, :], ident[0:N, 0:N])
                if kind == "O":
                    pe.wait_ge(w_read, w_at("G0", n) + 1)
                    last = nc.tensor.matmul(wk[0:N, 0:P], yT[:, :], xWT[:, 4, :], start=True, stop=True)
                last.then_inc(w_filled, 1)

            def max_unit(batch, unit):
                n, s = num(batch), batch[1]
                rt, c = unit // CH, unit % CH
                w = P if rt < RT - 1 else LASTR
                if unit == 0:
                    pe.wait_ge(qbd_done, n + 1)
                    pe.wait_ge(khi_done, KC * (n + 1))
                wait_past(pe, mx_reduced, UNITS * n + unit - 1)
                rows = qbd[s][:, :, :].rearrange("p h q -> p (h q)")[:, P * rt:P * rt + w]
                nc.tensor.matmul(mxp[unit_slot(s, unit)][0:w, 0:CHW[c]], rows, khi[s][:, CHO[c]:CHO[c] + CHW[c]],
                                 start=True, stop=True).then_inc(mx_filled, 1)

            def score_step(batch, u):
                n, s = num(batch), batch[1]
                kt, h = u // 2, u % 2
                w = P if kt < KT - 1 else LAST
                if u == 0:
                    pe.wait_ge(ks_in[s], 16 * 3 * GR * (batch[0] + 1))
                    pe.wait_ge(qs_done, n + 1)
                    pe.wait_ge(max_stacked, n + 1)
                wait_past(pe, exp_done, STEPS * n + u - 1)
                for g in range(2):
                    group = 2 * h + g
                    last = nc.tensor.matmul(score[h][0:w, g, :], ks[s][:, group, P * kt:P * kt + w],
                                            qs[s][:, GW * group:GW * group + GW], start=True, stop=True)
                last.then_inc(scored, 1)

            def value_step(batch, u):
                n, s = num(batch), batch[1]
                kt, h = u // 2, u % 2
                if u == 0:
                    wait_past(pe, pv_copied, n)
                    pe.wait_ge(w_read, w_at("V2", n) + 1)
                pe.wait_ge(exp_done, STEPS * n + u + 1)
                for c in range(HG):
                    place = kt * H + 2 * (HG * h + c)
                    last = nc.tensor.matmul(
                        pvp[32 * c:32 * c + 2 * VW, 2 * N * h:2 * N * (h + 1)],
                        vs[s][:, place:place + 2, :].rearrange("p g i -> p (g i)"), pr[h][:, :, c, :],
                        start=(u == 0), stop=(kt == KT - 1), skip_group_check=True)
                last.then_inc(pv_done, 1)

            def phase(batch, has):
                for u in range(STEPS):
                    if "C" in has:
                        score_step(batch, u)
                    name = FILLS.get(u)
                    if name and STAGE_OF[name[0]] in has:
                        fill_work(name, later(batch, AHEAD[STAGE_OF[name[0]]]))
                    for ahead, unit in mx_units(u, has, UNITS):
                        max_unit(later(batch, ahead), unit)
                    if "C" in has and u > 0:
                        value_step(batch, u - 1)
                if "C" in has:
                    value_step(batch, STEPS - 1)

            phases(pe, phase)

            pe.wait_ge(x2_done, 1)
            transpose_tokens(post, "x2T", X2)
            dst = post.start(pe, "logits")
            for b in range(B):
                if b % BPB == 0:
                    post.taken(pe, "x2T", b // BPB)
                last = nc.tensor.matmul(dst[0:N, E * b:E * b + E], X2T[:, N * b:N * b + N], Wr[:, :], start=True, stop=True)
            last.then_inc(post.filled_sem, 1)
            pe.wait_ge(comb_done, 1)
            for k in range(TB):
                dst = post.start(pe, "cT", k)
                for i in range(BPB):
                    last = nc.tensor.transpose(dst[0:E, N * i:N * i + N], ex[:, BPB * k + i, :], ident[0:N, 0:N])
                last.then_inc(post.filled_sem, 1)
            for k in range(TB):
                post.taken(pe, "cT", k)
            for k in range(TB):
                nc.tensor.matmul(PS[:, 4 + k, 0:TW], zero[:, :], x2hi[:, TW * k:TW * k + TW], start=True, stop=True)

            def expert(pair, s):
                e = 2 * pair + s
                pe.wait_ge(w_split, e + 1)
                pe.wait_ge(xelo_done, e + 1)
                pe.wait_ge(wd_in[s], 16 * (pair + 1))

                def up(i):
                    tb, c = i // HC, i % HC
                    cols, hid = slice(TW * tb, TW * tb + TW), slice(P * c, P * c + P)
                    if not isinstance(pair, int) or pair > 0 or UPE * s + i >= 2:
                        pe.wait_ge(h_done, UPE * e + i - 1)
                    for m, (hi, lo) in enumerate(((x2hi, x2lo), (xehi[s], xelo[s]))):
                        dst = PS[:, 2 * (i % 2) + m, 0:TW]
                        nc.tensor.matmul(dst, whi[s][:, m, hid], hi[:, cols], start=True, stop=False)
                        nc.tensor.matmul(dst, whi[s][:, m, hid], lo[:, cols], start=False, stop=False)
                        last = nc.tensor.matmul(dst, wlo[s][:, m, hid], hi[:, cols], start=False, stop=True)
                    last.then_inc(gu_filled, 1)

                def down(i):
                    tb, c = i // HC, i % HC
                    pe.wait_ge(h_done, UPE * e + i + 1)
                    nc.tensor.matmul(PS[:, 4 + tb, 0:TW], wd[s][:, c, :], hh[i % 2][:, :], start=False, stop=True,
                                     skip_group_check=True).then_inc(d_done, 1)

                for i in range(UPE):
                    up(i)
                    if i:
                        down(i - 1)
                down(UPE - 1)

            expert(0, 0)
            expert(0, 1)
            with pe.Fori(1, E // 2) as j:
                for s in range(2):
                    expert(j, s)
            for k in range(TB):
                dst = post.start(pe, "yN", k)
                pe.wait_ge(out_copied, k + 1)
                for i in range(BPB):
                    last = nc.tensor.transpose(dst[0:N, P * i:P * i + P], OT[:, TW * k + N * i:TW * k + N * i + N], ident[:, :])
                last.then_inc(post.filled_sem, 1)


def kernel(**inputs):
    import numpy as _np
    import concourse.bacc as _bacc
    from concourse import mybir as _mybir
    from concourse.bass_utils import run_bass_kernel_spmd as _run

    nc = _bacc.Bacc("TRN2", target_bir_lowering=False, num_devices=1)
    arrays, tensors = {}, {}
    for name, value in inputs.items():
        a = _np.ascontiguousarray(value)
        arrays[f"in_{name}"] = a
        tensors[name] = nc.dram_tensor(f"in_{name}", a.shape, _mybir.dt.from_np(a.dtype), kind="ExternalInput").ap()
    shape = tensors["x"].shape
    out = nc.dram_tensor("out", shape, F32, kind="ExternalOutput").ap()
    comb = nc.dram_tensor("comb", (tensors["L0_ffn_Wr"].shape[1], shape[0] * shape[1]), F32, kind="Internal").ap()
    decoder_layer(nc, tensors, out, comb)
    r = _run(nc, [arrays], core_ids=[0])
    return r.results[0]["out"]
```

```python
from contextlib import ExitStack

import concourse.bass as bass
from concourse import mybir

ALU = mybir.AluOpType
ACT = mybir.ActivationFunctionType
AXL = mybir.AxisListType
F32 = mybir.dt.float32
F16 = mybir.dt.float16

P = 128
BANK = 512
EPS = 1e-5
STEPS = 24
MX_EARLY = 17
MX_FROM = 14
MX_UNTIL = 14
STATS_FROM = 6

FILLS = {1: "Y0", 2: "T0", 3: "T1", 4: "T2", 5: "K0", 7: "K1", 9: "K2", 11: "K3",
         13: "G0", 14: "O0", 15: "M0", 17: "V0", 18: "V1", 20: "V2"}
STAGE_OF = {"T": "A", "K": "A", "V": "B", "M": "B", "Y": "D", "G": "D", "O": "D"}
AHEAD = {"A": 2, "B": 1, "C": 0, "D": -1}


def stages(p, batches):
    return "".join(x for x in "ABCD" if 0 <= p + AHEAD[x] < batches)


def fills_of(has):
    return [FILLS[u] for u in sorted(FILLS) if STAGE_OF[FILLS[u][0]] in has]


def fills_before(p, batches):
    return sum(len(fills_of(stages(q, batches))) for q in range(-2, p))


def mx_units(u, has, units):
    def late(v):
        return MX_EARLY + min(v, MX_UNTIL) * (units - MX_EARLY) // MX_UNTIL

    def first(v):
        return max(0, v - MX_FROM) * MX_EARLY // (STEPS - MX_FROM)

    found = [(1, k) for k in range(late(u), late(u + 1)) if "B" in has]
    return found + [(2, k) for k in range(first(u), first(u + 1)) if "A" in has]


def wait_past(eng, semaphore, value):
    if not isinstance(value, int) or value > 0:
        eng.wait_ge(semaphore, value)


class Ring:

    def __init__(self, psum, filled, read, order):
        self.psum, self.filled_sem, self.read, self.n = psum, filled, read, len(read)
        self.at = {key: i for i, key in enumerate(order)}

    def bank(self, *key):
        return self.psum[:, self.at[key] % self.n, :]

    def start(self, pe, *key):
        i = self.at[key]
        if i >= self.n:
            pe.wait_ge(self.read[i % self.n], i // self.n)
        return self.bank(*key)

    def filled(self, eng, *key):
        eng.wait_ge(self.filled_sem, self.at[key] + 1)
        return self.bank(*key)

    def reader(self, *key):
        return self.read[self.at[key] % self.n]

    def taken(self, eng, *key):
        i = self.at[key]
        eng.wait_ge(self.read[i % self.n], i // self.n + 1)


def decoder_layer(nc, t, out, comb_dram):
    B, N, D = t["x"].shape
    S = t["ctx_1024"].shape[1]
    H, DH = 16, 8
    E = t["L0_ffn_Wr"].shape[1]
    HID = t["L0_ffn_Wg"].shape[2]
    TOK = B * N
    KT = -(-S // P)
    LAST = S - (KT - 1) * P
    GR = 4
    HG = H // GR
    GW = HG * N
    QW = H * N
    RT = -(-QW // P)
    LASTR = QW - (RT - 1) * P
    CH = 3
    CHW = [S // CH + (1 if c < S % CH else 0) for c in range(CH)]
    CHO = [sum(CHW[:c]) for c in range(CH)]
    UNITS = RT * CH
    MROW = 96
    DEPTH = MROW + RT
    KC = 4
    KCW = S // KC
    TB = 4
    TW = TOK // TB
    BPB = B // TB
    HC = HID // P
    UPE = TB * HC
    HS = 4
    LAG = 3
    VW = DH + 1
    SCALE = float(DH) ** -0.5
    DEPTH_SCALE = 12 ** -0.5
    NF = len(fills_of("ABCD"))
    assert D == P and STEPS == 2 * KT and KC * KCW == S and B % 2 == 0 and GW <= BANK

    def later(batch, k):
        return batch[0] + (batch[1] + k) // 2, (batch[1] + k) % 2

    def num(batch):
        return 2 * batch[0] + batch[1]

    def unit_slot(s, unit):
        return (UNITS * s + unit) % 2

    def w_at(name, n):
        stage = STAGE_OF[name[0]]
        p = n - AHEAD[stage]
        if isinstance(n, int):
            return fills_before(p, B) + fills_of(stages(p, B)).index(name)
        return NF * p + (fills_before(1, B) - NF + fills_of("ABCD").index(name))

    def phases(eng, phase, peeled=2):
        for p in (-2, -1, 0, 1):
            phase((p // 2, p % 2), stages(p, B))
        with eng.Fori(1, (B - peeled) // 2) as j:
            for s in range(2):
                phase((j, s), "ABCD")
        for p in range(B - peeled, B + 1):
            phase((p // 2, p % 2), stages(p, B))

    SCALE_AT = (2, 4, 6, 8)
    SPLIT_AT = (9, 10, 11, 12)

    def experts(eng, expert):
        expert(0, 0)
        expert(0, 1)
        with eng.Fori(1, E // 2 - 1) as j:
            for s in range(2):
                expert(j, s)
        expert(E // 2 - 1, 0)
        expert(E // 2 - 1, 1, more=False)

    def widen(ap, n, width):
        return ap.unsqueeze(2).to_broadcast([n, ap.shape[1], width])

    def repeat(ap, n, k):
        return ap.unsqueeze(1).to_broadcast([n, k, ap.shape[1]])

    with ExitStack() as ctx:
        def sb(name, shape, dt=F32, stack=ctx):
            return stack.enter_context(nc.sbuf_tensor(name, shape, dt))

        def sem(name):
            return ctx.enter_context(nc.semaphore(name))

        PS = ctx.enter_context(nc.psum_tensor("PS", [P, 8, BANK], F32))
        score = [PS[:, 2 * h:2 * h + 2, 0:GW] for h in range(2)]
        mxp = [PS[:, 4 + i, :] for i in range(2)]
        pvp = PS[:, 6, 0:GR * N]
        wk = PS[:, 7, :]

        ident = sb("ident", [P, P])
        headmask = sb("headmask", [P, H], F16)
        stackmask = sb("stackmask", [96, HG], F16)
        kvmask = sb("kvmask", [P, P + H])
        rowmask = sb("rowmask", [P, RT], F16)
        minushalf = sb("minushalf", [P, B])
        ones = sb("ones", [P, H])
        before = sb("before", [N, E, E])
        aWq = sb("aWq", [P, P])
        aWo = sb("aWo", [P, P])
        aWkvh = sb("aWkvh", [P, 3 * P])
        abq = sb("abq", [P, 1])
        kvhrow = sb("kvhrow", [N, 3 * P])
        arow = {n: sb("arow_" + n, [N, P]) for n in ("beta", "ln_w", "ln_b", "bo")}
        xW = sb("xW", [P, 5, P])
        xWT = sb("xWT", [P, 5, P])
        WkTg = sb("WkTg", [P, P])
        WvTg = sb("WvTg", [P, P])
        kvg = sb("kvg", [P, 1])
        kvb = sb("kvb", [P, 1])
        kbias = sb("kbias", [P, 1])
        vrow = sb("vrow", [N, P])
        xrow = {n: sb("xrow_" + n, [N, P]) for n in ("qln_g", "qln_b", "bg")}
        Wr = sb("Wr", [P, E])
        X1 = sb("X1", [N, B, P])
        X2 = sb("X2", [N, B, P])
        GATE = sb("GATE", [N, B, P])
        qhi = sb("qhi", [P, TOK], F16)
        qlo = sb("qlo", [P, TOK], F16)
        qrows = sb("qrows", [96, GR, TOK], F16)
        tstat = sb("tstat", [N, B, 6])
        tsm = sb("tsm", [N, 8, B])

        first = ExitStack()
        XT = sb("XT", [P, TOK], stack=first)
        QT = sb("QT", [P, TOK], stack=first)
        KVH = sb("KVH", [N, B, 3 * P], stack=first)
        R = sb("R", [P, 6, P + H], stack=first)
        DEN = sb("DEN", [N, B, H], stack=first)
        first.close()
        wst = [sb(f"wst{i}", [P, 3, HID]) for i in range(2)]
        whi = [sb(f"whi{i}", [P, 3, HID], F16) for i in range(2)]
        wlo = [sb(f"wlo{i}", [P, 3, HID], F16) for i in range(2)]
        cb = [sb(f"cb{i}", [P, TOK]) for i in range(2)]
        X2T = sb("X2T", [P, TOK])
        assert 4 * (TOK * 2 + B * (3 * P + H) + 6 * (P + H)) <= 2 * 3 * HID * 8 + 3 * 4 * TOK
        early = ExitStack()
        ct = [sb(f"ct{i}", [P, KT, P], stack=early) for i in range(2)]
        xn = sb("xn", [P, KT, P], stack=early)
        cstat = [sb(f"cstat{i}", [P, KT, 6], stack=early) for i in range(2)]
        csm = sb("csm", [P, 8, KT], stack=early)
        xnT = [sb(f"xnT{i}", [P, S], stack=early) for i in range(2)]
        khi = [sb(f"khi{i}", [P, S], F16, early) for i in range(2)]
        klo = [sb(f"klo{i}", [P, S], F16, early) for i in range(2)]
        k32 = sb("k32", [P, S], stack=early)
        ks = [sb(f"ks{i}", [DEPTH, GR, S], F16, early) for i in range(2)]
        vs = [sb(f"vs{i}", [P, KT * H, VW], stack=early) for i in range(2)]
        qbd = [sb(f"qbd{i}", [P, H, N], F16, early) for i in range(2)]
        qs = [sb(f"qs{i}", [DEPTH, RT * P], F16, early) for i in range(2)]
        pr = [sb(f"pr{i}", [P, 2, HG, N], stack=early) for i in range(2)]
        mxs = [sb(f"mxs{i}", [P, RT, CH], stack=early) for i in range(2)]
        mx = sb("mx", [P, RT], stack=early)
        mrow = sb("mrow", [DEPTH, P], F16, early)
        pvs = sb("pvs", [P, GR * N], stack=early)
        rden = sb("rden", [N, GR, HG], stack=early)
        y = sb("y", [N, P], stack=early)
        yT = sb("yT", [P, N], stack=early)
        early.close()
        late = ExitStack()
        x2hi = sb("x2hi", [P, TOK], F16, late)
        x2lo = sb("x2lo", [P, TOK], F16, late)
        LG = sb("LG", [N, B, E], stack=late)
        RK = [sb(f"RK{i}", [N, B, E, E], stack=late) for i in range(2)]
        rank = sb("rank", [N, B, E], stack=late)
        ex = sb("ex", [N, B, E], stack=late)
        rsm = sb("rsm", [N, 3, B], stack=late)
        combT = sb("combT", [E, TOK], stack=late)
        xe = sb("xe", [P, TOK], stack=late)
        xehi = [sb(f"xehi{i}", [P, TOK], F16, late) for i in range(2)]
        xelo = [sb(f"xelo{i}", [P, TOK], F16, late) for i in range(2)]
        sg = [sb(f"sg{i}", [P, TW], stack=late) for i in range(2)]
        hh = [sb(f"hh{i}", [P, TW], stack=late) for i in range(HS)]
        hhi = [sb(f"hhi{i}", [P, TW], F16, late) for i in range(HS)]
        hlo = [sb(f"hlo{i}", [P, TW], F16, late) for i in range(HS)]
        zero = sb("zero", [P, P], F16, late)
        OT = sb("OT", [P, TOK], stack=late)
        late.close()

        x_in, weights_in = sem("x_in"), sem("weights_in")
        consts_done, zeros_done = sem("consts_done"), sem("zeros_done")
        tok_stats, tok_scale = sem("tok_stats"), sem("tok_scale")
        folded, k_done, nd_split, attn_done, x1_pre, qn_done = (
            sem(n) for n in ("folded", "k_done", "nd_split", "attn_done", "x1_pre", "qn_done"))
        qhi_done, gate_done, qrows_in = sem("qhi_done"), sem("gate_done"), sem("qrows_in")
        ctx_in = [sem(f"ctx_in{i}") for i in range(2)]
        ks_in = [sem(f"ks_in{i}") for i in range(2)]
        ctx_stats, ctx_normed = sem("ctx_stats"), sem("ctx_normed")
        khi_done, klo_done = sem("khi_done"), sem("klo_done")
        qbd_done, qs_done = sem("qbd_done"), sem("qs_done")
        mx_filled, mx_reduced, max_done, max_stacked = (
            sem(n) for n in ("mx_filled", "mx_reduced", "max_done", "max_stacked"))
        scored, exp_done, pv_done, pv_copied = (sem(n) for n in ("scored", "exp_done", "pv_done", "pv_copied"))
        y_gated = sem("y_gated")
        w_filled, w_read = sem("w_filled"), sem("w_read")
        x2_done, x2hi_done, logits_less_max, exped, comb_done, comb_stored = (
            sem(n) for n in ("x2_done", "x2hi_done", "logits_less_max", "exped", "comb_done", "comb_stored"))
        cb_in = [sem(f"cb_in{i}") for i in range(2)]
        wst_in = [sem(f"wst_in{i}") for i in range(2)]
        xe_done, xehi_done, xelo_done, whi_done, w_split = (sem(n) for n in ("xe_done", "xehi_done", "xelo_done", "whi_done", "w_split"))
        gu_filled, silu_done, h_done, hhi_done, hlo_done, d_done = (
            sem(n) for n in ("gu_filled", "silu_done", "h_done", "hhi_done", "hlo_done", "d_done"))
        out_copied, y_done, stored = sem("out_copied"), sem("y_done"), sem("stored")

        kv_nd = []
        for g in range(-(-B // 3) + 1):
            kv_nd += [("kv", b) for b in range(3 * g, min(3 * g + 3, B))]
            kv_nd += [("nd", g - 1)] if g else []
        pre = Ring(PS, sem("pre_filled"), [sem(f"pre_read{i}") for i in range(4)],
                   [("wT",), ("woT",)] + [("xT", k) for k in range(TB)] + [("bias",)] + [("qT", k) for k in range(TB)]
                   + [("kvh", b) for b in range(B)] + kv_nd
                   + [(n, k) for n in ("gT", "o", "qnT", "Q", "gate") for k in range(TB)])
        post = Ring(PS, sem("post_filled"), [sem(f"post_read{i}") for i in range(4)],
                    [("x2T", k) for k in range(TB)] + [("logits",)] + [("cT", k) for k in range(TB)]
                    + [("yN", k) for k in range(TB)])

        block = ctx.enter_context(nc.Block())

        loads = [(xW[:, i, :], t["L0_xattn_" + n]) for i, n in enumerate(("Wq", "Wk", "Wv", "Wg", "Wo"))]
        loads += [(aWq[:, :], t["L0_attn_Wq"]), (aWo[:, :], t["L0_attn_Wo"])]
        loads += [(aWkvh[:, P * i:P * i + P], t["L0_attn_" + n]) for i, n in enumerate(("Wk", "Wv", "Wh"))]
        loads += [(c[:, :], t[n].rearrange("(p o) -> p o", o=1)) for c, n in
                  ((abq, "L0_attn_bq"), (kvg, "L0_xattn_kvln_g"), (kvb, "L0_xattn_kvln_b"))]
        loads += [(kvhrow[:, P * i:P * i + P], t["L0_attn_" + n].partition_broadcast(N))
                  for i, n in enumerate(("bk", "bv", "bh"))]
        loads += [(arow[n][:, :], t["L0_attn_" + n].partition_broadcast(N)) for n in arow]
        loads += [(xrow[n][:, :], t["L0_xattn_" + n].partition_broadcast(N)) for n in xrow]
        loads += [(Wr[:, :], t["L0_ffn_Wr"])]
        WEIGHTS = 16 * len(loads)

        @block.sync
        def _(sp):
            sp.dma_start(X2[:, :, :], t["x"].rearrange("b n d -> n b d")).then_inc(x_in, 16)
            for dst, src in loads:
                sp.dma_start(dst, src).then_inc(weights_in, 16)

            def load_context(batch):
                n, s = num(batch), batch[1]
                if isinstance(n, int) and n < 4:
                    wait_past(sp, ctx_normed, n - 1)
                else:
                    sp.wait_ge(scored, STEPS * (n - 3))
                src = t["ctx_1024"]
                src = src[n] if isinstance(n, int) else src[bass.ds(n, 1)].rearrange("o s d -> (o s) d")
                sp.dma_start(ct[s][:, 0:KT - 1, :],
                             src[0:(KT - 1) * P, :].rearrange("(p t) d -> p t d", p=P)).then_inc(ctx_in[s], 16)
                sp.dma_start(ct[s][0:LAST, KT - 1, :], src[(KT - 1) * P:S, :]).then_inc(ctx_in[s], 16)

            sp.wait_ge(zeros_done, 1)
            load_context((0, 0))
            load_context((0, 1))
            for k in range(TB):
                pre.taken(sp, "Q", k)
            for k, part in enumerate((qhi, qlo, qhi)):
                for g in range(GR):
                    sp.dma_start(qrows[32 * k:32 * k + 32, g, :], part[32 * g:32 * g + 32, :]).then_inc(qrows_in, 16)

            def load_expert(pair, s):
                e = 2 * pair + s
                if not isinstance(pair, int) or pair > 0:
                    sp.wait_ge(d_done, UPE * (e - 1))
                for i, w in enumerate(("Wg", "Wu")):
                    src = t["L0_ffn_" + w]
                    src = src[e] if isinstance(e, int) else src[bass.ds(e, 1)].rearrange("o c h -> (o c) h")
                    sp.dma_start(wst[s][:, i, :], src).then_inc(wst_in[s], 16)
                src = t["L0_ffn_Wd"]
                src = src[e] if isinstance(e, int) else src[bass.ds(e, 1)].rearrange("o h c -> (o h) c")
                sp.dma_start(wst[s][:, 2, :].rearrange("p (k c) -> p k c", c=P),
                             src.rearrange("(k p) c -> p k c", p=P)).then_inc(wst_in[s], 16)

            def phase(batch, has):
                if isinstance(batch[0], int) and num(batch) == B - 3:
                    for s in range(2):
                        load_expert(0, s)
                ahead = later(batch, 3)
                if not isinstance(batch[0], int) or 2 <= num(ahead) < B:
                    load_context(ahead)
                if "B" in has:
                    n, s = num(later(batch, 1)), later(batch, 1)[1]
                    if isinstance(n, int):
                        wait_past(sp, scored, STEPS * (n - 1))
                    sp.wait_ge(klo_done, KC * (n + 1))
                    for k, part in enumerate((khi, khi, klo)):
                        for g in range(GR):
                            sp.dma_start(ks[s][32 * k:32 * k + 32, g, :], part[s][32 * g:32 * g + 32, :])\
                              .then_inc(ks_in[s], 16)

            phases(sp, phase, peeled=4)

            def load_comb(pair, s):
                e = 2 * pair + s
                if not isinstance(pair, int) or pair > 0:
                    sp.wait_ge(xe_done, TB * (e - 1))
                src = comb_dram[e:e + 1, :] if isinstance(e, int) else comb_dram[bass.ds(e, 1), :]
                sp.dma_start(cb[s][:, :], src.to_broadcast([P, TOK])).then_inc(cb_in[s], 16)

            for k in range(TB):
                post.taken(sp, "cT", k)
            sp.dma_start(comb_dram, combT[:, :]).then_inc(comb_stored, 16)
            sp.wait_ge(comb_stored, 16)
            for s in range(2):
                load_comb(0, s)
            with sp.Fori(1, E // 2) as j:
                for s in range(2):
                    load_comb(j, s)
                    load_expert(j, s)
            sp.wait_ge(y_done, 1)
            sp.dma_start(out.rearrange("b n d -> n b d"), X2[:, :, :]).then_inc(stored, 16)
            sp.wait_ge(stored, 16)

        def moments(pool, stat, small, n, k):
            r = [small[0:n, i, 0:k] for i in range(8)]
            st = [stat[0:n, 0:k, i] for i in range(6)]
            nc.gpsimd.tensor_tensor(r[2], st[1], st[4], ALU.add)
            nc.gpsimd.tensor_tensor(r[3], st[1], st[4], ALU.subtract)
            nc.gpsimd.tensor_tensor(r[4], st[2], st[5], ALU.add)
            pool.drain()
            nc.gpsimd.tensor_scalar(r[0], r[2], 0.5, None, ALU.mult)
            nc.gpsimd.tensor_scalar(r[5], r[3], 0.5, None, ALU.mult)
            nc.gpsimd.tensor_scalar(r[6], r[4], 1.0 / D, EPS, ALU.mult, ALU.add)
            pool.drain()
            nc.gpsimd.tensor_tensor(r[7], r[5], r[5], ALU.mult)
            pool.drain()
            nc.gpsimd.tensor_tensor(r[2], r[7], r[6], ALU.add)
            pool.drain()
            return nc.gpsimd.tensor_tensor(r[1], r[2], minushalf[0:n, 0:k], ALU.pow)

        @block.gpsimd
        def _(pool):
            nc.gpsimd.memset(ident[:, :], 0.0)
            nc.gpsimd.memset(headmask[:, :], 1.0)
            nc.gpsimd.memset(kvmask[:, :], 0.0)
            nc.gpsimd.memset(rowmask[:, :], 0.0)
            nc.gpsimd.memset(minushalf[:, :], -0.5)
            nc.gpsimd.memset(before[:, :, :], 1.0)
            pool.drain()
            nc.gpsimd.affine_select(out=ident[:, :], in_=ident[:, :], compare_op=ALU.not_equal, fill=1.0,
                                    base=0, pattern=[[-1, P]], channel_multiplier=1)
            nc.gpsimd.affine_select(out=rowmask[:, :], in_=rowmask[:, :], compare_op=ALU.not_equal, fill=1.0,
                                    base=-MROW, pattern=[[-1, RT]], channel_multiplier=1)
            nc.gpsimd.affine_select(out=headmask[:, :], in_=headmask[:, :], compare_op=ALU.is_ge, fill=0.0,
                                    base=0, pattern=[[-DH, H]], channel_multiplier=1)
            nc.gpsimd.affine_select(out=before[:, :, :], in_=before[:, :, :], compare_op=ALU.is_gt, fill=0.0,
                                    base=0, pattern=[[1, E], [-1, E]], channel_multiplier=0)
            pool.drain()
            nc.gpsimd.affine_select(out=headmask[:, :], in_=headmask[:, :], compare_op=ALU.is_ge, fill=0.0,
                                    base=DH - 1, pattern=[[DH, H]], channel_multiplier=-1)
            for k in range(1 - P // H, P // H):
                nc.gpsimd.affine_select(out=kvmask[:, 0:P], in_=kvmask[:, 0:P], compare_op=ALU.not_equal, fill=1.0,
                                        base=-H * k, pattern=[[-1, P]], channel_multiplier=1)
                pool.drain()
            nc.gpsimd.tensor_copy(kvmask[:, P:P + H], kvmask[:, 0:H])
            for k in range(3):
                pool.drain()
                nc.gpsimd.tensor_copy(stackmask[32 * k:32 * k + 32, :], headmask[0:32, 0:HG])
            pool.drain()
            nc.gpsimd.memset(ones[:, :], 1.0).then_inc(consts_done, 1)

            def token_moments(count):
                pool.wait_ge(tok_stats, count)
                moments(pool, tstat, tsm, N, B).then_inc(tok_scale, 1)

            def norm_context(batch):
                n, s = num(batch), batch[1]
                pool.wait_ge(ctx_stats, n + 1)
                moments(pool, cstat[s], csm, P, KT)
                pool.drain()
                nc.gpsimd.tensor_tensor(ct[s][:, :, :], ct[s][:, :, :], widen(csm[:, 0, :], P, P), ALU.subtract)
                pool.drain()
                if not isinstance(n, int) or n > 0:
                    pool.wait_ge(w_filled, w_at("T2", n - 1) + 1)
                nc.gpsimd.tensor_tensor(xn[:, :, :], ct[s][:, :, :], widen(csm[:, 1, :], P, P), ALU.mult)\
                  .then_inc(ctx_normed, 1)

            def place_queries(batch):
                n, s = num(batch), batch[1]
                wait_past(pool, mx_filled, UNITS * (n - 1))
                src = qhi[:, n * N:n * N + N] if isinstance(n, int) else qhi[:, bass.ds(n * N, N)]
                nc.gpsimd.tensor_tensor(qbd[s][:, :, :], repeat(src, P, H), widen(headmask[:, :], P, N), ALU.mult)\
                  .then_inc(qbd_done, 1)

            def low_keys(batch):
                n, s = num(batch), batch[1]
                for k in range(KC):
                    pool.wait_ge(w_read, w_at(f"K{k}", n) + 1)
                    cols = slice(KCW * k, KCW * k + KCW)
                    nc.gpsimd.tensor_tensor(klo[s][:, cols], k32[:, cols], khi[s][:, cols], ALU.subtract)\
                      .then_inc(klo_done, 1)

            for count in (1, 2):
                token_moments(count)
            for k in range(TB):
                pre.taken(pool, "Q", k)

            def phase(batch, has):
                n, s = num(later(batch, 1)), later(batch, 1)[1]
                if "D" in has:
                    m = num(later(batch, -1))
                    pool.wait_ge(w_read, w_at("Y0", m) + 1)
                    nc.gpsimd.tensor_tensor(y[:, :], y[:, :], vrow[:, :], ALU.add)
                    pool.drain()
                    if isinstance(m, int) and m == 0:
                        pool.wait_ge(gate_done, 1)
                    gate = GATE[:, m, :] if isinstance(m, int) else GATE[:, bass.ds(m, 1), :].rearrange("p o d -> p (o d)")
                    nc.gpsimd.tensor_tensor(y[:, :], y[:, :], gate, ALU.mult).then_inc(y_gated, 1)
                if "B" in has:
                    if isinstance(n, int) and n == 0:
                        pool.wait_ge(qrows_in, 16 * 3 * GR)
                    wait_past(pool, scored, STEPS * (n - 1))
                    for g in range(GR):
                        src = qrows[:, g, n * N:n * N + N] if isinstance(n, int) else qrows[:, g, bass.ds(n * N, N)]
                        last = nc.gpsimd.tensor_tensor(
                            qs[s][0:96, g * GW:g * GW + GW].rearrange("p (h q) -> p h q", h=HG),
                            repeat(src, 96, HG), widen(stackmask[:, :], 96, N), ALU.mult)
                    last.then_inc(qs_done, 1)
                if "A" in has:
                    place_queries(later(batch, 2))
                    low_keys(later(batch, 2))
                if not isinstance(batch[0], int) or num(batch) + 3 < B:
                    norm_context(later(batch, 3))
                if "B" in has:
                    pool.drain()
                    pool.wait_ge(w_read, w_at("M0", n) + 1)
                    nc.gpsimd.tensor_tensor(qs[s][MROW:DEPTH, :].rearrange("p (c q) -> p c q", q=P),
                                            repeat(mrow[MROW:DEPTH, :], RT, RT), widen(rowmask[MROW:DEPTH, :], RT, P),
                                            ALU.mult).then_inc(max_stacked, 1)
                    pool.drain()
                if isinstance(batch[0], int) and num(batch) == B - 1:
                    for k in range(HC):
                        split_weights(0, 0, k)

            norm_context((0, 0))
            def split_weights(pair, s, k):
                pool.wait_ge(whi_done, HC * (2 * pair + s) + k + 1)
                part = slice(P * k, P * k + P)
                nc.gpsimd.tensor_tensor(wlo[s][:, :, part], wst[s][:, :, part], whi[s][:, :, part], ALU.subtract)\
                  .then_inc(w_split, 1)

            phases(pool, phase, peeled=4)
            token_moments(3)

            def expert(pair, s, more=True):
                e = 2 * pair + s
                for i in range(UPE):
                    pool.wait_ge(hhi_done, UPE * e + i + 1)
                    nc.gpsimd.tensor_tensor(hlo[i % HS][:, :], hh[i % HS][:, :], hhi[i % HS][:, :], ALU.subtract)\
                      .then_inc(hlo_done, 1)
                    if more and i in SPLIT_AT:
                        split_weights(*later((pair, s), 1), SPLIT_AT.index(i))

            experts(pool, expert)
            token_moments(4)

        @block.scalar
        def _(act):
            act.wait_ge(weights_in, WEIGHTS)
            for k in range(TB):
                src = pre.filled(act, "xT", k)
                nc.scalar.activation(XT[:, TW * k:TW * k + TW], src[:, 0:TW], ACT.Copy).then_inc(pre.reader("xT", k), 1)
            for k in range(TB):
                src = pre.filled(act, "qT", k)
                nc.scalar.activation(QT[:, TW * k:TW * k + TW], src[:, 0:TW], ACT.Sigmoid, bias=abq[:, 0:1])\
                  .then_inc(pre.reader("qT", k), 1)
            for k in range(TB):
                for b in range(BPB * k, BPB * k + BPB):
                    pre.taken(act, "kvh", b)
                keys = KVH[:, BPB * k:BPB * k + BPB, 0:P]
                nc.scalar.activation(keys, keys, ACT.Sigmoid).then_inc(k_done, 1)
            for g in range(-(-B // 3)):
                src = pre.filled(act, "nd", g)
                k = min(3, B - 3 * g)
                src = src[0:N, 0:k * (P + H)].rearrange("p (b c) -> p b c", b=k)
                nc.scalar.activation(GATE[:, 3 * g:3 * g + k, :], src[:, :, 0:P], ACT.Copy)
                nc.scalar.activation(DEN[:, 3 * g:3 * g + k, :], src[:, :, P:P + H], ACT.Copy)\
                  .then_inc(pre.reader("nd", g), 1)
                act.wait_ge(pre.reader("nd", g), pre.at["nd", g] // 4 + 1)
            act.sem_inc(nd_split, 1)
            for name in ("gT", "qnT"):
                for k in range(TB):
                    src = pre.filled(act, name, k)
                    nc.scalar.activation(XT[:, TW * k:TW * k + TW], src[:, 0:TW], ACT.Copy)\
                      .then_inc(pre.reader(name, k), 1)
            for k in range(TB):
                src = pre.filled(act, "Q", k)
                nc.scalar.activation(qhi[:, TW * k:TW * k + TW], src[:, 0:TW], ACT.Copy).then_inc(qhi_done, 1)
            for k in range(TB):
                pre.taken(act, "gate", k)
            nc.scalar.activation(GATE[:, :, :], GATE[:, :, :], ACT.Sigmoid).then_inc(gate_done, 1)
            pre.taken(act, "bias")

            def read_work(name, batch):
                n, s = num(batch), batch[1]
                kind, k = name[0], int(name[1])
                act.wait_ge(w_filled, w_at(name, n) + 1)
                if kind == "T":
                    w = min(4 * P, S - 4 * P * k)
                    nc.scalar.activation(xnT[s][:, 4 * P * k:4 * P * k + w], wk[:, 0:w], ACT.Copy).then_inc(w_read, 1)
                if kind == "K":
                    if k == 0:
                        wait_past(act, mx_filled, UNITS * (n - 1))
                        if not isinstance(batch[0], int) or batch[0] > 0:
                            act.wait_ge(ks_in[s], 16 * 3 * GR * batch[0])
                    nc.scalar.activation(khi[s][:, KCW * k:KCW * k + KCW], wk[:, 0:KCW], ACT.Identity,
                                         bias=kbias[:, 0:1]).then_inc(khi_done, 1)
                    if k == 0:
                        wait_past(act, klo_done, KC * n)
                    nc.scalar.activation(k32[:, KCW * k:KCW * k + KCW], wk[:, 0:KCW], ACT.Identity,
                                         bias=kbias[:, 0:1]).then_inc(w_read, 1)
                if kind == "V":
                    if k == 0:
                        wait_past(act, pv_done, STEPS * (n - 1))
                    full = min(4, KT - 1 - 4 * k)
                    dst = vs[s][:, 4 * k * H:(4 * k + full) * H, 0:DH]
                    ins = nc.scalar.activation(dst, wk[:, 0:full * P].rearrange("p (h d) -> p h d", d=DH), ACT.Copy)
                    if full < 4:
                        ins = nc.scalar.activation(vs[s][0:LAST, (KT - 1) * H:KT * H, 0:DH],
                                                   wk[0:LAST, full * P:full * P + P].rearrange("p (h d) -> p h d", d=DH),
                                                   ACT.Copy)
                    ins.then_inc(w_read, 1)
                if kind == "G":
                    nc.scalar.activation(yT[:, :], wk[:, 0:N], ACT.Copy).then_inc(w_read, 1)

            def phase(batch, has):
                for u in range(STEPS):
                    if "C" in has:
                        n, h, w = num(batch), u % 2, P if u // 2 < KT - 1 else LAST
                        act.wait_ge(scored, STEPS * n + u + 1)
                        wait_past(act, pv_done, STEPS * n + u - 1)
                        nc.scalar.activation(pr[h][0:w, :, :, :].rearrange("p g h q -> p g (h q)"), score[h][0:w],
                                             ACT.Exp, scale=SCALE).then_inc(exp_done, 1)
                    name = FILLS.get(u)
                    if name and name[0] in "TKVG" and STAGE_OF[name[0]] in has:
                        read_work(name, later(batch, AHEAD[STAGE_OF[name[0]]]))
                if isinstance(batch[0], int) and num(batch) == B - 2:
                    for k in range(HC):
                        split_weights(0, 0, k)

            def split_weights(pair, s, k):
                if k == 0:
                    act.wait_ge(wst_in[s], 16 * 3 * (pair + 1))
                    if not isinstance(pair, int) or 2 * pair + s > 1:
                        act.wait_ge(d_done, UPE * (2 * pair + s - 1))
                part = slice(P * k, P * k + P)
                nc.scalar.activation(whi[s][:, :, part], wst[s][:, :, part], ACT.Copy).then_inc(whi_done, 1)

            act.wait_ge(zeros_done, 1)
            phases(act, phase)

            for k in range(TB):
                src = post.filled(act, "x2T", k)
                nc.scalar.activation(X2T[:, TW * k:TW * k + TW], src[:, 0:TW], ACT.Copy)
                nc.scalar.activation(x2hi[:, TW * k:TW * k + TW], src[:, 0:TW], ACT.Copy).then_inc(x2hi_done, 1)
            act.wait_ge(logits_less_max, 1)
            nc.scalar.activation(ex[:, :, :], ex[:, :, :], ACT.Exp).then_inc(exped, 1)
            for k in range(TB):
                src = post.filled(act, "cT", k)
                nc.scalar.activation(combT[:, TW * k:TW * k + TW], src[0:E, 0:TW], ACT.Copy)\
                  .then_inc(post.reader("cT", k), 1)

            def scale_tokens(pair, s, k):
                act.wait_ge(xe_done, TB * (2 * pair + s) + k + 1)
                cols = slice(TW * k, TW * k + TW)
                nc.scalar.activation(xehi[s][:, cols], xe[:, cols], ACT.Copy).then_inc(xehi_done, 1)

            def high_hidden(pair, s, i):
                e = 2 * pair + s
                act.wait_ge(h_done, UPE * e + i + 1)
                if not isinstance(pair, int) or UPE * e + i >= HS:
                    act.wait_ge(d_done, UPE * e + i - HS + 1)
                nc.scalar.activation(hhi[i % HS][:, :], hh[i % HS][:, :], ACT.Copy).then_inc(hhi_done, 1)

            def expert(pair, s, more=True):
                e = 2 * pair + s
                for i in range(UPE):
                    act.wait_ge(gu_filled, UPE * e + i + 1)
                    if not isinstance(pair, int) or UPE * e + i >= 2:
                        act.wait_ge(h_done, UPE * e + i - 1)
                    nc.scalar.activation(sg[i % 2][:, :], PS[:, 2 * (i % 2), 0:TW], ACT.Silu).then_inc(silu_done, 1)
                    if not isinstance(pair, int) or UPE * e + i > 0:
                        high_hidden(pair, s, i - 1)
                    if more and i in SPLIT_AT:
                        split_weights(*later((pair, s), 1), SPLIT_AT.index(i))
                    if more and i in SCALE_AT:
                        scale_tokens(*later((pair, s), 1), SCALE_AT.index(i))

            for k in range(TB):
                scale_tokens(0, 0, k)
            experts(act, expert)
            high_hidden(E // 2 - 1, 1, UPE - 1)
            act.wait_ge(d_done, UPE * E)
            for k in range(TB):
                nc.scalar.activation(OT[:, TW * k:TW * k + TW], PS[:, 4 + k, 0:TW], ACT.Copy).then_inc(out_copied, 1)

        @block.vector
        def _(dve):
            for s in range(2):
                nc.vector.memset(ct[s][:, KT - 1, :], 0.0)
                nc.vector.memset(cstat[s][:, KT - 1, :], 0.0)
                nc.vector.memset(mxs[s][:, :, :], 0.0)
                nc.vector.memset(ks[s][MROW:DEPTH, :, :], 1.0)
                nc.vector.memset(vs[s][:, :, :], 0.0)
                dve.drain()
                nc.vector.memset(vs[s][:, 0:(KT - 1) * H, DH:VW], 1.0)
                nc.vector.memset(vs[s][0:LAST, (KT - 1) * H:KT * H, DH:VW], 1.0)
            nc.vector.memset(pvp, 0.0).then_inc(zeros_done, 1)

            def token_norm(src, dst, count):
                for b in range(B):
                    last = nc.vector.bn_stats(tstat[:, b, :], src[:, b, :])
                last.then_inc(tok_stats, 1)
                dve.wait_ge(tok_scale, count)
                nc.vector.tensor_tensor(dst[:, :, :], src[:, :, :], widen(tsm[:, 0, :], N, P), ALU.subtract)
                dve.drain()
                return nc.vector.tensor_tensor(dst[:, :, :], dst[:, :, :], widen(tsm[:, 1, :], N, P), ALU.mult)

            dve.wait_ge(weights_in, WEIGHTS)
            src = pre.filled(dve, "wT")
            nc.vector.tensor_copy(xWT[:, 0:4, :], src.rearrange("p (i c) -> p i c", i=4)).then_inc(pre.reader("wT"), 1)
            src = pre.filled(dve, "woT")
            nc.vector.tensor_copy(xWT[:, 4, :], src[:, 0:P]).then_inc(pre.reader("woT"), 1)
            dve.drain()
            nc.vector.tensor_scalar(WkTg[:, :], xWT[:, 1, :], kvg[:, 0:1], None, ALU.mult)
            for h in range(2):
                half = slice(h * P // 2, (h + 1) * P // 2)
                last = nc.vector.tensor_scalar(WvTg[:, half].rearrange("p (c g d) -> p c g d", c=HG, g=2),
                                               xWT[:, 2, half].rearrange("p (g c d) -> p c g d", c=HG, g=2),
                                               kvg[:, 0:1], None, ALU.mult)
            last.then_inc(folded, 1)
            src = pre.filled(dve, "bias")
            nc.vector.tensor_copy(kbias[:, :], src[:, 0:1])
            nc.vector.tensor_copy(vrow[:, :], src[0:N, P:2 * P]).then_inc(pre.reader("bias"), 1)
            for b in range(B):
                src = pre.filled(dve, "kvh", b)
                nc.vector.tensor_tensor(KVH[:, b, :], src[0:N, 0:3 * P], kvhrow[:, :], ALU.add)\
                  .then_inc(pre.reader("kvh", b), 1)
            dve.wait_ge(consts_done, 1)
            for b in range(B):
                src = pre.filled(dve, "kv", b)
                if b >= 6:
                    pre.filled(dve, "nd", (b - 6) // 3)
                nc.vector.tensor_tensor(R[:, b % 6, :], src[:, 0:P + H], kvmask[:, :], ALU.mult)\
                  .then_inc(pre.reader("kv", b), 1)
            dve.wait_ge(nd_split, 1)
            nc.vector.reciprocal(DEN[:, :, :], DEN[:, :, :])
            dve.drain()
            for b in range(B):
                att = GATE[:, b, :].rearrange("p (m h) -> p m h", h=H)
                nc.vector.tensor_tensor(att, att, repeat(DEN[:, b, :], N, P // H), ALU.mult)
            dve.drain()
            token_norm(GATE, GATE, 1)
            dve.drain()
            nc.vector.tensor_tensor(GATE[:, :, :], GATE[:, :, :], repeat(arow["ln_w"][:, :], N, B), ALU.mult)
            nc.vector.tensor_tensor(KVH[:, :, 2 * P:3 * P], KVH[:, :, 2 * P:3 * P],
                                    repeat(arow["beta"][:, :], N, B), ALU.add)
            dve.drain()
            nc.vector.tensor_tensor(GATE[:, :, :], GATE[:, :, :], repeat(arow["ln_b"][:, :], N, B), ALU.add)
            dve.drain()
            nc.vector.tensor_tensor(GATE[:, :, :], GATE[:, :, :], KVH[:, :, 2 * P:3 * P], ALU.mult).then_inc(attn_done, 1)
            for k in range(TB):
                src = pre.filled(dve, "o", k)
                blk = slice(BPB * k, BPB * k + BPB)
                nc.vector.tensor_tensor(GATE[:, blk, :], src[0:N, :].rearrange("p (b c) -> p b c", b=BPB),
                                        repeat(arow["bo"][:, :], N, BPB), ALU.add).then_inc(pre.reader("o", k), 1)
                dve.drain()
                if k == 0:
                    dve.wait_ge(x_in, 16)
                nc.vector.scalar_tensor_tensor(X1[:, blk, :], GATE[:, blk, :], 0.0, X2[:, blk, :], ALU.max, ALU.add)
            dve.drain()
            token_norm(X1, X1, 2)
            dve.drain()
            nc.vector.tensor_tensor(GATE[:, :, :], X1[:, :, :], repeat(xrow["qln_g"][:, :], N, B), ALU.mult)
            dve.drain()
            nc.vector.tensor_tensor(GATE[:, :, :], GATE[:, :, :], repeat(xrow["qln_b"][:, :], N, B), ALU.add)\
              .then_inc(qn_done, 1)
            for k in range(TB):
                src = pre.filled(dve, "Q", k)
                dve.wait_ge(qhi_done, k + 1)
                cols = slice(TW * k, TW * k + TW)
                nc.vector.tensor_tensor(qlo[:, cols], src[:, 0:TW], qhi[:, cols], ALU.subtract)\
                  .then_inc(pre.reader("Q", k), 1)
            for k in range(TB):
                src = pre.filled(dve, "gate", k)
                nc.vector.tensor_tensor(GATE[:, BPB * k:BPB * k + BPB, :], src[0:N, :].rearrange("p (b c) -> p b c", b=BPB),
                                        repeat(xrow["bg"][:, :], N, BPB), ALU.add).then_inc(pre.reader("gate", k), 1)

            def context_stats(batch, tiles):
                n, s = num(batch), batch[1]
                for k in tiles:
                    if k == 0:
                        dve.wait_ge(ctx_in[s], 32 * (batch[0] + 1))
                    w = P if k < KT - 1 else LAST
                    ins = nc.vector.bn_stats(cstat[s][0:w, k, :], ct[s][0:w, k, :])
                    if k == KT - 1:
                        ins.then_inc(ctx_stats, 1)

            def read_work(name, batch):
                n, s = num(batch), batch[1]
                kind, k = name[0], int(name[1])
                dve.wait_ge(w_filled, w_at(name, n) + 1)
                if kind == "M":
                    nc.vector.tensor_scalar(mrow[MROW:DEPTH, :], wk[MROW:DEPTH, 0:P], -1.0, None, ALU.mult).then_inc(w_read, 1)
                if kind == "Y":
                    blocks = wk[0:N, :].rearrange("p (h g c i) -> p g h c i", h=2, g=2, c=HG)
                    for g in range(2):
                        nc.vector.reciprocal(rden[:, g::2, :], blocks[:, g, :, :, VW * g + DH])
                    dve.drain()
                    yv = y[:, :].rearrange("p (h g c d) -> p g h c d", h=2, g=2, c=HG)
                    for h in range(2):
                        for g in range(2):
                            ins = nc.vector.tensor_tensor(
                                yv[:, g, h], blocks[:, g, h, :, VW * g:VW * g + DH],
                                widen(rden[:, 2 * h + g, :], N, DH), ALU.mult)
                    ins.then_inc(w_read, 1)
                if kind == "O":
                    at = (slice(n, n + 1) if isinstance(n, int) else bass.ds(n, 1))
                    tokens = X2[:, at, :].rearrange("p o d -> p (o d)")
                    nc.vector.tensor_tensor(tokens, wk[0:N, 0:P], X1[:, at, :].rearrange("p o d -> p (o d)"), ALU.add)\
                      .then_inc(w_read, 1)
                    dve.drain()
                    ins = nc.vector.bn_stats(tstat[:, at, :].rearrange("p o d -> p (o d)"), tokens)
                    if isinstance(n, int) and n == B - 1:
                        ins.then_inc(tok_stats, 1)

            def phase(batch, has):
                for u in range(STEPS):
                    if u == 0 and "D" in has:
                        n = num(later(batch, -1))
                        dve.wait_ge(pv_done, STEPS * (n + 1))
                        if not isinstance(n, int) or n > 0:
                            dve.wait_ge(w_filled, w_at("Y0", n - 1) + 1)
                        nc.vector.tensor_copy(pvs[:, :], pvp).then_inc(pv_copied, 1)
                    name = FILLS.get(u)
                    if name and name[0] in "YO" and STAGE_OF[name[0]] in has:
                        read_work(name, later(batch, AHEAD[STAGE_OF[name[0]]]))
                    for ahead, unit in mx_units(u, has, UNITS):
                        n, s = num(later(batch, ahead)), later(batch, ahead)[1]
                        rt, c = unit // CH, unit % CH
                        w = P if rt < RT - 1 else LASTR
                        dve.wait_ge(mx_filled, UNITS * n + unit + 1)
                        nc.vector.reduce_max(mxs[s][0:w, rt, c:c + 1], mxp[unit_slot(s, unit)][0:w, 0:CHW[c]], AXL.X)\
                          .then_inc(mx_reduced, 1)
                        if unit == UNITS - 1:
                            dve.drain()
                            nc.vector.reduce_max(mx[:, :], mxs[s][:, :, :], AXL.X).then_inc(max_done, 1)
                    k = u - STATS_FROM
                    if 0 <= k < KT // 2 and (not isinstance(batch[0], int) or num(batch) + 3 < B):
                        context_stats(later(batch, 3), (2 * k, 2 * k + 1))
                    if name and name[0] == "M" and STAGE_OF[name[0]] in has:
                        read_work(name, later(batch, AHEAD[STAGE_OF[name[0]]]))

            context_stats((0, 0), range(KT))
            phases(dve, phase, peeled=4)

            dve.wait_ge(tok_scale, 3)
            for k in range(TB):
                blk = slice(BPB * k, BPB * k + BPB)
                nc.vector.tensor_tensor(X2[:, blk, :], X2[:, blk, :], widen(tsm[:, 0, blk], N, P), ALU.subtract)
                dve.drain()
                nc.vector.tensor_tensor(X2[:, blk, :], X2[:, blk, :], widen(tsm[:, 1, blk], N, P), ALU.mult)\
                  .then_inc(x2_done, 1)
            for k in range(TB):
                src = post.filled(dve, "x2T", k)
                dve.wait_ge(x2hi_done, k + 1)
                cols = slice(TW * k, TW * k + TW)
                nc.vector.tensor_tensor(x2lo[:, cols], src[:, 0:TW], x2hi[:, cols], ALU.subtract)\
                  .then_inc(post.reader("x2T", k), 1)
            nc.vector.memset(zero[:, :], 0.0)
            src = post.filled(dve, "logits")
            nc.vector.tensor_copy(LG[:, :, :], src[0:N, 0:B * E].rearrange("p (b e) -> p b e", b=B))\
              .then_inc(post.reader("logits"), 1)
            dve.drain()
            shape = [N, B, E, E]
            other, own = LG[:, :, :].unsqueeze(2).to_broadcast(shape), LG[:, :, :].unsqueeze(3).to_broadcast(shape)
            nc.vector.reduce_max(rsm[:, 0, :], LG[:, :, :], AXL.X)
            nc.vector.tensor_tensor(RK[0][:, :, :, :], other, own, ALU.is_gt)
            nc.vector.tensor_tensor(RK[1][:, :, :, :], other, own, ALU.is_equal)
            dve.drain()
            nc.vector.tensor_tensor(ex[:, :, :], LG[:, :, :], widen(rsm[:, 0, :], N, E), ALU.subtract)\
              .then_inc(logits_less_max, 1)
            nc.vector.tensor_tensor(RK[1][:, :, :, :], RK[1][:, :, :, :],
                                    before[:, :, :].unsqueeze(1).to_broadcast(shape), ALU.mult)
            dve.drain()
            nc.vector.tensor_tensor(RK[0][:, :, :, :], RK[0][:, :, :, :], RK[1][:, :, :, :], ALU.add)
            dve.drain()
            nc.vector.reduce_sum(rank[:, :, :], RK[0][:, :, :, :], AXL.X)
            dve.drain()
            dve.wait_ge(exped, 1)
            nc.vector.scalar_tensor_tensor(ex[:, :, :], rank[:, :, :], 1.5, ex[:, :, :], ALU.is_lt, ALU.mult)
            dve.drain()
            nc.vector.reduce_sum(rsm[:, 1, :], ex[:, :, :], AXL.X)
            dve.drain()
            nc.vector.reciprocal(rsm[:, 2, :], rsm[:, 1, :])
            dve.drain()
            nc.vector.tensor_scalar(rsm[:, 1, :], rsm[:, 2, :], DEPTH_SCALE, None, ALU.mult)
            dve.drain()
            nc.vector.tensor_tensor(ex[:, :, :], ex[:, :, :], widen(rsm[:, 1, :], N, E), ALU.mult).then_inc(comb_done, 1)

            def scale_tokens(pair, s, k):
                if k == 0:
                    dve.wait_ge(cb_in[s], 16 * (pair + 1))
                cols = slice(TW * k, TW * k + TW)
                nc.vector.tensor_tensor(xe[:, cols], X2T[:, cols], cb[s][:, cols], ALU.mult).then_inc(xe_done, 1)

            def low_tokens(pair, s, k):
                dve.wait_ge(xehi_done, TB * (2 * pair + s) + k + 1)
                cols = slice(TW * k, TW * k + TW)
                nc.vector.tensor_tensor(xelo[s][:, cols], xe[:, cols], xehi[s][:, cols], ALU.subtract)\
                  .then_inc(xelo_done, 1)

            def expert(pair, s, more=True):
                e = 2 * pair + s
                for i in range(UPE):
                    dve.wait_ge(silu_done, UPE * e + i + 1)
                    if not isinstance(pair, int) or UPE * e + i >= HS:
                        dve.wait_ge(hlo_done, UPE * e + i - HS + 1)
                    nc.vector.tensor_tensor(hh[i % HS][:, :], sg[i % 2][:, :], PS[:, 2 * (i % 2) + 1, 0:TW], ALU.mult)\
                      .then_inc(h_done, 1)
                    if more and i in SCALE_AT:
                        scale_tokens(*later((pair, s), 1), SCALE_AT.index(i))
                    if more and i - 1 in SCALE_AT:
                        low_tokens(*later((pair, s), 1), SCALE_AT.index(i - 1))

            for k in range(TB):
                scale_tokens(0, 0, k)
            for k in range(TB):
                low_tokens(0, 0, k)
            experts(dve, expert)
            for k in range(TB):
                src = post.filled(dve, "yN", k)
                blk = slice(BPB * k, BPB * k + BPB)
                nc.vector.tensor_tensor(X2[:, blk, :], X2[:, blk, :], src[0:N, :].rearrange("p (b c) -> p b c", b=BPB),
                                        ALU.add).then_inc(post.reader("yN", k), 1)
            dve.drain()
            token_norm(X2, X2, 4).then_inc(y_done, 1)

        @block.tensor
        def _(pe):
            def transpose_tokens(ring, name, src, done=None):
                for k in range(TB):
                    if done is not None:
                        pe.wait_ge(done, k + 1)
                    dst = ring.start(pe, name, k)
                    for i in range(BPB):
                        last = nc.tensor.transpose(dst[:, N * i:N * i + N], src[:, BPB * k + i, :], ident[0:N, 0:N])
                    last.then_inc(ring.filled_sem, 1)

            def project(ring, name, rhs):
                for k in range(TB):
                    dst = ring.start(pe, name, k)
                    for i in range(BPB):
                        b = BPB * k + i
                        last = nc.tensor.matmul(dst[0:N, P * i:P * i + P], XT[:, N * b:N * b + N], rhs, start=True, stop=True)
                    last.then_inc(ring.filled_sem, 1)

            pe.wait_ge(consts_done, 1)
            pe.wait_ge(weights_in, WEIGHTS)
            dst = pre.start(pe, "wT")
            for i in range(4):
                last = nc.tensor.transpose(dst[:, P * i:P * i + P], xW[:, i, :], ident[:, :])
            last.then_inc(pre.filled_sem, 1)
            nc.tensor.transpose(pre.start(pe, "woT")[:, 0:P], xW[:, 4, :], ident[:, :]).then_inc(pre.filled_sem, 1)
            pe.wait_ge(x_in, 16)
            transpose_tokens(pre, "xT", X2)
            dst = pre.start(pe, "bias")
            pre.taken(pe, "wT")
            nc.tensor.matmul(dst[:, 0:1], xWT[:, 1, :], kvb[:, 0:1], start=True, stop=True)
            nc.tensor.matmul(dst[0:N, P:2 * P], kvb[:, 0:1].to_broadcast([P, N]), xWT[:, 2, :], start=True, stop=True)\
              .then_inc(pre.filled_sem, 1)
            for k in range(TB):
                pre.taken(pe, "xT", k)
                nc.tensor.matmul(pre.start(pe, "qT", k)[:, 0:TW], aWq[:, :], XT[:, TW * k:TW * k + TW], start=True, stop=True)\
                  .then_inc(pre.filled_sem, 1)
            for b in range(B):
                nc.tensor.matmul(pre.start(pe, "kvh", b)[0:N, 0:3 * P], XT[:, N * b:N * b + N], aWkvh[:, :],
                                 start=True, stop=True).then_inc(pre.filled_sem, 1)
            for k in range(TB):
                pre.taken(pe, "qT", k)
            for name, b in kv_nd:
                dst = pre.start(pe, name, b)
                if name == "kv":
                    pe.wait_ge(k_done, b // BPB + 1)
                    keys = KVH[:, b, 0:P]
                    nc.tensor.matmul(dst[:, 0:P], keys, KVH[:, b, P:2 * P], start=True, stop=True)
                    last = nc.tensor.matmul(dst[:, P:P + H], keys, ones[0:N, :], start=True, stop=True)
                else:
                    for i in range(min(3, B - 3 * b)):
                        c = 3 * b + i
                        pre.taken(pe, "kv", c)
                        last = nc.tensor.matmul(dst[0:N, (P + H) * i:(P + H) * (i + 1)], QT[:, N * c:N * c + N],
                                                R[:, c % 6, :], start=True, stop=True)
                last.then_inc(pre.filled_sem, 1)
            pe.wait_ge(attn_done, 1)
            transpose_tokens(pre, "gT", GATE)
            for k in range(TB):
                pre.taken(pe, "gT", k)
            project(pre, "o", aWo[:, :])
            pe.wait_ge(qn_done, 1)
            transpose_tokens(pre, "qnT", GATE)
            for k in range(TB):
                pre.taken(pe, "qnT", k)
                nc.tensor.matmul(pre.start(pe, "Q", k)[:, 0:TW], xWT[:, 0, :], XT[:, TW * k:TW * k + TW],
                                 start=True, stop=True).then_inc(pre.filled_sem, 1)
            project(pre, "gate", xWT[:, 3, :])
            for k in range(TB):
                pre.taken(pe, "gate", k)
            pre.taken(pe, "woT")
            pe.wait_ge(zeros_done, 1)
            pe.wait_ge(folded, 1)

            def fill_work(name, batch):
                n, s = num(batch), batch[1]
                kind, k = name[0], int(name[1])
                wait_past(pe, w_read, w_at(name, n))
                if kind == "T":
                    if k == 0:
                        pe.wait_ge(ctx_normed, n + 1)
                    for i in range(4 * k, min(4 * k + 4, KT)):
                        w = P if i < KT - 1 else LAST
                        last = nc.tensor.transpose(wk[:, P * (i - 4 * k):P * (i - 4 * k) + w], xn[0:w, i, :], ident[0:w, 0:w])
                if kind == "K":
                    last = nc.tensor.matmul(wk[:, 0:KCW], WkTg[:, :], xnT[s][:, KCW * k:KCW * k + KCW], start=True, stop=True)
                if kind == "V":
                    for i in range(4 * k, min(4 * k + 4, KT)):
                        w = P if i < KT - 1 else LAST
                        last = nc.tensor.matmul(wk[0:w, P * (i - 4 * k):P * (i - 4 * k) + P], xnT[s][:, P * i:P * i + w],
                                                WvTg[:, :], start=True, stop=True)
                if kind == "M":
                    pe.wait_ge(max_done, n + 1)
                    last = nc.tensor.matmul(wk[MROW:DEPTH, 0:P], mx[:, :], ident[:, :], start=True, stop=True)
                if kind == "Y":
                    pe.wait_ge(pv_copied, n + 1)
                    for g in range(GR):
                        last = nc.tensor.transpose(wk[0:N, P * g:P * g + P], pvs[:, N * g:N * g + N], ident[:, :])
                if kind == "G":
                    pe.wait_ge(y_gated, n + 1)
                    last = nc.tensor.transpose(wk[:, 0:N], y[:, :], ident[0:N, 0:N])
                if kind == "O":
                    pe.wait_ge(w_read, w_at("G0", n) + 1)
                    last = nc.tensor.matmul(wk[0:N, 0:P], yT[:, :], xWT[:, 4, :], start=True, stop=True)
                last.then_inc(w_filled, 1)

            def max_unit(batch, unit):
                n, s = num(batch), batch[1]
                rt, c = unit // CH, unit % CH
                w = P if rt < RT - 1 else LASTR
                if unit == 0:
                    pe.wait_ge(qbd_done, n + 1)
                    pe.wait_ge(khi_done, KC * (n + 1))
                wait_past(pe, mx_reduced, UNITS * n + unit - 1)
                rows = qbd[s][:, :, :].rearrange("p h q -> p (h q)")[:, P * rt:P * rt + w]
                nc.tensor.matmul(mxp[unit_slot(s, unit)][0:w, 0:CHW[c]], rows, khi[s][:, CHO[c]:CHO[c] + CHW[c]],
                                 start=True, stop=True).then_inc(mx_filled, 1)

            def score_step(batch, u):
                n, s = num(batch), batch[1]
                kt, h = u // 2, u % 2
                w = P if kt < KT - 1 else LAST
                if u == 0:
                    pe.wait_ge(ks_in[s], 16 * 3 * GR * (batch[0] + 1))
                    pe.wait_ge(qs_done, n + 1)
                    pe.wait_ge(max_stacked, n + 1)
                wait_past(pe, exp_done, STEPS * n + u - 1)
                for g in range(2):
                    group = 2 * h + g
                    last = nc.tensor.matmul(score[h][0:w, g, :], ks[s][:, group, P * kt:P * kt + w],
                                            qs[s][:, GW * group:GW * group + GW], start=True, stop=True)
                last.then_inc(scored, 1)

            def value_step(batch, u):
                n, s = num(batch), batch[1]
                kt, h = u // 2, u % 2
                if u == 0:
                    wait_past(pe, pv_copied, n)
                    pe.wait_ge(w_read, w_at("V2", n) + 1)
                pe.wait_ge(exp_done, STEPS * n + u + 1)
                for c in range(HG):
                    place = kt * H + 2 * (HG * h + c)
                    last = nc.tensor.matmul(
                        pvp[32 * c:32 * c + 2 * VW, 2 * N * h:2 * N * (h + 1)],
                        vs[s][:, place:place + 2, :].rearrange("p g i -> p (g i)"), pr[h][:, :, c, :],
                        start=(u == 0), stop=(kt == KT - 1), skip_group_check=True)
                last.then_inc(pv_done, 1)

            def phase(batch, has):
                for u in range(STEPS):
                    if "C" in has:
                        score_step(batch, u)
                    name = FILLS.get(u)
                    if name and STAGE_OF[name[0]] in has:
                        fill_work(name, later(batch, AHEAD[STAGE_OF[name[0]]]))
                    for ahead, unit in mx_units(u, has, UNITS):
                        max_unit(later(batch, ahead), unit)
                    if "C" in has and u > 0:
                        value_step(batch, u - 1)
                if "C" in has:
                    value_step(batch, STEPS - 1)

            phases(pe, phase)

            transpose_tokens(post, "x2T", X2, x2_done)
            dst = post.start(pe, "logits")
            for b in range(B):
                if b % BPB == 0:
                    post.taken(pe, "x2T", b // BPB)
                last = nc.tensor.matmul(dst[0:N, E * b:E * b + E], X2T[:, N * b:N * b + N], Wr[:, :], start=True, stop=True)
            last.then_inc(post.filled_sem, 1)
            pe.wait_ge(comb_done, 1)
            for k in range(TB):
                dst = post.start(pe, "cT", k)
                for i in range(BPB):
                    last = nc.tensor.transpose(dst[0:E, N * i:N * i + N], ex[:, BPB * k + i, :], ident[0:N, 0:N])
                last.then_inc(post.filled_sem, 1)
            for k in range(TB):
                post.taken(pe, "cT", k)
            for k in range(TB):
                nc.tensor.matmul(PS[:, 4 + k, 0:TW], zero[:, :], x2hi[:, TW * k:TW * k + TW], start=True, stop=True)

            def split_product(dst, hi, lo, right_hi, right_lo, start):
                nc.tensor.matmul(dst, hi, right_hi, start=start, stop=False, skip_group_check=not start)
                nc.tensor.matmul(dst, hi, right_lo, start=False, stop=False, skip_group_check=not start)
                return nc.tensor.matmul(dst, lo, right_hi, start=False, stop=True, skip_group_check=not start)

            def up(pair, s, i):
                e, tb, c = 2 * pair + s, i // HC, i % HC
                cols, hid = slice(TW * tb, TW * tb + TW), slice(P * c, P * c + P)
                if not isinstance(pair, int) or UPE * e + i >= 2:
                    pe.wait_ge(h_done, UPE * e + i - 1)
                for m, (hi, lo) in enumerate(((x2hi, x2lo), (xehi[s], xelo[s]))):
                    last = split_product(PS[:, 2 * (i % 2) + m, 0:TW], whi[s][:, m, hid], wlo[s][:, m, hid],
                                         hi[:, cols], lo[:, cols], True)
                last.then_inc(gu_filled, 1)

            def down(pair, s, i):
                e, tb, c = 2 * pair + s, i // HC, i % HC
                hid = slice(P * c, P * c + P)
                pe.wait_ge(hlo_done, UPE * e + i + 1)
                split_product(PS[:, 4 + tb, 0:TW], whi[s][:, 2, hid], wlo[s][:, 2, hid],
                              hhi[i % HS][:, :], hlo[i % HS][:, :], False).then_inc(d_done, 1)

            def expert(pair, s, more=True):
                e = 2 * pair + s
                pe.wait_ge(w_split, HC * (e + 1))
                pe.wait_ge(xelo_done, TB * (e + 1))
                for i in range(UPE):
                    up(pair, s, i)
                    if i >= LAG:
                        down(pair, s, i - LAG)
                    elif not isinstance(e, int) or e > 0:
                        down(*later((pair, s), -1), UPE + i - LAG)
                if not more:
                    for i in range(UPE - LAG, UPE):
                        down(pair, s, i)

            experts(pe, expert)
            for k in range(TB):
                dst = post.start(pe, "yN", k)
                pe.wait_ge(out_copied, k + 1)
                for i in range(BPB):
                    last = nc.tensor.transpose(dst[0:N, P * i:P * i + P], OT[:, TW * k + N * i:TW * k + N * i + N], ident[:, :])
                last.then_inc(post.filled_sem, 1)


def kernel(**inputs):
    import numpy as _np
    import concourse.bacc as _bacc
    from concourse import mybir as _mybir
    from concourse.bass_utils import run_bass_kernel_spmd as _run

    nc = _bacc.Bacc("TRN2", target_bir_lowering=False, num_devices=1)
    arrays, tensors = {}, {}
    for name, value in inputs.items():
        a = _np.ascontiguousarray(value)
        arrays[f"in_{name}"] = a
        tensors[name] = nc.dram_tensor(f"in_{name}", a.shape, _mybir.dt.from_np(a.dtype), kind="ExternalInput").ap()
    shape = tensors["x"].shape
    out = nc.dram_tensor("out", shape, F32, kind="ExternalOutput").ap()
    comb = nc.dram_tensor("comb", (tensors["L0_ffn_Wr"].shape[1], shape[0] * shape[1]), F32, kind="Internal").ap()
    decoder_layer(nc, tensors, out, comb)
    r = _run(nc, [arrays], core_ids=[0])
    return r.results[0]["out"]
```

```python
from contextlib import ExitStack

import concourse.bass as bass
from concourse import mybir

ALU = mybir.AluOpType
ACT = mybir.ActivationFunctionType
AXL = mybir.AxisListType
F32 = mybir.dt.float32
F16 = mybir.dt.float16

P = 128
BANK = 512
EPS = 1e-5
STEPS = 24
MX_EARLY = 16
MX_FROM = 15
GATE_AT = ((-2, 17), (-2, 21), (-1, 2), (-1, 6))
MX_UNTIL = 15
STATS_FROM = 5

FILLS = {1: "T0", 3: "T1", 5: "T2", 6: "Y0", 7: "K0", 9: "K1", 11: "K2", 12: "K3",
         15: "G0", 16: "M0", 18: "O0", 19: "V0", 22: "V1", 23: "V2"}
X2T_AT = (2, 3, 5)
LOGITS_AT = 7
EXP_AT = 10
COMB_AT = (15, 16, 17)
STAGE_OF = {"T": "A", "K": "A", "V": "B", "M": "B", "Y": "D", "G": "D", "O": "D"}
AHEAD = {"A": 2, "B": 1, "C": 0, "D": -1}


def stages(p, batches):
    return "".join(x for x in "ABCD" if 0 <= p + AHEAD[x] < batches)


def fills_of(has):
    return [FILLS[u] for u in sorted(FILLS) if STAGE_OF[FILLS[u][0]] in has]


def fills_before(p, batches):
    return sum(len(fills_of(stages(q, batches))) for q in range(-2, p))


def mx_units(u, has, units):
    def late(v):
        return MX_EARLY + min(v, MX_UNTIL) * (units - MX_EARLY) // MX_UNTIL

    def first(v):
        return max(0, v - MX_FROM) * MX_EARLY // (STEPS - MX_FROM)

    found = [(1, k) for k in range(late(u), late(u + 1)) if "B" in has]
    return found + [(2, k) for k in range(first(u), first(u + 1)) if "A" in has]


X_FILLS = ("T0", "T1", "T2")
K_FILLS = ("K0", "K1", "K2", "K3")


def prepared(name, n):
    return isinstance(n, int) and (n == 0 and name in X_FILLS + K_FILLS or n == 1 and name in X_FILLS)


def wait_past(eng, semaphore, value):
    if not isinstance(value, int) or value > 0:
        eng.wait_ge(semaphore, value)


class Ring:

    def __init__(self, psum, filled, read, order):
        self.psum, self.filled_sem, self.read, self.n = psum, filled, read, len(read)
        self.at = {key: i for i, key in enumerate(order)}

    def bank(self, *key):
        return self.psum[:, self.at[key] % self.n, :]

    def start(self, pe, *key):
        i = self.at[key]
        if i >= self.n:
            pe.wait_ge(self.read[i % self.n], i // self.n)
        return self.bank(*key)

    def filled(self, eng, *key):
        eng.wait_ge(self.filled_sem, self.at[key] + 1)
        return self.bank(*key)

    def reader(self, *key):
        return self.read[self.at[key] % self.n]

    def taken(self, eng, *key):
        i = self.at[key]
        eng.wait_ge(self.read[i % self.n], i // self.n + 1)


def decoder_layer(nc, t, out, comb_dram):
    B, N, D = t["x"].shape
    S = t["ctx_1024"].shape[1]
    H, DH = 16, 8
    E = t["L0_ffn_Wr"].shape[1]
    HID = t["L0_ffn_Wg"].shape[2]
    TOK = B * N
    KT = -(-S // P)
    LAST = S - (KT - 1) * P
    GR = 4
    HG = H // GR
    GW = HG * N
    QW = H * N
    RT = -(-QW // P)
    LASTR = QW - (RT - 1) * P
    CH = 3
    CHW = [S // CH + (1 if c < S % CH else 0) for c in range(CH)]
    CHO = [sum(CHW[:c]) for c in range(CH)]
    UNITS = RT * CH
    MROW = 96
    DEPTH = MROW + RT
    TF = -(-KT // 4)
    KC = 4
    KCW = S // KC
    TB = 4
    TW = TOK // TB
    BPB = B // TB
    HC = HID // P
    UPE = TB * HC
    HS = 4
    LAG = 3
    VW = DH + 1
    SCALE = float(DH) ** -0.5
    DEPTH_SCALE = 12 ** -0.5
    NF = len(fills_of("ABCD"))
    assert D == P and STEPS == 2 * KT and KC * KCW == S and B % 2 == 0 and GW <= BANK

    def later(batch, k):
        return batch[0] + (batch[1] + k) // 2, (batch[1] + k) % 2

    last_batch = ((B - 1) // 2, (B - 1) % 2)

    def num(batch):
        return 2 * batch[0] + batch[1]

    def unit_slot(s, unit):
        return (UNITS * s + unit) % 2

    def w_at(name, n):
        stage = STAGE_OF[name[0]]
        p = n - AHEAD[stage]
        if isinstance(n, int):
            return fills_before(p, B) + fills_of(stages(p, B)).index(name)
        return NF * p + (fills_before(1, B) - NF + fills_of("ABCD").index(name))

    def phases(eng, phase, peeled=2):
        for p in (-2, -1, 0, 1):
            phase((p // 2, p % 2), stages(p, B))
        with eng.Fori(1, (B - peeled) // 2) as j:
            for s in range(2):
                phase((j, s), "ABCD")
        for p in range(B - peeled, B):
            phase((p // 2, p % 2), stages(p, B))

    EARLY = TB - 1
    SCALE_AT = (2, 4, 6, 8)
    SPLIT_AT = (9, 10, 11, 12)

    OPENING = ([(0, i) for i in range(3 * HC)] + [(1, i) for i in range(2 * HC)]
               + [(0, i) for i in range(3 * HC, UPE)] + [(1, i) for i in range(2 * HC, UPE)])
    OPENING_SCALES = [(0, 0), (0, 1), (0, 2), (1, 0), (1, 1), (1, 2), (0, 3), (1, 3)]
    PE_AT = {0: "Y", 4: "G", 6: "O", 11: "X", 13: "L", 17: "C", 18: "B"}
    ACT_AT = {4: "G", 11: "X", 14: "E", 17: "C"}
    DVE_AT = {0: "Y", 6: "O", 10: "N", 11: "X", 13: "L", 14: "R"}
    POOL_AT = {0: "Y", 6: "N"}
    OPEN_SCALE_AT = {1: (1, 0), 3: (1, 1), 5: (1, 2), 17: (0, 3), 18: (1, 3),
                     20: (2, 0), 22: (2, 1), 24: (2, 2), 26: (2, 3)}
    OPEN_SPLIT_AT = (26, 27, 28, 29)

    OUT_AT = (7, 11, 15)
    FLIP_AT = (8, 12)
    ADD_AT = (9, 13)
    MOMENTS_AT = (10,)
    NORM_AT = (13,)

    def scale_count(e, k):
        if isinstance(e, int) and e < 2:
            return OPENING_SCALES.index((e, k)) + 1
        return TB * e + k + 1

    def experts(eng, opening, expert):
        opening()
        with eng.Fori(1, E // 2 - 1) as j:
            for s in range(2):
                expert(j, s)
        expert(E // 2 - 1, 0)
        expert(E // 2 - 1, 1, more=False)

    def widen(ap, n, width):
        return ap.unsqueeze(2).to_broadcast([n, ap.shape[1], width])

    def repeat(ap, n, k):
        return ap.unsqueeze(1).to_broadcast([n, k, ap.shape[1]])

    with ExitStack() as ctx:
        def sb(name, shape, dt=F32, stack=ctx):
            return stack.enter_context(nc.sbuf_tensor(name, shape, dt))

        def sem(name):
            return ctx.enter_context(nc.semaphore(name))

        PS = ctx.enter_context(nc.psum_tensor("PS", [P, 8, BANK], F32))
        score = [PS[:, 2 * h:2 * h + 2, 0:GW] for h in range(2)]
        mxp = [PS[:, 4 + i, :] for i in range(2)]
        pvp = PS[:, 6, 0:GR * N]
        wk = PS[:, 7, :]

        ident = sb("ident", [P, P])
        headmask = sb("headmask", [P, H], F16)
        stackmask = sb("stackmask", [96, HG], F16)
        kvmask = sb("kvmask", [P, P + H])
        rowmask = sb("rowmask", [P, RT], F16)
        minushalf = sb("minushalf", [P, B])
        ones = sb("ones", [P, H])
        before = sb("before", [N, E, E])
        aWq = sb("aWq", [P, P])
        aWo = sb("aWo", [P, P])
        aWkvh = sb("aWkvh", [P, 3 * P])
        abq = sb("abq", [P, 1])
        arow = {n: sb("arow_" + n, [N, P]) for n in ("beta", "ln_w", "ln_b", "bo")}
        xW = sb("xW", [P, 5, P])
        xWT = sb("xWT", [P, 5, P])
        WkTg = [sb("WkTg_" + part, [P, P], F16) for part in ("hi", "lo")]
        WvTg = [sb("WvTg_" + part, [P, P], F16) for part in ("hi", "lo")]
        kvg = sb("kvg", [P, 1])
        kvb = sb("kvb", [P, 1])
        kbias = sb("kbias", [P, 1])
        vrow = sb("vrow", [N, P])
        bgrow = sb("bgrow", [N, P])
        grow = sb("grow", [N, P])
        WqTg = sb("WqTg", [P, P])
        WgTg = sb("WgTg", [P, P])
        qg = sb("qg", [P, 1])
        qb = sb("qb", [P, 1])
        qbias = sb("qbias", [P, 1])
        Wr = sb("Wr", [P, E])
        X1 = sb("X1", [N, B, P])
        X2 = sb("X2", [N, B, P])
        GATE = sb("GATE", [N, B, P])
        qhi = sb("qhi", [P, TOK], F16)
        qlo = sb("qlo", [P, TOK], F16)
        qrows = sb("qrows", [96, GR, TOK], F16)
        tstat = sb("tstat", [N, B, 6])
        tsm = sb("tsm", [N, 8, B])

        first = ExitStack()
        XT = sb("XT", [P, TOK], stack=first)
        QT = sb("QT", [P, TOK], stack=first)
        KVH = sb("KVH", [N, B, 3 * P], stack=first)
        R = sb("R", [P, 6, P + H], stack=first)
        DEN = sb("DEN", [N, B, H], stack=first)
        kvhrow = sb("kvhrow", [N, 3 * P], stack=first)
        first.close()
        wst = [sb(f"wst{i}", [P, 3, HID]) for i in range(2)]
        whi = [sb(f"whi{i}", [P, 3, HID], F16) for i in range(2)]
        wlo = [sb(f"wlo{i}", [P, 3, HID], F16) for i in range(2)]
        cb = [sb(f"cb{i}", [P, TOK]) for i in range(2)]
        X2T = sb("X2T", [P, TOK])
        assert 4 * (TOK * 2 + B * (3 * P + H) + 6 * (P + H) + 3 * P) <= 2 * 3 * HID * 8 + 3 * 4 * TOK
        early = ExitStack()
        ct = [sb(f"ct{i}", [P, KT, P], stack=early) for i in range(2)]
        xn = sb("xn", [P, KT, P], stack=early)
        cstat = [sb(f"cstat{i}", [P, KT, 6], stack=early) for i in range(2)]
        csm = sb("csm", [P, 8, KT], stack=early)
        xhi = [sb(f"xhi{i}", [P, S], F16, early) for i in range(2)]
        xlo = [sb(f"xlo{i}", [P, S], F16, early) for i in range(2)]
        exact = sb("exact", [P, S], stack=early)
        khi = [sb(f"khi{i}", [P, S], F16, early) for i in range(2)]
        klo = [sb(f"klo{i}", [P, S], F16, early) for i in range(2)]
        qbd = [sb(f"qbd{i}", [P, H, N], F16, early) for i in range(2)]
        ks = [sb(f"ks{i}", [DEPTH, GR, S], F16, early) for i in range(2)]
        vs = [sb(f"vs{i}", [P, KT * H, VW], stack=early) for i in range(2)]
        qs = [sb(f"qs{i}", [DEPTH, RT * P], F16, early) for i in range(2)]
        pr = [sb(f"pr{i}", [P, 2, HG, N], stack=early) for i in range(2)]
        mxs = [sb(f"mxs{i}", [P, RT, CH], stack=early) for i in range(2)]
        mx = sb("mx", [P, RT], stack=early)
        mrow = sb("mrow", [DEPTH, P], F16, early)
        pvs = sb("pvs", [P, GR * N], stack=early)
        rden = sb("rden", [N, GR, HG], stack=early)
        y = sb("y", [N, P], stack=early)
        yT = sb("yT", [P, N], stack=early)
        early.close()
        late = ExitStack()
        x2hi = sb("x2hi", [P, TOK], F16, late)
        x2lo = sb("x2lo", [P, TOK], F16, late)
        LG = sb("LG", [N, B, E], stack=late)
        RK = [sb(f"RK{i}", [N, B - BPB, E, E], stack=late) for i in range(2)]
        rank = sb("rank", [N, B, E], stack=late)
        ex = sb("ex", [N, B, E], stack=late)
        rsm = sb("rsm", [N, 3, B], stack=late)
        combT = sb("combT", [E, TOK], stack=late)
        xe = sb("xe", [P, TOK], stack=late)
        xehi = [sb(f"xehi{i}", [P, TOK], F16, late) for i in range(2)]
        xelo = [sb(f"xelo{i}", [P, TOK], F16, late) for i in range(2)]
        zero = sb("zero", [P, P], F16, late)
        sg = [sb(f"sg{i}", [P, TW], stack=late) for i in range(2)]
        hh = [sb(f"hh{i}", [P, TW], stack=late) for i in range(HS)]
        hhi = [sb(f"hhi{i}", [P, TW], F16, late) for i in range(HS)]
        hlo = [sb(f"hlo{i}", [P, TW], F16, late) for i in range(HS)]
        OT = sb("OT", [P, TOK], stack=late)
        late.close()

        x_in, attn_weights_in, weights_in = sem("x_in"), sem("attn_weights_in"), sem("weights_in")
        ident_done, consts_done, ct_zeroed, zeros_done, ones_done = (
            sem(n) for n in ("ident_done", "consts_done", "ct_zeroed", "zeros_done", "ones_done"))
        tok_stats, tok_scale = sem("tok_stats"), sem("tok_scale")
        folded, k_done, h_scaled, attn_done, qn_done = (
            sem(n) for n in ("folded", "k_done", "h_scaled", "attn_done", "qn_done"))
        qhi_done, gate_done, qrows_in = sem("qhi_done"), sem("gate_done"), sem("qrows_in")
        ctx_in = [sem(f"ctx_in{i}") for i in range(2)]
        ks_in = [sem(f"ks_in{i}") for i in range(2)]
        ctx_stats, ctx_normed = sem("ctx_stats"), sem("ctx_normed")
        xlo_done, khi_done, klo_done = sem("xlo_done"), sem("khi_done"), sem("klo_done")
        qbd_done, qs_done = sem("qbd_done"), sem("qs_done")
        mx_filled, mx_reduced, max_done, max_stacked = (
            sem(n) for n in ("mx_filled", "mx_reduced", "max_done", "max_stacked"))
        scored, exp_done, pv_done, pv_copied = (sem(n) for n in ("scored", "exp_done", "pv_done", "pv_copied"))
        y_gated = sem("y_gated")
        w_filled, w_read = sem("w_filled"), sem("w_read")
        x2_done, x2hi_done, x2lo_done, logits_less_max, exped, comb_done, comb_stored = (
            sem(n) for n in ("x2_done", "x2hi_done", "x2lo_done", "logits_less_max", "exped", "comb_done", "comb_stored"))
        cb_in = [sem(f"cb_in{i}") for i in range(2)]
        wst_in = [sem(f"wst_in{i}") for i in range(2)]
        xe_done, xehi_done, xelo_done, whi_done, w_split = (sem(n) for n in ("xe_done", "xehi_done", "xelo_done", "whi_done", "w_split"))
        gu_filled, silu_done, h_done, hhi_done, hlo_done, d_done = (
            sem(n) for n in ("gu_filled", "silu_done", "h_done", "hhi_done", "hlo_done", "d_done"))
        out_copied, out_flipped, y_done, stored = (sem(n) for n in ("out_copied", "out_flipped", "y_done", "stored"))

        def staggered(first, second):
            return [key for k in range(TB + 1) for key in ([(first, k)] if k < TB else []) + ([(second, k - 1)] if k else [])]

        kv_nd = []
        for g in range(-(-B // 3) + 1):
            kv_nd += [("kv", b) for b in range(3 * g, min(3 * g + 3, B))]
            kv_nd += [("nd", g - 1)] if g else []
        pre = Ring(PS, sem("pre_filled"), [sem(f"pre_read{i}") for i in range(4)],
                   [(n, k) for n in ("xT", "qT") for k in range(TB)] + [("kvh", b) for b in range(B)]
                   + [("wT",), ("woT",), ("bias",)] + kv_nd
                   + staggered("gT", "o") + staggered("qnT", "Q") + [("gate", k) for k in range(TB)])
        route = [Ring(PS[:, 4:6, :], sem("route_filled"), [sem(f"route_read{i}") for i in range(2)],
                      [("x2T", k) for k in range(EARLY)] + [("logits", 0)] + [("cT", k) for k in range(EARLY)]),
                 Ring(PS[:, 7:8, :], sem("last_filled"), [sem("last_read")],
                      [("x2T", EARLY), ("logits", EARLY), ("cT", EARLY), ("rows", 0), ("rows", 1)])]

        def ring_of(k):
            return route[k == EARLY]

        block = ctx.enter_context(nc.Block())

        attn_loads = [(aWq[:, :], t["L0_attn_Wq"])]
        attn_loads += [(aWkvh[:, P * i:P * i + P], t["L0_attn_" + n]) for i, n in enumerate(("Wk", "Wv", "Wh"))]
        attn_loads += [(abq[:, :], t["L0_attn_bq"].rearrange("(p o) -> p o", o=1))]
        attn_loads += [(kvhrow[:, P * i:P * i + P], t["L0_attn_" + n].partition_broadcast(N))
                       for i, n in enumerate(("bk", "bv", "bh"))]
        loads = [(xW[:, i, :], t["L0_xattn_" + n]) for i, n in enumerate(("Wq", "Wk", "Wv", "Wg", "Wo"))]
        loads += [(aWo[:, :], t["L0_attn_Wo"])]
        loads += [(c[:, :], t["L0_xattn_" + n].rearrange("(p o) -> p o", o=1)) for c, n in
                  ((kvg, "kvln_g"), (kvb, "kvln_b"), (qg, "qln_g"), (qb, "qln_b"))]
        loads += [(arow[n][:, :], t["L0_attn_" + n].partition_broadcast(N)) for n in arow]
        loads += [(bgrow[:, :], t["L0_xattn_bg"].partition_broadcast(N)), (Wr[:, :], t["L0_ffn_Wr"])]
        ATTN_WEIGHTS = 16 * len(attn_loads)
        WEIGHTS = 16 * len(loads)

        @block.sync
        def _(sp):
            sp.dma_start(X2[:, :, :], t["x"].rearrange("b n d -> n b d")).then_inc(x_in, 16)
            for dst, src in attn_loads:
                sp.dma_start(dst, src).then_inc(attn_weights_in, 16)

            def load_context(batch):
                n, s = num(batch), batch[1]
                if isinstance(n, int) and n < 4:
                    wait_past(sp, ctx_normed, n - 1)
                else:
                    sp.wait_ge(scored, STEPS * (n - 3))
                src = t["ctx_1024"]
                src = src[n] if isinstance(n, int) else src[bass.ds(n, 1)].rearrange("o s d -> (o s) d")
                sp.dma_start(ct[s][:, 0:KT - 1, :],
                             src[0:(KT - 1) * P, :].rearrange("(p t) d -> p t d", p=P)).then_inc(ctx_in[s], 16)
                sp.dma_start(ct[s][0:LAST, KT - 1, :], src[(KT - 1) * P:S, :]).then_inc(ctx_in[s], 16)

            sp.wait_ge(ct_zeroed, 1)
            load_context((0, 0))
            for dst, src in loads:
                sp.dma_start(dst, src).then_inc(weights_in, 16)
            load_context((0, 1))
            for k in range(TB):
                pre.taken(sp, "Q", k)
            for k, part in enumerate((qhi, qlo, qhi)):
                for g in range(GR):
                    sp.dma_start(qrows[32 * k:32 * k + 32, g, :], part[32 * g:32 * g + 32, :]).then_inc(qrows_in, 16)

            def load_expert(pair, s):
                e = 2 * pair + s
                if not isinstance(pair, int) or pair > 0:
                    sp.wait_ge(d_done, UPE * (e - 1))
                for i, w in enumerate(("Wg", "Wu")):
                    src = t["L0_ffn_" + w]
                    src = src[e] if isinstance(e, int) else src[bass.ds(e, 1)].rearrange("o c h -> (o c) h")
                    sp.dma_start(wst[s][:, i, :], src).then_inc(wst_in[s], 16)
                src = t["L0_ffn_Wd"]
                src = src[e] if isinstance(e, int) else src[bass.ds(e, 1)].rearrange("o h c -> (o h) c")
                sp.dma_start(wst[s][:, 2, :].rearrange("p (k c) -> p k c", c=P),
                             src.rearrange("(k p) c -> p k c", p=P)).then_inc(wst_in[s], 16)

            def phase(batch, has):
                if isinstance(batch[0], int) and num(batch) == B - 3:
                    for s in range(2):
                        load_expert(0, s)
                ahead = later(batch, 3)
                if not isinstance(batch[0], int) or 2 <= num(ahead) < B:
                    load_context(ahead)
                if "B" in has:
                    n, s = num(later(batch, 1)), later(batch, 1)[1]
                    if isinstance(n, int):
                        wait_past(sp, scored, STEPS * (n - 1))
                    sp.wait_ge(klo_done, KC * (n + 1))
                    for k, part in enumerate((khi, khi, klo)):
                        for g in range(GR):
                            sp.dma_start(ks[s][32 * k:32 * k + 32, g, :], part[s][32 * g:32 * g + 32, :])\
                              .then_inc(ks_in[s], 16)

            phases(sp, phase, peeled=4)

            def load_comb(pair, s, cols=slice(0, TOK)):
                e = 2 * pair + s
                if not isinstance(pair, int):
                    sp.wait_ge(xe_done, TB * e)
                src = comb_dram[e:e + 1, cols] if isinstance(e, int) else comb_dram[bass.ds(e, 1), cols]
                sp.dma_start(cb[s][:, cols], src.to_broadcast([P, cols.stop - cols.start])).then_inc(cb_in[s], 16)

            for k, cols in ((0, slice(0, EARLY * TW)), (EARLY, slice(EARLY * TW, TOK))):
                for i in range(k, EARLY) if k < EARLY else (EARLY,):
                    ring_of(i).taken(sp, "cT", i)
                sp.dma_start(comb_dram[:, cols], combT[:, cols]).then_inc(comb_stored, 16)
                sp.wait_ge(comb_stored, 16 * (1 + (k > 0)))
                if k < EARLY:
                    for s in range(2):
                        load_comb(0, s, cols)
            with sp.Fori(1, E // 2) as j:
                for s in range(2):
                    load_comb(j, s)
                    load_expert(j, s)
            for k in range(TB):
                sp.wait_ge(y_done, k + 1)
                blk = slice(BPB * k, BPB * k + BPB)
                sp.dma_start(out[blk].rearrange("b n d -> n b d"), X2[:, blk, :]).then_inc(stored, 16)
            sp.wait_ge(stored, 16 * TB)

        def moments(pool, stat, small, n, cols):
            r = [small[0:n, i, cols] for i in range(8)]
            st = [stat[0:n, cols, i] for i in range(6)]
            nc.gpsimd.tensor_tensor(r[2], st[1], st[4], ALU.add)
            nc.gpsimd.tensor_tensor(r[3], st[1], st[4], ALU.subtract)
            nc.gpsimd.tensor_tensor(r[4], st[2], st[5], ALU.add)
            pool.drain()
            nc.gpsimd.tensor_scalar(r[0], r[2], 0.5, None, ALU.mult)
            nc.gpsimd.tensor_scalar(r[5], r[3], 0.5, None, ALU.mult)
            nc.gpsimd.tensor_scalar(r[6], r[4], 1.0 / D, EPS, ALU.mult, ALU.add)
            pool.drain()
            nc.gpsimd.tensor_tensor(r[7], r[5], r[5], ALU.mult)
            pool.drain()
            nc.gpsimd.tensor_tensor(r[2], r[7], r[6], ALU.add)
            pool.drain()
            return nc.gpsimd.tensor_tensor(r[1], r[2], minushalf[0:n, cols], ALU.pow)

        @block.gpsimd
        def _(pool):
            nc.gpsimd.memset(ident[:, :], 0.0)
            pool.drain()
            nc.gpsimd.affine_select(out=ident[:, :], in_=ident[:, :], compare_op=ALU.not_equal, fill=1.0,
                                    base=0, pattern=[[-1, P]], channel_multiplier=1).then_inc(ident_done, 1)
            nc.gpsimd.memset(headmask[:, :], 1.0)
            nc.gpsimd.memset(kvmask[:, :], 0.0)
            nc.gpsimd.memset(rowmask[:, :], 0.0)
            nc.gpsimd.memset(minushalf[:, :], -0.5)
            nc.gpsimd.memset(before[:, :, :], 1.0)
            pool.drain()
            nc.gpsimd.affine_select(out=rowmask[:, :], in_=rowmask[:, :], compare_op=ALU.not_equal, fill=1.0,
                                    base=-MROW, pattern=[[-1, RT]], channel_multiplier=1)
            nc.gpsimd.affine_select(out=headmask[:, :], in_=headmask[:, :], compare_op=ALU.is_ge, fill=0.0,
                                    base=0, pattern=[[-DH, H]], channel_multiplier=1)
            nc.gpsimd.affine_select(out=before[:, :, :], in_=before[:, :, :], compare_op=ALU.is_gt, fill=0.0,
                                    base=0, pattern=[[1, E], [-1, E]], channel_multiplier=0)
            pool.drain()
            nc.gpsimd.affine_select(out=headmask[:, :], in_=headmask[:, :], compare_op=ALU.is_ge, fill=0.0,
                                    base=DH - 1, pattern=[[DH, H]], channel_multiplier=-1)
            for k in range(1 - P // H, P // H):
                nc.gpsimd.affine_select(out=kvmask[:, 0:P], in_=kvmask[:, 0:P], compare_op=ALU.not_equal, fill=1.0,
                                        base=-H * k, pattern=[[-1, P]], channel_multiplier=1)
                pool.drain()
            nc.gpsimd.tensor_copy(kvmask[:, P:P + H], kvmask[:, 0:H])
            for k in range(3):
                pool.drain()
                nc.gpsimd.tensor_copy(stackmask[32 * k:32 * k + 32, :], headmask[0:32, 0:HG])
            pool.drain()
            nc.gpsimd.memset(ones[:, :], 1.0).then_inc(consts_done, 1)

            def token_moments(count, cols=slice(0, B)):
                pool.wait_ge(tok_stats, count)
                moments(pool, tstat, tsm, N, cols).then_inc(tok_scale, 1)

            def norm_context(batch):
                n, s = num(batch), batch[1]
                pool.wait_ge(ctx_stats, n + 1)
                moments(pool, cstat[s], csm, P, slice(0, KT))
                pool.drain()
                nc.gpsimd.tensor_tensor(ct[s][:, :, :], ct[s][:, :, :], widen(csm[:, 0, :], P, P), ALU.subtract)
                pool.drain()
                if not isinstance(n, int) or n > 0:
                    pool.wait_ge(w_filled, w_at("T2", n - 1) + 1)
                nc.gpsimd.tensor_tensor(xn[:, :, :], ct[s][:, :, :], widen(csm[:, 1, :], P, P), ALU.mult)\
                  .then_inc(ctx_normed, 1)

            def place_queries(batch):
                n, s = num(batch), batch[1]
                wait_past(pool, mx_filled, UNITS * (n - 1))
                src = qhi[:, n * N:n * N + N] if isinstance(n, int) else qhi[:, bass.ds(n * N, N)]
                nc.gpsimd.tensor_tensor(qbd[s][:, :, :], repeat(src, P, H), widen(headmask[:, :], P, N), ALU.mult)\
                  .then_inc(qbd_done, 1)

            def low_context(batch):
                n, s = num(batch), batch[1]
                for k in range(TF):
                    pool.wait_ge(w_read, w_at(f"T{k}", n) + 1)
                    cols = slice(4 * P * k, min(4 * P * k + 4 * P, S))
                    nc.gpsimd.tensor_tensor(xlo[s][:, cols], exact[:, cols], xhi[s][:, cols], ALU.subtract)\
                      .then_inc(xlo_done, 1)

            def low_keys(batch):
                n, s = num(batch), batch[1]
                for k in range(KC):
                    pool.wait_ge(w_read, w_at(f"K{k}", n) + 1)
                    cols = slice(KCW * k, KCW * k + KCW)
                    nc.gpsimd.tensor_tensor(klo[s][:, cols], exact[:, cols], khi[s][:, cols], ALU.subtract)\
                      .then_inc(klo_done, 1)

            def gate_values(batch):
                m = num(batch)
                pool.wait_ge(w_read, w_at("Y0", m) + 1)
                nc.gpsimd.tensor_tensor(y[:, :], y[:, :], vrow[:, :], ALU.add)
                pool.drain()
                if isinstance(m, int) and m == 0:
                    pool.wait_ge(gate_done, TB)
                gate = GATE[:, m, :] if isinstance(m, int) else GATE[:, bass.ds(m, 1), :].rearrange("p o d -> p (o d)")
                nc.gpsimd.tensor_tensor(y[:, :], y[:, :], gate, ALU.mult).then_inc(y_gated, 1)

            norm_context((0, 0))
            gain, shift = KVH[:, :, 2 * P:3 * P], KVH[:, :, P:2 * P]
            for k in range(TB):
                blk = slice(BPB * k, BPB * k + BPB)
                for b in range(BPB * k, BPB * k + BPB):
                    pre.taken(pool, "kvh", b)
                if k == 0:
                    pool.wait_ge(weights_in, WEIGHTS)
                nc.gpsimd.tensor_tensor(gain[:, blk, :], gain[:, blk, :], repeat(arow["beta"][:, :], N, BPB), ALU.add)
            low_context((0, 0))
            norm_context((0, 1))

            def scale_h(k):
                blk = slice(BPB * k, BPB * k + BPB)
                pre.filled(pool, "kv", BPB * k + BPB - 1)
                nc.gpsimd.tensor_tensor(shift[:, blk, :], gain[:, blk, :], repeat(arow["ln_b"][:, :], N, BPB), ALU.mult)
                nc.gpsimd.tensor_tensor(gain[:, blk, :], gain[:, blk, :], repeat(arow["ln_w"][:, :], N, BPB), ALU.mult)\
                  .then_inc(h_scaled, 1)

            scale_h(0)
            for k in range(TB):
                if k + 1 < TB:
                    scale_h(k + 1)
                token_moments(1 + k, slice(BPB * k, BPB * k + BPB))
            low_keys((0, 0))
            for k in range(TB):
                token_moments(1 + TB + k, slice(BPB * k, BPB * k + BPB))
            pool.wait_ge(qhi_done, 1)
            place_queries((0, 0))
            low_context((0, 1))
            pool.wait_ge(qhi_done, TB)
            pool.drain()
            for s in range(2):
                last = nc.gpsimd.memset(ks[s][MROW:DEPTH, :, :], 1.0)
            last.then_inc(ones_done, 1)
            pool.drain()

            def phase(batch, has):
                n, s = num(later(batch, 1)), later(batch, 1)[1]
                if "A" in has and not prepared("T0", num(later(batch, 2))):
                    low_context(later(batch, 2))
                if "D" in has:
                    gate_values(later(batch, -1))
                if "B" in has:
                    if isinstance(n, int) and n == 0:
                        pool.wait_ge(qrows_in, 16 * 3 * GR)
                    wait_past(pool, scored, STEPS * (n - 1))
                    for g in range(GR):
                        src = qrows[:, g, n * N:n * N + N] if isinstance(n, int) else qrows[:, g, bass.ds(n * N, N)]
                        last = nc.gpsimd.tensor_tensor(
                            qs[s][0:96, g * GW:g * GW + GW].rearrange("p (h q) -> p h q", h=HG),
                            repeat(src, 96, HG), widen(stackmask[:, :], 96, N), ALU.mult)
                    last.then_inc(qs_done, 1)
                if "A" in has:
                    if not isinstance(batch[0], int) or num(batch) != -2:
                        place_queries(later(batch, 2))
                    if not prepared("K0", num(later(batch, 2))):
                        low_keys(later(batch, 2))
                if not isinstance(batch[0], int) or 2 <= num(batch) + 3 < B:
                    norm_context(later(batch, 3))
                if "B" in has:
                    pool.drain()
                    pool.wait_ge(w_read, w_at("M0", n) + 1)
                    nc.gpsimd.tensor_tensor(qs[s][MROW:DEPTH, :].rearrange("p (c q) -> p c q", q=P),
                                            repeat(mrow[MROW:DEPTH, :], RT, RT), widen(rowmask[MROW:DEPTH, :], RT, P),
                                            ALU.mult).then_inc(max_stacked, 1)
                    pool.drain()
                if isinstance(batch[0], int) and num(batch) == B - 2:
                    token_moments(1 + 2 * TB, slice(0, EARLY * BPB))
                if isinstance(batch[0], int) and num(batch) == B - 1:
                    for e in range(2):
                        for k in range(HC):
                            split_weights(0, e, k)

            def split_weights(pair, s, k):
                pool.wait_ge(whi_done, HC * (2 * pair + s) + k + 1)
                part = slice(P * k, P * k + P)
                nc.gpsimd.tensor_tensor(wlo[s][:, :, part], wst[s][:, :, part], whi[s][:, :, part], ALU.subtract)\
                  .then_inc(w_split, 1)

            phases(pool, phase, peeled=4)

            def low_hidden(unit, i):
                pool.wait_ge(hhi_done, unit + 1)
                nc.gpsimd.tensor_tensor(hlo[i % HS][:, :], hh[i % HS][:, :], hhi[i % HS][:, :], ALU.subtract)\
                  .then_inc(hlo_done, 1)

            def opening():
                for u in range(2 * UPE):
                    low_hidden(u, u)
                    if POOL_AT.get(u) == "Y":
                        gate_values(last_batch)
                    if POOL_AT.get(u) == "N":
                        token_moments(2 + 2 * TB, slice(EARLY * BPB, B))
                    if u in OPEN_SPLIT_AT:
                        split_weights(1, 0, OPEN_SPLIT_AT.index(u))

            def expert(pair, s, more=True):
                for i in range(UPE):
                    low_hidden(UPE * (2 * pair + s) + i, i)
                    if more and i in SPLIT_AT:
                        split_weights(*later((pair, s), 1), SPLIT_AT.index(i))
                    if not more and i in MOMENTS_AT:
                        last_moments(MOMENTS_AT.index(i))

            def last_moments(k):
                token_moments(3 + 2 * TB + k, slice(BPB * k, BPB * k + BPB))

            experts(pool, opening, expert)
            for k in range(len(MOMENTS_AT), TB):
                last_moments(k)

        @block.scalar
        def _(act):
            def read_work(name, batch):
                n, s = num(batch), batch[1]
                kind, k = name[0], int(name[1])
                act.wait_ge(w_filled, w_at(name, n) + 1)
                if kind == "T":
                    w = min(4 * P, S - 4 * P * k)
                    cols = slice(4 * P * k, 4 * P * k + w)
                    if k == 0:
                        wait_past(act, klo_done, KC * n)
                    nc.scalar.activation(xhi[s][:, cols], wk[:, 0:w], ACT.Copy)
                    nc.scalar.activation(exact[:, cols], wk[:, 0:w], ACT.Copy).then_inc(w_read, 1)
                if kind == "K":
                    if k == 0:
                        wait_past(act, mx_filled, UNITS * (n - 1))
                        if not isinstance(batch[0], int) or batch[0] > 0:
                            act.wait_ge(ks_in[s], 16 * 3 * GR * batch[0])
                    nc.scalar.activation(khi[s][:, KCW * k:KCW * k + KCW], wk[:, 0:KCW], ACT.Identity,
                                         bias=kbias[:, 0:1]).then_inc(khi_done, 1)
                    nc.scalar.activation(exact[:, KCW * k:KCW * k + KCW], wk[:, 0:KCW], ACT.Identity,
                                         bias=kbias[:, 0:1]).then_inc(w_read, 1)
                if kind == "V":
                    if k == 0:
                        wait_past(act, pv_done, STEPS * (n - 1))
                    full = min(4, KT - 1 - 4 * k)
                    dst = vs[s][:, 4 * k * H:(4 * k + full) * H, 0:DH]
                    ins = nc.scalar.activation(dst, wk[:, 0:full * P].rearrange("p (h d) -> p h d", d=DH), ACT.Copy)
                    if full < 4:
                        ins = nc.scalar.activation(vs[s][0:LAST, (KT - 1) * H:KT * H, 0:DH],
                                                   wk[0:LAST, full * P:full * P + P].rearrange("p (h d) -> p h d", d=DH),
                                                   ACT.Copy)
                    ins.then_inc(w_read, 1)
                if kind == "G":
                    nc.scalar.activation(yT[:, :], wk[:, 0:N], ACT.Copy).then_inc(w_read, 1)

            def copy_block(name, k):
                src = pre.filled(act, name, k)
                nc.scalar.activation(XT[:, TW * k:TW * k + TW], src[:, 0:TW], ACT.Copy).then_inc(pre.reader(name, k), 1)

            for k in range(TB):
                copy_block("xT", k)
            act.wait_ge(attn_weights_in, ATTN_WEIGHTS)
            for k in range(TB):
                src = pre.filled(act, "qT", k)
                nc.scalar.activation(QT[:, TW * k:TW * k + TW], src[:, 0:TW], ACT.Sigmoid, bias=abq[:, 0:1])\
                  .then_inc(pre.reader("qT", k), 1)
            for k in range(TB):
                for b in range(BPB * k, BPB * k + BPB):
                    pre.taken(act, "kvh", b)
                keys = KVH[:, BPB * k:BPB * k + BPB, 0:P]
                nc.scalar.activation(keys, keys, ACT.Sigmoid).then_inc(k_done, 1)
            pre.taken(act, "bias")
            for name in X_FILLS:
                read_work(name, (0, 0))
            for g in range(-(-B // 3)):
                src = pre.filled(act, "nd", g)
                k = min(3, B - 3 * g)
                src = src[0:N, 0:k * (P + H)].rearrange("p (b c) -> p b c", b=k)
                nc.scalar.activation(GATE[:, 3 * g:3 * g + k, :], src[:, :, 0:P], ACT.Copy)
                nc.scalar.activation(DEN[:, 3 * g:3 * g + k, :], src[:, :, P:P + H], ACT.Copy)\
                  .then_inc(pre.reader("nd", g), 1)
            for name in K_FILLS:
                read_work(name, (0, 0))
            for k in range(TB):
                copy_block("gT", k)
            for name in X_FILLS:
                read_work(name, (0, 1))
            for name, k in staggered("qnT", "Q"):
                if name == "qnT":
                    copy_block(name, k)
                else:
                    src = pre.filled(act, "Q", k)
                    nc.scalar.activation(qhi[:, TW * k:TW * k + TW], src[:, 0:TW], ACT.Identity, bias=qbias[:, 0:1])\
                      .then_inc(qhi_done, 1)
            for k in range(TB):
                src = pre.filled(act, "gate", k)
                nc.scalar.activation(GATE[:, BPB * k:BPB * k + BPB, :], src[0:N, :].rearrange("p (b c) -> p b c", b=BPB),
                                     ACT.Sigmoid).then_inc(pre.reader("gate", k), 1)
                act.wait_ge(pre.reader("gate", k), pre.at["gate", k] // 4 + 1)
            act.sem_inc(gate_done, TB)

            def phase(batch, has):
                for u in range(STEPS):
                    if "C" in has:
                        n, h, w = num(batch), u % 2, P if u // 2 < KT - 1 else LAST
                        act.wait_ge(scored, STEPS * n + u + 1)
                        wait_past(act, pv_done, STEPS * n + u - 1)
                        nc.scalar.activation(pr[h][0:w, :, :, :].rearrange("p g h q -> p g (h q)"), score[h][0:w],
                                             ACT.Exp, scale=SCALE).then_inc(exp_done, 1)
                    name = FILLS.get(u)
                    if name and name[0] in "TKVG" and STAGE_OF[name[0]] in has:
                        other = later(batch, AHEAD[STAGE_OF[name[0]]])
                        if not prepared(name, num(other)):
                            read_work(name, other)
                    if isinstance(batch[0], int) and num(batch) == B - 1:
                        if u in X2T_AT:
                            copy_tokens(X2T_AT.index(u))
                        if u == EXP_AT:
                            exponentials(0)
                        if u in COMB_AT:
                            copy_comb(COMB_AT.index(u))
                        if u in (18, 19, 20, 21):
                            split_weights(0, 1, u - 18)
                if isinstance(batch[0], int) and num(batch) == B - 2:
                    for k in range(HC):
                        split_weights(0, 0, k)

            def copy_tokens(k):
                src = ring_of(k).filled(act, "x2T", k)
                cols = slice(TW * k, TW * k + TW)
                nc.scalar.activation(X2T[:, cols], src[:, 0:TW], ACT.Copy)
                nc.scalar.activation(x2hi[:, cols], src[:, 0:TW], ACT.Copy).then_inc(x2hi_done, 1)

            def exponentials(k):
                blk = slice(0, EARLY * BPB) if k < EARLY else slice(EARLY * BPB, B)
                act.wait_ge(logits_less_max, 1 + (k == EARLY))
                nc.scalar.activation(ex[:, blk, :], ex[:, blk, :], ACT.Exp).then_inc(exped, 1)

            def copy_comb(k):
                src = ring_of(k).filled(act, "cT", k)
                nc.scalar.activation(combT[:, TW * k:TW * k + TW], src[0:E, 0:TW], ACT.Copy)\
                  .then_inc(ring_of(k).reader("cT", k), 1)

            def split_weights(pair, s, k):
                if k == 0:
                    act.wait_ge(wst_in[s], 16 * 3 * (pair + 1))
                    if not isinstance(pair, int) or 2 * pair + s > 1:
                        late = isinstance(pair, int) and 2 * pair + s == 2
                        act.wait_ge(d_done, OPENING.index((0, UPE - 1)) + 1 if late else UPE * (2 * pair + s - 1))
                part = slice(P * k, P * k + P)
                nc.scalar.activation(whi[s][:, :, part], wst[s][:, :, part], ACT.Copy).then_inc(whi_done, 1)

            act.wait_ge(zeros_done, 1)
            phases(act, phase)

            def scale_tokens(pair, s, k):
                act.wait_ge(xe_done, scale_count(2 * pair + s, k))
                cols = slice(TW * k, TW * k + TW)
                nc.scalar.activation(xehi[s][:, cols], xe[:, cols], ACT.Copy).then_inc(xehi_done, 1)

            def high_hidden(unit, i):
                act.wait_ge(h_done, unit + 1)
                if not isinstance(unit, int) or unit >= HS:
                    act.wait_ge(d_done, unit - HS + 1)
                nc.scalar.activation(hhi[i % HS][:, :], hh[i % HS][:, :], ACT.Copy).then_inc(hhi_done, 1)

            def hidden(unit, i):
                act.wait_ge(gu_filled, unit + 1)
                if not isinstance(unit, int) or unit >= 2:
                    act.wait_ge(h_done, unit - 1)
                nc.scalar.activation(sg[i % 2][:, :], PS[:, 2 * (i % 2), 0:TW], ACT.Silu).then_inc(silu_done, 1)
                if not isinstance(unit, int) or unit > 0:
                    high_hidden(unit - 1, i - 1)

            def opening():
                for u in range(2 * UPE):
                    hidden(u, u)
                    if ACT_AT.get(u) == "G":
                        read_work("G0", last_batch)
                    if ACT_AT.get(u) == "X":
                        copy_tokens(EARLY)
                    if ACT_AT.get(u) == "E":
                        exponentials(EARLY)
                    if ACT_AT.get(u) == "C":
                        copy_comb(EARLY)
                    if u in OPEN_SPLIT_AT:
                        split_weights(1, 0, OPEN_SPLIT_AT.index(u))
                    if u in OPEN_SCALE_AT:
                        e, k = OPEN_SCALE_AT[u]
                        scale_tokens(e // 2, e % 2, k)

            def expert(pair, s, more=True):
                for i in range(UPE):
                    hidden(UPE * (2 * pair + s) + i, i)
                    if more and i in SPLIT_AT:
                        split_weights(*later((pair, s), 1), SPLIT_AT.index(i))
                    if more and i in SCALE_AT:
                        scale_tokens(*later((pair, s), 1), SCALE_AT.index(i))
                    if not more and i in OUT_AT:
                        copy_out(OUT_AT.index(i))

            def copy_out(k):
                act.wait_ge(d_done, UPE * (E - 1) + HC * (k + 1))
                nc.scalar.activation(OT[:, TW * k:TW * k + TW], PS[:, 4 + k, 0:TW], ACT.Copy).then_inc(out_copied, 1)

            for k in range(EARLY):
                scale_tokens(0, 0, k)
            experts(act, opening, expert)
            high_hidden(UPE * E - 1, UPE - 1)
            for k in range(len(OUT_AT), TB):
                copy_out(k)

        @block.vector
        def _(dve):
            for s in range(2):
                nc.vector.memset(ct[s][:, KT - 1, :], 0.0)
                last = nc.vector.memset(cstat[s][:, KT - 1, :], 0.0)
            last.then_inc(ct_zeroed, 1)
            for s in range(2):
                nc.vector.memset(mxs[s][:, :, :], 0.0)
                nc.vector.memset(vs[s][:, (KT - 1) * H:KT * H, :], 0.0)
                dve.drain()
                nc.vector.memset(vs[s][:, 0:(KT - 1) * H, DH:VW], 1.0)
                nc.vector.memset(vs[s][0:LAST, (KT - 1) * H:KT * H, DH:VW], 1.0)
            nc.vector.memset(pvp, 0.0).then_inc(zeros_done, 1)

            def context_stats(batch, tiles):
                n, s = num(batch), batch[1]
                for k in tiles:
                    if k == 0:
                        dve.wait_ge(ctx_in[s], 32 * (batch[0] + 1))
                    w = P if k < KT - 1 else LAST
                    ins = nc.vector.bn_stats(cstat[s][0:w, k, :], ct[s][0:w, k, :])
                    if k == KT - 1:
                        ins.then_inc(ctx_stats, 1)

            dve.wait_ge(attn_weights_in, ATTN_WEIGHTS)
            context_stats((0, 0), range(KT))
            for b in range(B):
                src = pre.filled(dve, "kvh", b)
                nc.vector.tensor_tensor(KVH[:, b, :], src[0:N, 0:3 * P], kvhrow[:, :], ALU.add)\
                  .then_inc(pre.reader("kvh", b), 1)
            src = pre.filled(dve, "wT")
            nc.vector.tensor_copy(xWT[:, 0:4, :], src.rearrange("p (i c) -> p i c", i=4)).then_inc(pre.reader("wT"), 1)
            src = pre.filled(dve, "woT")
            nc.vector.tensor_copy(xWT[:, 4, :], src[:, 0:P]).then_inc(pre.reader("woT"), 1)
            dve.wait_ge(weights_in, WEIGHTS)
            dve.drain()
            nc.vector.tensor_scalar(xW[:, 1, :], xWT[:, 1, :], kvg[:, 0:1], None, ALU.mult)
            nc.vector.tensor_scalar(WqTg[:, :], xWT[:, 0, :], qg[:, 0:1], None, ALU.mult)
            nc.vector.tensor_scalar(WgTg[:, :], xWT[:, 3, :], qg[:, 0:1], None, ALU.mult)
            for h in range(2):
                half = slice(h * P // 2, (h + 1) * P // 2)
                nc.vector.tensor_scalar(xW[:, 2, half].rearrange("p (c g d) -> p c g d", c=HG, g=2),
                                        xWT[:, 2, half].rearrange("p (g c d) -> p c g d", c=HG, g=2),
                                        kvg[:, 0:1], None, ALU.mult)
            dve.drain()
            for i, parts in ((1, WkTg), (2, WvTg)):
                nc.vector.tensor_copy(parts[0][:, :], xW[:, i, :])
            dve.drain()
            for i, parts in ((1, WkTg), (2, WvTg)):
                last = nc.vector.tensor_tensor(parts[1][:, :], xW[:, i, :], parts[0][:, :], ALU.subtract)
            last.then_inc(folded, 1)
            src = pre.filled(dve, "bias")
            nc.vector.tensor_copy(kbias[:, :], src[:, 0:1])
            nc.vector.tensor_copy(qbias[:, :], src[:, 1:2])
            nc.vector.tensor_copy(vrow[:, :], src[0:N, P:2 * P])
            nc.vector.tensor_tensor(grow[:, :], src[0:N, 2 * P:3 * P], bgrow[:, :], ALU.add).then_inc(pre.reader("bias"), 1)
            context_stats((0, 1), range(KT))
            dve.wait_ge(consts_done, 1)
            for b in range(B):
                src = pre.filled(dve, "kv", b)
                if b >= 6:
                    pre.filled(dve, "nd", (b - 6) // 3)
                nc.vector.tensor_tensor(R[:, b % 6, :], src[:, 0:P + H], kvmask[:, :], ALU.mult)\
                  .then_inc(pre.reader("kv", b), 1)

            def block_of(k):
                return slice(BPB * k, BPB * k + BPB)

            def block_stats(src, k):
                for b in range(BPB * k, BPB * k + BPB):
                    last = nc.vector.bn_stats(tstat[:, b, :], src[:, b, :])
                last.then_inc(tok_stats, 1)

            def block_norm(src, k, count):
                dve.wait_ge(tok_scale, count)
                for b in range(BPB * k, BPB * k + BPB):
                    last = nc.vector.tensor_scalar(src[:, b, :], src[:, b, :], tsm[:, 0, b:b + 1], tsm[:, 1, b:b + 1],
                                                   ALU.subtract, ALU.mult)
                return last

            def attention(k):
                for g in range(BPB * k // 3, (BPB * k + BPB - 1) // 3 + 1):
                    pre.taken(dve, "nd", g)
                nc.vector.reciprocal(DEN[:, block_of(k), :], DEN[:, block_of(k), :])
                dve.drain()
                for b in range(BPB * k, BPB * k + BPB):
                    att = GATE[:, b, :].rearrange("p (m h) -> p m h", h=H)
                    nc.vector.tensor_tensor(att, att, repeat(DEN[:, b, :], N, P // H), ALU.mult)
                dve.drain()
                block_stats(GATE, k)

            def gated_attention(k):
                blk = block_of(k)
                block_norm(GATE, k, 1 + k)
                dve.wait_ge(h_scaled, k + 1)
                dve.drain()
                nc.vector.tensor_tensor(GATE[:, blk, :], GATE[:, blk, :], KVH[:, blk, 2 * P:3 * P], ALU.mult)
                dve.drain()
                nc.vector.tensor_tensor(GATE[:, blk, :], GATE[:, blk, :], KVH[:, blk, P:2 * P], ALU.add)\
                  .then_inc(attn_done, 1)

            def residual(k):
                blk = block_of(k)
                src = pre.filled(dve, "o", k)
                nc.vector.scalar_tensor_tensor(X1[:, blk, :], src[0:N, :].rearrange("p (b c) -> p b c", b=BPB), 0.0,
                                               X2[:, blk, :], ALU.max, ALU.add).then_inc(pre.reader("o", k), 1)
                dve.drain()
                block_stats(X1, k)

            dve.wait_ge(x_in, 16)
            attention(0)
            for k in range(TB):
                if k + 1 < TB:
                    attention(k + 1)
                gated_attention(k)
            residual(0)
            for k in range(TB):
                if k + 1 < TB:
                    residual(k + 1)
                block_norm(X1, k, 1 + TB + k).then_inc(qn_done, 1)
            for k in range(TB):
                src = pre.filled(dve, "Q", k)
                dve.wait_ge(qhi_done, k + 1)
                cols = slice(TW * k, TW * k + TW)
                nc.vector.scalar_tensor_tensor(qlo[:, cols], src[:, 0:TW], qbias[:, 0:1], qhi[:, cols],
                                               ALU.add, ALU.subtract).then_inc(pre.reader("Q", k), 1)

            def read_work(name, batch):
                n, s = num(batch), batch[1]
                kind, k = name[0], int(name[1])
                dve.wait_ge(w_filled, w_at(name, n) + 1)
                if kind == "M":
                    nc.vector.tensor_scalar(mrow[MROW:DEPTH, :], wk[MROW:DEPTH, 0:P], -1.0, None, ALU.mult).then_inc(w_read, 1)
                if kind == "Y":
                    blocks = wk[0:N, :].rearrange("p (h g c i) -> p g h c i", h=2, g=2, c=HG)
                    for g in range(2):
                        nc.vector.reciprocal(rden[:, g::2, :], blocks[:, g, :, :, VW * g + DH])
                    dve.drain()
                    yv = y[:, :].rearrange("p (h g c d) -> p g h c d", h=2, g=2, c=HG)
                    for h in range(2):
                        for g in range(2):
                            ins = nc.vector.tensor_tensor(
                                yv[:, g, h], blocks[:, g, h, :, VW * g:VW * g + DH],
                                widen(rden[:, 2 * h + g, :], N, DH), ALU.mult)
                    ins.then_inc(w_read, 1)
                if kind == "O":
                    at = (slice(n, n + 1) if isinstance(n, int) else bass.ds(n, 1))
                    tokens = X2[:, at, :].rearrange("p o d -> p (o d)")
                    nc.vector.tensor_tensor(tokens, wk[0:N, 0:P], X1[:, at, :].rearrange("p o d -> p (o d)"), ALU.add)\
                      .then_inc(w_read, 1)
                    dve.drain()
                    ins = nc.vector.bn_stats(tstat[:, at, :].rearrange("p o d -> p (o d)"), tokens)
                    if isinstance(n, int) and n in (EARLY * BPB - 1, B - 1):
                        ins.then_inc(tok_stats, 1)

            def copy_values(batch):
                n = num(batch)
                dve.wait_ge(pv_done, STEPS * (n + 1))
                if not isinstance(n, int) or n > 0:
                    dve.wait_ge(w_filled, w_at("Y0", n - 1) + 1)
                nc.vector.tensor_copy(pvs[:, :], pvp).then_inc(pv_copied, 1)

            def low_x2(k):
                ring = ring_of(k)
                src = ring.filled(dve, "x2T", k)
                dve.wait_ge(x2hi_done, k + 1)
                cols = slice(TW * k, TW * k + TW)
                nc.vector.tensor_tensor(x2lo[:, cols], src[:, 0:TW], x2hi[:, cols], ALU.subtract)\
                  .then_inc(ring.reader("x2T", k), 1)

            def rank_experts(k):
                blk, n = (slice(0, EARLY * BPB), EARLY * BPB) if k < EARLY else (slice(EARLY * BPB, B), BPB)
                ring = ring_of(k)
                src = ring.filled(dve, "logits", k)
                nc.vector.tensor_copy(LG[:, blk, :], src[0:N, 0:n * E].rearrange("p (b e) -> p b e", b=n))\
                  .then_inc(ring.reader("logits", k), 1)
                dve.drain()
                shape = [N, n, E, E]
                other, own = LG[:, blk, :].unsqueeze(2).to_broadcast(shape), LG[:, blk, :].unsqueeze(3).to_broadcast(shape)
                larger, tied = RK[0][:, 0:n, :, :], RK[1][:, 0:n, :, :]
                nc.vector.reduce_max(rsm[:, 0, blk], LG[:, blk, :], AXL.X)
                nc.vector.tensor_tensor(larger, other, own, ALU.is_gt)
                nc.vector.tensor_tensor(tied, other, own, ALU.is_equal)
                dve.drain()
                nc.vector.tensor_tensor(ex[:, blk, :], LG[:, blk, :], widen(rsm[:, 0, blk], N, E), ALU.subtract)\
                  .then_inc(logits_less_max, 1)
                nc.vector.tensor_tensor(tied, tied, before[:, :, :].unsqueeze(1).to_broadcast(shape), ALU.mult)
                dve.drain()
                nc.vector.tensor_tensor(larger, larger, tied, ALU.add)
                dve.drain()
                nc.vector.reduce_sum(rank[:, blk, :], larger, AXL.X)

            def routing_weights(k):
                blk = slice(0, EARLY * BPB) if k < EARLY else slice(EARLY * BPB, B)
                dve.wait_ge(exped, 1 + (k == EARLY))
                dve.drain()
                nc.vector.scalar_tensor_tensor(ex[:, blk, :], rank[:, blk, :], 1.5, ex[:, blk, :], ALU.is_lt, ALU.mult)
                dve.drain()
                nc.vector.reduce_sum(rsm[:, 1, blk], ex[:, blk, :], AXL.X)
                dve.drain()
                nc.vector.reciprocal(rsm[:, 2, blk], rsm[:, 1, blk])
                dve.drain()
                nc.vector.tensor_scalar(rsm[:, 1, blk], rsm[:, 2, blk], DEPTH_SCALE, None, ALU.mult)
                dve.drain()
                nc.vector.tensor_tensor(ex[:, blk, :], ex[:, blk, :], widen(rsm[:, 1, blk], N, E), ALU.mult)\
                  .then_inc(comb_done, 1)

            def phase(batch, has):
                for u in range(STEPS):
                    if u == 0 and "D" in has:
                        copy_values(later(batch, -1))
                    name = FILLS.get(u)
                    if name and name[0] in "YO" and STAGE_OF[name[0]] in has:
                        read_work(name, later(batch, AHEAD[STAGE_OF[name[0]]]))
                    for ahead, unit in mx_units(u, has, UNITS):
                        n, s = num(later(batch, ahead)), later(batch, ahead)[1]
                        rt, c = unit // CH, unit % CH
                        w = P if rt < RT - 1 else LASTR
                        dve.wait_ge(mx_filled, UNITS * n + unit + 1)
                        nc.vector.reduce_max(mxs[s][0:w, rt, c:c + 1], mxp[unit_slot(s, unit)][0:w, 0:CHW[c]], AXL.X)\
                          .then_inc(mx_reduced, 1)
                        if unit == UNITS - 1:
                            dve.drain()
                            nc.vector.reduce_max(mx[:, :], mxs[s][:, :, :], AXL.X).then_inc(max_done, 1)
                    k = u - STATS_FROM
                    if 0 <= k < KT // 2 and (not isinstance(batch[0], int) or 2 <= num(batch) + 3 < B):
                        context_stats(later(batch, 3), (2 * k, 2 * k + 1))
                    if isinstance(batch[0], int) and num(batch) == B - 1:
                        if u in X2T_AT:
                            low_x2(X2T_AT.index(u))
                        if u == X2T_AT[0]:
                            nc.vector.memset(zero[:, :], 0.0)
                        if u == LOGITS_AT:
                            rank_experts(0)
                        if u == EXP_AT:
                            routing_weights(0)
                    if name and name[0] == "M" and STAGE_OF[name[0]] in has:
                        read_work(name, later(batch, AHEAD[STAGE_OF[name[0]]]))
                if isinstance(batch[0], int) and num(batch) == B - 2:
                    for k in range(EARLY):
                        block_norm(X2, k, 1 + 2 * TB).then_inc(x2_done, 1)

            phases(dve, phase, peeled=4)

            def scale_tokens(pair, s, k):
                cols = slice(TW * k, TW * k + TW)
                if isinstance(pair, int) and pair == 0 and k == EARLY:
                    rows = route[1].filled(dve, "rows", s)
                    nc.vector.tensor_tensor(xe[:, cols], X2T[:, cols], rows[:, 0:TW], ALU.mult).then_inc(xe_done, 1)
                    return
                if k == 0:
                    dve.wait_ge(cb_in[s], 16 * (pair + 1))
                nc.vector.tensor_tensor(xe[:, cols], X2T[:, cols], cb[s][:, cols], ALU.mult).then_inc(xe_done, 1)

            def low_tokens(pair, s, k):
                dve.wait_ge(xehi_done, scale_count(2 * pair + s, k))
                cols = slice(TW * k, TW * k + TW)
                nc.vector.tensor_tensor(xelo[s][:, cols], xe[:, cols], xehi[s][:, cols], ALU.subtract)\
                  .then_inc(xelo_done, 1)

            def hidden(unit, i):
                dve.wait_ge(silu_done, unit + 1)
                if not isinstance(unit, int) or unit >= HS:
                    dve.wait_ge(hlo_done, unit - HS + 1)
                nc.vector.tensor_tensor(hh[i % HS][:, :], sg[i % 2][:, :], PS[:, 2 * (i % 2) + 1, 0:TW], ALU.mult)\
                  .then_inc(h_done, 1)

            def opening():
                for u in range(2 * UPE):
                    hidden(u, u)
                    if u - 1 in OPEN_SCALE_AT:
                        e, k = OPEN_SCALE_AT[u - 1]
                        low_tokens(e // 2, e % 2, k)
                    if u in OPEN_SCALE_AT:
                        e, k = OPEN_SCALE_AT[u]
                        if OPEN_SCALE_AT.get(u - 1, (0, 0))[1] == k:
                            dve.drain()
                        scale_tokens(e // 2, e % 2, k)
                    if DVE_AT.get(u) in ("Y", "O"):
                        read_work(DVE_AT[u] + "0", last_batch)
                    if DVE_AT.get(u) == "N":
                        block_norm(X2, EARLY, 2 + 2 * TB).then_inc(x2_done, 1)
                    if DVE_AT.get(u) == "X":
                        low_x2(EARLY)
                    if DVE_AT.get(u) == "L":
                        rank_experts(EARLY)
                    if DVE_AT.get(u) == "R":
                        routing_weights(EARLY)

            def expert(pair, s, more=True):
                for i in range(UPE):
                    hidden(UPE * (2 * pair + s) + i, i)
                    if more and i in SCALE_AT:
                        scale_tokens(*later((pair, s), 1), SCALE_AT.index(i))
                    if more and i - 1 in SCALE_AT:
                        low_tokens(*later((pair, s), 1), SCALE_AT.index(i - 1))
                    if not more and i in ADD_AT:
                        add_experts(ADD_AT.index(i))
                    if not more and i in NORM_AT:
                        last_norm(NORM_AT.index(i))

            def add_experts(k):
                dve.wait_ge(out_flipped, k + 1)
                blk = block_of(k)
                nc.vector.tensor_tensor(X2[:, blk, :], X2[:, blk, :],
                                        PS[0:N, 4 + k, :].rearrange("p (b c) -> p b c", b=BPB), ALU.add)
                dve.drain()
                block_stats(X2, k)

            def last_norm(k):
                block_norm(X2, k, 3 + 2 * TB + k).then_inc(y_done, 1)

            for k in range(EARLY):
                scale_tokens(0, 0, k)
            copy_values(last_batch)
            for k in range(EARLY):
                low_tokens(0, 0, k)
            experts(dve, opening, expert)
            for k in range(len(NORM_AT), TB):
                last_norm(k)
                if k + 1 < TB:
                    add_experts(k + 1)

        @block.tensor
        def _(pe):
            def split_product(dst, hi, lo, right_hi, right_lo, start):
                nc.tensor.matmul(dst, hi, right_hi, start=start, stop=False, skip_group_check=not start)
                nc.tensor.matmul(dst, hi, right_lo, start=False, stop=False, skip_group_check=not start)
                return nc.tensor.matmul(dst, lo, right_hi, start=False, stop=True, skip_group_check=not start)

            def fill_work(name, batch):
                n, s = num(batch), batch[1]
                kind, k = name[0], int(name[1])
                wait_past(pe, w_read, w_at(name, n))
                if kind == "T":
                    if k == 0:
                        pe.wait_ge(ctx_normed, n + 1)
                    for i in range(4 * k, min(4 * k + 4, KT)):
                        w = P if i < KT - 1 else LAST
                        last = nc.tensor.transpose(wk[:, P * (i - 4 * k):P * (i - 4 * k) + w], xn[0:w, i, :], ident[0:w, 0:w])
                if kind == "K":
                    if k == 0:
                        pe.wait_ge(xlo_done, TF * (n + 1))
                    cols = slice(KCW * k, KCW * k + KCW)
                    last = split_product(wk[:, 0:KCW], WkTg[0][:, :], WkTg[1][:, :], xhi[s][:, cols], xlo[s][:, cols], True)
                if kind == "V":
                    for i in range(4 * k, min(4 * k + 4, KT)):
                        w = P if i < KT - 1 else LAST
                        keys = slice(P * i, P * i + w)
                        last = split_product(wk[0:w, P * (i - 4 * k):P * (i - 4 * k) + P], xhi[s][:, keys], xlo[s][:, keys],
                                             WvTg[0][:, :], WvTg[1][:, :], True)
                if kind == "M":
                    pe.wait_ge(max_done, n + 1)
                    last = nc.tensor.matmul(wk[MROW:DEPTH, 0:P], mx[:, :], ident[:, :], start=True, stop=True)
                if kind == "Y":
                    pe.wait_ge(pv_copied, n + 1)
                    for g in range(GR):
                        last = nc.tensor.transpose(wk[0:N, P * g:P * g + P], pvs[:, N * g:N * g + N], ident[:, :])
                if kind == "G":
                    pe.wait_ge(y_gated, n + 1)
                    last = nc.tensor.transpose(wk[:, 0:N], y[:, :], ident[0:N, 0:N])
                if kind == "O":
                    pe.wait_ge(w_read, w_at("G0", n) + 1)
                    last = nc.tensor.matmul(wk[0:N, 0:P], yT[:, :], xWT[:, 4, :], start=True, stop=True)
                last.then_inc(w_filled, 1)

            def transpose_block(name, k, src):
                dst = pre.start(pe, name, k)
                for i in range(BPB):
                    last = nc.tensor.transpose(dst[:, N * i:N * i + N], src[:, BPB * k + i, :], ident[0:N, 0:N])
                last.then_inc(pre.filled_sem, 1)

            def project_block(name, k, weight, bias):
                dst = pre.start(pe, name, k)
                nc.tensor.matmul(dst[0:N, :], ident[0:N, 0:N], repeat(bias, N, BPB), start=True, stop=True)
                for i in range(BPB):
                    b = BPB * k + i
                    last = nc.tensor.matmul(dst[0:N, P * i:P * i + P], XT[:, N * b:N * b + N], weight, start=False, stop=True,
                                            skip_group_check=True)
                last.then_inc(pre.filled_sem, 1)

            pe.wait_ge(ident_done, 1)
            pe.wait_ge(x_in, 16)
            for k in range(TB):
                transpose_block("xT", k, X2)
            pe.wait_ge(attn_weights_in, ATTN_WEIGHTS)
            for k in range(TB):
                pre.taken(pe, "xT", k)
                nc.tensor.matmul(pre.start(pe, "qT", k)[:, 0:TW], aWq[:, :], XT[:, TW * k:TW * k + TW], start=True, stop=True)\
                  .then_inc(pre.filled_sem, 1)
            for b in range(B):
                nc.tensor.matmul(pre.start(pe, "kvh", b)[0:N, 0:3 * P], XT[:, N * b:N * b + N], aWkvh[:, :],
                                 start=True, stop=True).then_inc(pre.filled_sem, 1)
            pe.wait_ge(weights_in, WEIGHTS)
            dst = pre.start(pe, "wT")
            for i in range(4):
                last = nc.tensor.transpose(dst[:, P * i:P * i + P], xW[:, i, :], ident[:, :])
            last.then_inc(pre.filled_sem, 1)
            nc.tensor.transpose(pre.start(pe, "woT")[:, 0:P], xW[:, 4, :], ident[:, :]).then_inc(pre.filled_sem, 1)
            dst = pre.start(pe, "bias")
            pre.taken(pe, "wT")
            nc.tensor.matmul(dst[:, 0:1], xWT[:, 1, :], kvb[:, 0:1], start=True, stop=True)
            nc.tensor.matmul(dst[:, 1:2], xWT[:, 0, :], qb[:, 0:1], start=True, stop=True)
            nc.tensor.matmul(dst[0:N, P:2 * P], kvb[:, 0:1].to_broadcast([P, N]), xWT[:, 2, :], start=True, stop=True)
            nc.tensor.matmul(dst[0:N, 2 * P:3 * P], qb[:, 0:1].to_broadcast([P, N]), xWT[:, 3, :], start=True, stop=True)\
              .then_inc(pre.filled_sem, 1)
            for name in X_FILLS:
                fill_work(name, (0, 0))
            for k in range(TB):
                pre.taken(pe, "qT", k)
            for name, b in kv_nd:
                dst = pre.start(pe, name, b)
                if name == "kv":
                    pe.wait_ge(k_done, b // BPB + 1)
                    keys = KVH[:, b, 0:P]
                    nc.tensor.matmul(dst[:, 0:P], keys, KVH[:, b, P:2 * P], start=True, stop=True)
                    last = nc.tensor.matmul(dst[:, P:P + H], keys, ones[0:N, :], start=True, stop=True)
                else:
                    for i in range(min(3, B - 3 * b)):
                        c = 3 * b + i
                        pre.taken(pe, "kv", c)
                        last = nc.tensor.matmul(dst[0:N, (P + H) * i:(P + H) * (i + 1)], QT[:, N * c:N * c + N],
                                                R[:, c % 6, :], start=True, stop=True)
                last.then_inc(pre.filled_sem, 1)
            pe.wait_ge(folded, 1)
            for name in K_FILLS:
                fill_work(name, (0, 0))
            for name, k in staggered("gT", "o"):
                if name == "gT":
                    pe.wait_ge(attn_done, k + 1)
                    transpose_block(name, k, GATE)
                else:
                    pre.taken(pe, "gT", k)
                    project_block(name, k, aWo[:, :], arow["bo"][:, :])
            for name in X_FILLS:
                fill_work(name, (0, 1))
            for name, k in staggered("qnT", "Q"):
                if name == "qnT":
                    pe.wait_ge(qn_done, k + 1)
                    transpose_block(name, k, X1)
                else:
                    pre.taken(pe, "qnT", k)
                    nc.tensor.matmul(pre.start(pe, "Q", k)[:, 0:TW], WqTg[:, :], XT[:, TW * k:TW * k + TW],
                                     start=True, stop=True).then_inc(pre.filled_sem, 1)
            pe.wait_ge(zeros_done, 1)

            def max_unit(batch, unit):
                n, s = num(batch), batch[1]
                rt, c = unit // CH, unit % CH
                w = P if rt < RT - 1 else LASTR
                if unit == 0:
                    pe.wait_ge(qbd_done, n + 1)
                    pe.wait_ge(khi_done, KC * (n + 1))
                wait_past(pe, mx_reduced, UNITS * n + unit - 1)
                rows = qbd[s][:, :, :].rearrange("p h q -> p (h q)")[:, P * rt:P * rt + w]
                nc.tensor.matmul(mxp[unit_slot(s, unit)][0:w, 0:CHW[c]], rows, khi[s][:, CHO[c]:CHO[c] + CHW[c]],
                                 start=True, stop=True).then_inc(mx_filled, 1)

            def score_step(batch, u):
                n, s = num(batch), batch[1]
                kt, h = u // 2, u % 2
                w = P if kt < KT - 1 else LAST
                if u == 0 and isinstance(n, int) and n == 0:
                    for k in range(TB):
                        pre.taken(pe, "gate", k)
                    pe.wait_ge(ones_done, 1)
                if u == 0:
                    pe.wait_ge(ks_in[s], 16 * 3 * GR * (batch[0] + 1))
                    pe.wait_ge(qs_done, n + 1)
                    pe.wait_ge(max_stacked, n + 1)
                wait_past(pe, exp_done, STEPS * n + u - 1)
                for g in range(2):
                    group = 2 * h + g
                    last = nc.tensor.matmul(score[h][0:w, g, :], ks[s][:, group, P * kt:P * kt + w],
                                            qs[s][:, GW * group:GW * group + GW], start=True, stop=True)
                last.then_inc(scored, 1)

            def value_step(batch, u):
                n, s = num(batch), batch[1]
                kt, h = u // 2, u % 2
                if u == 0:
                    wait_past(pe, pv_copied, n)
                    pe.wait_ge(w_read, w_at("V2", n) + 1)
                pe.wait_ge(exp_done, STEPS * n + u + 1)
                for c in range(HG):
                    place = kt * H + 2 * (HG * h + c)
                    last = nc.tensor.matmul(
                        pvp[32 * c:32 * c + 2 * VW, 2 * N * h:2 * N * (h + 1)],
                        vs[s][:, place:place + 2, :].rearrange("p g i -> p (g i)"), pr[h][:, :, c, :],
                        start=(u == 0), stop=(kt == KT - 1), skip_group_check=True)
                last.then_inc(pv_done, 1)

            def transpose_x2(k):
                ring = ring_of(k)
                pe.wait_ge(x2_done, k + 1)
                dst = ring.start(pe, "x2T", k)
                for i in range(BPB):
                    last = nc.tensor.transpose(dst[:, N * i:N * i + N], X2[:, BPB * k + i, :], ident[0:N, 0:N])
                last.then_inc(ring.filled_sem, 1)

            def logits(k):
                ring = ring_of(k)
                first = 0 if k < EARLY else k
                dst = ring.start(pe, "logits", k)
                for i in range(first, EARLY) if k < EARLY else (k,):
                    ring.taken(pe, "x2T", i)
                    for b in range(BPB * i, BPB * i + BPB):
                        at = E * (b - BPB * first)
                        last = nc.tensor.matmul(dst[0:N, at:at + E], X2T[:, N * b:N * b + N], Wr[:, :], start=True, stop=True)
                last.then_inc(ring.filled_sem, 1)

            def transpose_comb(k):
                ring = ring_of(k)
                pe.wait_ge(comb_done, 1 + (k == EARLY))
                dst = ring.start(pe, "cT", k)
                for i in range(BPB):
                    last = nc.tensor.transpose(dst[0:E, N * i:N * i + N], ex[:, BPB * k + i, :], ident[0:N, 0:N])
                last.then_inc(ring.filled_sem, 1)

            def phase(batch, has):
                for u in range(STEPS):
                    if "C" in has:
                        score_step(batch, u)
                    name = FILLS.get(u)
                    if name and STAGE_OF[name[0]] in has:
                        other = later(batch, AHEAD[STAGE_OF[name[0]]])
                        if not prepared(name, num(other)):
                            fill_work(name, other)
                    units = mx_units(u, has, UNITS)
                    for ahead, unit in units[:1]:
                        max_unit(later(batch, ahead), unit)
                    if (num(batch) if isinstance(batch[0], int) else 0, u) in GATE_AT:
                        project_block("gate", GATE_AT.index((num(batch), u)), WgTg[:, :], grow[:, :])
                    if "C" in has and u > 0:
                        value_step(batch, u - 1)
                    if "D" in has and u == 0:
                        value_step(later(batch, -1), STEPS - 1)
                    for ahead, unit in units[1:]:
                        max_unit(later(batch, ahead), unit)
                    if isinstance(batch[0], int) and num(batch) == B - 1:
                        if u == X2T_AT[0]:
                            pe.wait_ge(mx_reduced, UNITS * B)
                        if u in X2T_AT:
                            transpose_x2(X2T_AT.index(u))
                        if u == LOGITS_AT:
                            logits(0)
                        if u in COMB_AT:
                            transpose_comb(COMB_AT.index(u))

            phases(pe, phase)
            value_step(last_batch, STEPS - 1)

            def clear(tb):
                nc.tensor.matmul(PS[:, 4 + tb, 0:TW], zero[:, :], x2hi[:, 0:TW], start=True, stop=True)

            def up(unit, slot, s, i):
                tb, c = i // HC, i % HC
                cols, hid = slice(TW * tb, TW * tb + TW), slice(P * c, P * c + P)
                if not isinstance(unit, int) or unit >= 2:
                    pe.wait_ge(h_done, unit - 1)
                for m, (hi, lo) in enumerate(((x2hi, x2lo), (xehi[s], xelo[s]))):
                    last = split_product(PS[:, 2 * (slot % 2) + m, 0:TW], whi[s][:, m, hid], wlo[s][:, m, hid],
                                         hi[:, cols], lo[:, cols], True)
                last.then_inc(gu_filled, 1)

            def down(unit, slot, s, i):
                tb, c = i // HC, i % HC
                hid = slice(P * c, P * c + P)
                pe.wait_ge(hlo_done, unit + 1)
                split_product(PS[:, 4 + tb, 0:TW], whi[s][:, 2, hid], wlo[s][:, 2, hid],
                              hhi[slot % HS][:, :], hlo[slot % HS][:, :], False).then_inc(d_done, 1)

            def expert_row(e):
                if e == 0:
                    route[1].taken(pe, "cT", EARLY)
                else:
                    pe.wait_ge(xe_done, scale_count(0, EARLY))
                dst = route[1].bank("rows", e)
                nc.tensor.matmul(dst[:, 0:TW], ident[0:E, e:e + 1].to_broadcast([E, P]),
                                 combT[:, TW * EARLY:TW * EARLY + TW], start=True, stop=True).then_inc(route[1].filled_sem, 1)

            def opening():
                for k in range(EARLY):
                    route[0].taken(pe, "cT", k)
                for u, (e, i) in enumerate(OPENING):
                    if PE_AT.get(u) in ("Y", "G", "O"):
                        fill_work(PE_AT[u] + "0", last_batch)
                    if u == 0:
                        for tb in range(EARLY):
                            clear(tb)
                    if PE_AT.get(u) == "X":
                        pe.wait_ge(w_read, w_at("O0", B - 1) + 1)
                        transpose_x2(EARLY)
                    if PE_AT.get(u) == "L":
                        logits(EARLY)
                    if PE_AT.get(u) == "C":
                        transpose_comb(EARLY)
                    if PE_AT.get(u) == "B" or PE_AT.get(u - 1) == "B":
                        expert_row(u - 18)
                    if (e, i) == (0, EARLY * HC):
                        pe.wait_ge(xe_done, scale_count(1, EARLY))
                        clear(EARLY)
                    if i % HC == 0:
                        if i == 0:
                            pe.wait_ge(w_split, HC * (e + 1))
                        pe.wait_ge(xelo_done, scale_count(e, i // HC))
                    up(u, u, e, i)
                    if u >= LAG:
                        down(u - LAG, u - LAG, *OPENING[u - LAG])

            def flip(k):
                pe.wait_ge(out_copied, k + 1)
                for i in range(BPB):
                    at = TW * k + N * i
                    last = nc.tensor.transpose(PS[0:N, 4 + k, P * i:P * i + P], OT[:, at:at + N], ident[:, :])
                last.then_inc(out_flipped, 1)

            def expert(pair, s, more=True):
                e = 2 * pair + s
                pe.wait_ge(w_split, HC * (e + 1))
                pe.wait_ge(xelo_done, TB * (e + 1))
                for i in range(UPE):
                    up(UPE * e + i, i, s, i)
                    down(UPE * e + i - LAG, i - LAG, s if i >= LAG else 1 - s, (i - LAG) % UPE)
                    if not more and i in FLIP_AT:
                        flip(FLIP_AT.index(i))
                if not more:
                    for i in range(UPE - LAG, UPE):
                        down(UPE * e + i, i, s, i)

            experts(pe, opening, expert)
            for k in range(len(FLIP_AT), TB):
                flip(k)


def kernel(**inputs):
    import numpy as _np
    import concourse.bacc as _bacc
    from concourse import mybir as _mybir
    from concourse.bass_utils import run_bass_kernel_spmd as _run

    nc = _bacc.Bacc("TRN2", target_bir_lowering=False, num_devices=1)
    arrays, tensors = {}, {}
    for name, value in inputs.items():
        a = _np.ascontiguousarray(value)
        arrays[f"in_{name}"] = a
        tensors[name] = nc.dram_tensor(f"in_{name}", a.shape, _mybir.dt.from_np(a.dtype), kind="ExternalInput").ap()
    shape = tensors["x"].shape
    out = nc.dram_tensor("out", shape, F32, kind="ExternalOutput").ap()
    comb = nc.dram_tensor("comb", (tensors["L0_ffn_Wr"].shape[1], shape[0] * shape[1]), F32, kind="Internal").ap()
    decoder_layer(nc, tensors, out, comb)
    r = _run(nc, [arrays], core_ids=[0])
    return r.results[0]["out"]
```
